# Optimizing a Trainium2 kernel written in Bass

```python
import numpy as np
import jax
import jax.numpy as jnp

def _softmax(x, axis=-1):
    return jax.nn.softmax(x, axis=axis)

def _gelu(x):
    return jax.nn.gelu(x, approximate=True)

def _silu(x):
    return jax.nn.silu(x)

def _sigmoid(x):
    return jax.nn.sigmoid(x)

def _layernorm(x, axis=-1, eps=1e-05):
    m = jnp.mean(x, axis=axis, keepdims=True)
    v = jnp.var(x, axis=axis, keepdims=True)
    return (x - m) / jnp.sqrt(v + eps)

def _scatter_add(tgt, idx, src, axis=0):
    return tgt.at[idx].add(src)

def _segment_sum(src, seg, n):
    return jax.ops.segment_sum(src, seg, n)
kernel_name = 'mk_xattn_ffn_d4_seqx_r8_530e8c'

def setup_inputs(seed: int=0):
    np.random.seed(seed)
    _w = jnp.asarray

    def _rec_inputs():
        import jax
        import jax.numpy as jnp
        _rk = jax.random.key(seed)
        x = -0.000125 + 0.9999 * jax.random.normal(jax.random.fold_in(_rk, 1), (4, 256, 256), jnp.float32)
        _lenS = 256 - jax.random.randint(jax.random.fold_in(_rk, 7), (4,), 0, max(1, 256 // 4) + 1, jnp.int32)
        _lenS2 = 256 - jax.random.randint(jax.random.fold_in(_rk, 8), (4,), 0, max(1, 256 // 4) + 1, jnp.int32)
        itok_BxS_13_99985 = jax.random.randint(jax.random.fold_in(_rk, 11), (4, 256), 13, 99986, jnp.int32)
        _ctx_2048P = jax.random.normal(jax.random.fold_in(_rk, 12), (4, 16, 256), jnp.float32)
        _ctx_2048c = jax.random.dirichlet(jax.random.fold_in(_rk, 512), 0.3 * jnp.ones((16,), jnp.float32), (4, 256))
        _ctx_2048t = jnp.einsum('bsk,bkd->bsd', _ctx_2048c, _ctx_2048P)
        _ctx_2048t = _ctx_2048t * jax.lax.rsqrt(jnp.mean(jnp.square(_ctx_2048t)) + 1e-12) * 0.953939
        ctx_2048 = 6.82029e-06 + 0.0200006 * (_ctx_2048t + 0.3 * jax.random.normal(jax.random.fold_in(_rk, 612), (4, 256, 256), jnp.float32))
        return (x, itok_BxS_13_99985, ctx_2048)
    x, itok_BxS_13_99985, ctx_2048 = _rec_inputs()

    def _L0_xattn_setup():
        import jax, jax.numpy as jnp
        import numpy as np
        B, S, D = (4, 512, 256)
        E = 4
        F = 1024 // E
        VOCAB = 12500
        key = jax.random.key(seed)
        k1, k2, k3, k4, k5 = jax.random.split(key, 5)
        hidden_states = jax.random.normal(k1, (B, S, D), dtype=jnp.float32)
        token_ids = jax.random.randint(k2, (B, S), 0, VOCAB, dtype=jnp.int64)
        Wg = jax.random.normal(k3, (E, F, D), dtype=jnp.float32) * 0.02
        Wu = jax.random.normal(k4, (E, F, D), dtype=jnp.float32) * 0.02
        Wd = jax.random.normal(k5, (E, D, F), dtype=jnp.float32) * 0.02
        return {'hidden_states': hidden_states, 'token_ids': token_ids, 'Wg': Wg, 'Wu': Wu, 'Wd': Wd}
    _L0_xattn_all = _L0_xattn_setup()
    _L0_xattn_in = {k: v for k, v in _L0_xattn_all.items() if k in ()}
    del _L0_xattn_all

    def _L0_ffn_setup():
        import jax, jax.numpy as jnp
        import numpy as np
        D_MODEL = 256
        HIDDEN = int(2 * D_MODEL * 4 / 3)

        def ternary_quant(w):
            s = jnp.mean(jnp.abs(w))
            q = jnp.clip(jnp.round(w / s), -1.0, 1.0) * s
            return w + jax.lax.stop_gradient(q - w)
        key = jax.random.key(seed)
        k0, k1, k2, k3 = jax.random.split(key, 4)
        x = jax.random.normal(k0, (4, 512, D_MODEL), dtype=jnp.float32)
        std_in = 1.0 / np.sqrt(D_MODEL)
        std_h = 1.0 / np.sqrt(HIDDEN)
        w1 = jax.random.uniform(k1, (HIDDEN, D_MODEL), jnp.float32, -std_in, std_in)
        w3 = jax.random.uniform(k2, (HIDDEN, D_MODEL), jnp.float32, -std_in, std_in)
        w2 = jax.random.uniform(k3, (D_MODEL, HIDDEN), jnp.float32, -std_h, std_h)
        return {'x': x, 'w1': w1, 'w3': w3, 'w2': w2}
    _L0_ffn_all = _L0_ffn_setup()
    _L0_ffn_in = {k: v for k, v in _L0_ffn_all.items() if k in ('w1', 'w3', 'w2')}
    del _L0_ffn_all

    def _L1_xattn_setup():
        import jax, jax.numpy as jnp
        import numpy as np
        B_DIM, T_DIM, C_DIM = (16, 128, 256)

        def _wkv(w, u, k, v):
            Bn, Tn, Cn = k.shape
            NEG_INF = jnp.float32(-1e+38)

            def step(carry, kv_t):
                p, q, o = carry
                kt, vt = kv_t
                no = jnp.maximum(o, u + kt)
                A = jnp.exp(o - no)
                E = jnp.exp(u + kt - no)
                y = (A * p + E * vt) / (A * q + E)
                no2 = jnp.maximum(w + o, kt)
                A2 = jnp.exp(w + o - no2)
                E2 = jnp.exp(kt - no2)
                return ((A2 * p + E2 * vt, A2 * q + E2, no2), y)
            init = (jnp.zeros((Bn, Cn), k.dtype), jnp.zeros((Bn, Cn), k.dtype), jnp.full((Bn, Cn), NEG_INF, k.dtype))
            kT = jnp.moveaxis(k, 1, 0)
            vT = jnp.moveaxis(v, 1, 0)
            _, yT = jax.lax.scan(step, init, (kT, vT))
            return jnp.moveaxis(yT, 0, 1)
        key = jax.random.key(seed)
        k1, k2, k3, k4 = jax.random.split(key, 4)
        w = -jnp.exp(jax.random.normal(k1, (C_DIM,), jnp.float32))
        u = jax.random.normal(k2, (C_DIM,), jnp.float32)
        k = jax.random.normal(k3, (B_DIM, T_DIM, C_DIM), jnp.float32)
        v = jax.random.normal(k4, (B_DIM, T_DIM, C_DIM), jnp.float32)
        return {'B': B_DIM, 'T': T_DIM, 'C': C_DIM, 'w': w, 'u': u, 'k': k, 'v': v}
    _L1_xattn_all = _L1_xattn_setup()
    _L1_xattn_in = {k: v for k, v in _L1_xattn_all.items() if k in ('w', 'u')}
    del _L1_xattn_all

    def _L1_ffn_setup():
        import jax, jax.numpy as jnp
        import numpy as np
        B, S, H, I, E, F, K, R, TOPK = (1, 128, 256, 176, 64, 8, 8, 8, 6)
        ISH = 2 * I

        def _fused_linear(x, W, qa, qb, scale, w):
            out = x @ W.T
            a = jnp.einsum('th,krh->tkr', x, qa)
            b = jnp.einsum('tkr,khr->tkh', a, qb)
            mix = jnp.einsum('tkh,tk->th', b, w)
            return out + scale[None, :] * mix

        def _moe_forward(hidden_states, gate_weight, inv_mapping, mask_up_W, gate_W, gate_qa, gate_qb, gate_scale, up_W, up_qa, up_qb, up_scale, down_W, down_qa, down_qb, down_scale, sh_gate_W, sh_up_W, sh_down_W):
            b, s, h = hidden_states.shape
            x = hidden_states.reshape(-1, h)
            T = x.shape[0]
            scores = jax.nn.softmax(x @ gate_weight.T, axis=-1)
            topk_w, topk_idx = jax.lax.top_k(scores, TOPK)
            w_dense = jnp.zeros((T, E), x.dtype).at[jnp.arange(T)[:, None], topk_idx].add(topk_w)
            flat = w_dense[:, inv_mapping]
            scalar = flat.sum(-1)
            soft = jax.nn.softmax(jnp.where(flat == 0, -1000000000.0, flat), axis=-1)

            def expert(muW, gW, gqa, gqb, gs, uW, uqa, uqb, us, dW, dqa, dqb, ds, w):
                xe = x + w @ muW.T
                gate = jax.nn.silu(_fused_linear(xe, gW, gqa, gqb, gs, w))
                up = _fused_linear(xe, uW, uqa, uqb, us, w)
                return _fused_linear(gate * up, dW, dqa, dqb, ds, w)
            outs = jax.vmap(expert, in_axes=(0,) * 13 + (1,))(mask_up_W, gate_W, gate_qa, gate_qb, gate_scale, up_W, up_qa, up_qb, up_scale, down_W, down_qa, down_qb, down_scale, soft)
            y = jnp.einsum('fth,tf->th', outs, scalar).reshape(b, s, h)
            sh = jax.nn.silu(hidden_states @ sh_gate_W.T) * (hidden_states @ sh_up_W.T) @ sh_down_W.T
            return y + sh
        key = jax.random.key(seed)
        ks = jax.random.split(key, 20)
        g = lambda k, shape, s=0.02: jax.random.normal(k, shape, jnp.float32) * s
        return {'hidden_states': jax.random.normal(ks[0], (B, S, H), jnp.float32), 'gate_weight': g(ks[1], (E, H)), 'inv_mapping': jnp.arange(E, dtype=jnp.int32).reshape(F, K), 'mask_up_W': g(ks[2], (F, H, K)), 'gate_W': g(ks[3], (F, I, H)), 'gate_qa': g(ks[4], (F, K, R, H)), 'gate_qb': g(ks[5], (F, K, I, R)), 'gate_scale': jnp.full((F, I), 0.1, jnp.float32), 'up_W': g(ks[6], (F, I, H)), 'up_qa': g(ks[7], (F, K, R, H)), 'up_qb': g(ks[8], (F, K, I, R)), 'up_scale': jnp.full((F, I), 0.1, jnp.float32), 'down_W': g(ks[9], (F, H, I)), 'down_qa': g(ks[10], (F, K, R, I)), 'down_qb': g(ks[11], (F, K, H, R)), 'down_scale': jnp.full((F, H), 0.1, jnp.float32), 'sh_gate_W': g(ks[12], (ISH, H)), 'sh_up_W': g(ks[13], (ISH, H)), 'sh_down_W': g(ks[14], (H, ISH))}
    _L1_ffn_all = _L1_ffn_setup()
    _L1_ffn_in = {k: v for k, v in _L1_ffn_all.items() if k in ('gate_weight', 'inv_mapping', 'mask_up_W', 'gate_W', 'gate_qa', 'gate_qb', 'gate_scale', 'up_W', 'up_qa', 'up_qb', 'up_scale', 'down_W', 'down_qa', 'down_qb', 'down_scale', 'sh_gate_W', 'sh_up_W', 'sh_down_W')}
    del _L1_ffn_all

    def _L2_xattn_setup():
        import jax, jax.numpy as jnp
        import numpy as np
        D_MODEL = 256
        NUM_HEADS = 16
        HEAD_DIM = D_MODEL // NUM_HEADS

        def _fq_sym(x, axis):
            s = jnp.max(jnp.abs(x), axis=axis, keepdims=True) / 127.0
            s = jnp.maximum(s, 1e-08)
            q = jnp.clip(jnp.round(x / s), -127.0, 127.0) * s
            return x + jax.lax.stop_gradient(q - x)

        def _fq_unsigned(x, axis):
            s = jnp.max(x, axis=axis, keepdims=True) / 255.0
            s = jnp.maximum(s, 1e-08)
            q = jnp.clip(jnp.round(x / s), 0.0, 255.0) * s
            return x + jax.lax.stop_gradient(q - x)
        key = jax.random.key(seed)
        ks = jax.random.split(key, 8)
        B, N, M, C = (2, 256, 64, D_MODEL)
        return {'x': jax.random.normal(ks[0], (B, N, C), jnp.float32), 'cond': jax.random.normal(ks[1], (B, M, C), jnp.float32), 'Wq': jax.random.normal(ks[2], (C, C), jnp.float32) * 0.02, 'bq': jnp.zeros((C,), jnp.float32), 'Wkv': jax.random.normal(ks[3], (C, 2 * C), jnp.float32) * 0.02, 'bkv': jnp.zeros((2 * C,), jnp.float32), 'Wp': jax.random.normal(ks[4], (C, C), jnp.float32) * 0.02, 'bp': jnp.zeros((C,), jnp.float32)}
    _L2_xattn_all = _L2_xattn_setup()
    _L2_xattn_in = {k: v for k, v in _L2_xattn_all.items() if k in ('Wq', 'bq', 'Wkv', 'bkv', 'Wp', 'bp')}
    del _L2_xattn_all

    def _L2_ffn_setup():
        import jax, jax.numpy as jnp
        import numpy as np
        EPS = 1e-08

        def _quantize(w):
            gamma = jnp.mean(jnp.abs(w))
            return jnp.clip(jnp.round(w / (gamma + EPS)), -1.0, 1.0)

        def _bitlinear(x, w):
            return jnp.matmul(x, _quantize(w).T)
        key = jax.random.key(seed)
        k1, k2, k3, k4 = jax.random.split(key, 4)
        d, h = (256, 704)
        x = jax.random.normal(k1, (4, 256, d), dtype=jnp.float32)
        w1 = jax.random.normal(k2, (h, d), dtype=jnp.float32)
        w2 = jax.random.normal(k3, (h, d), dtype=jnp.float32)
        w3 = jax.random.normal(k4, (d, h), dtype=jnp.float32)
        return {'x': x, 'w1': w1, 'w2': w2, 'w3': w3}
    _L2_ffn_all = _L2_ffn_setup()
    _L2_ffn_in = {k: v for k, v in _L2_ffn_all.items() if k in ('w1', 'w2', 'w3')}
    del _L2_ffn_all

    def _L3_xattn_setup():
        import jax, jax.numpy as jnp
        import numpy as np
        EPS = 1e-06
        NUM_HEADS = 16

        def _feature_map(x):
            return jnp.where(x > 0, x + 1.0, jnp.exp(x))
        key = jax.random.key(seed)
        ks = jax.random.split(key, 7)
        B, L, S, D = (4, 512, 512, 256)
        sc = 1.0 / np.sqrt(D)
        return {'query': jax.random.normal(ks[0], (B, L, D), jnp.float32), 'kv': jax.random.normal(ks[1], (B, S, D), jnp.float32), 'Wq': jax.random.normal(ks[2], (D, D), jnp.float32) * sc, 'Wg': jax.random.normal(ks[3], (D, D), jnp.float32) * sc, 'bg': jnp.ones((D,), jnp.float32), 'Wkv': jax.random.normal(ks[4], (2 * D, D), jnp.float32) * sc, 'Wo': jax.random.normal(ks[5], (D, D), jnp.float32) * sc}
    _L3_xattn_all = _L3_xattn_setup()
    _L3_xattn_in = {k: v for k, v in _L3_xattn_all.items() if k in ('Wq', 'Wg', 'bg', 'Wkv', 'Wo')}
    del _L3_xattn_all

    def _L3_ffn_setup():
        import jax, jax.numpy as jnp
        import numpy as np
        _FP8_MAX = 448.0
        _BLOCK = 32
        _EPS = 1e-30

        def _mx_dequant(t):
            rows, feat = t.shape
            blocks = t.reshape(rows, feat // _BLOCK, _BLOCK)
            max_abs = jnp.max(jnp.abs(blocks), axis=-1)
            scales = jnp.maximum(max_abs / _FP8_MAX, _EPS)
            q = (blocks / scales[..., None]).astype(jnp.float8_e4m3fn).astype(jnp.float32)
            return (q * scales[..., None]).reshape(rows, feat)

        def _mx_linear(x2d, w):
            return _mx_dequant(x2d) @ _mx_dequant(w).T
        key = jax.random.key(seed)
        k1, k2, k3, k4 = jax.random.split(key, 4)
        B, S, H, I = (2, 128, 256, 1024)
        return {'x': jax.random.normal(k1, (B, S, H), dtype=jnp.float32), 'gate_w': jax.random.normal(k2, (I, H), dtype=jnp.float32) * 0.02, 'up_w': jax.random.normal(k3, (I, H), dtype=jnp.float32) * 0.02, 'down_w': jax.random.normal(k4, (H, I), dtype=jnp.float32) * 0.02}
    _L3_ffn_all = _L3_ffn_setup()
    _L3_ffn_in = {k: v for k, v in _L3_ffn_all.items() if k in ('gate_w', 'up_w', 'down_w')}
    del _L3_ffn_all
    return {'x': x, 'itok_BxS_13_99985': itok_BxS_13_99985, 'ctx_2048': ctx_2048, 'L0_ffn_w1': _L0_ffn_in['w1'], 'L0_ffn_w3': _L0_ffn_in['w3'], 'L0_ffn_w2': _L0_ffn_in['w2'], 'L1_xattn_w': _L1_xattn_in['w'], 'L1_xattn_u': _L1_xattn_in['u'], 'L1_ffn_gate_weight': _L1_ffn_in['gate_weight'], 'L1_ffn_inv_mapping': _L1_ffn_in['inv_mapping'], 'L1_ffn_mask_up_W': _L1_ffn_in['mask_up_W'], 'L1_ffn_gate_W': _L1_ffn_in['gate_W'], 'L1_ffn_gate_qa': _L1_ffn_in['gate_qa'], 'L1_ffn_gate_qb': _L1_ffn_in['gate_qb'], 'L1_ffn_gate_scale': _L1_ffn_in['gate_scale'], 'L1_ffn_up_W': _L1_ffn_in['up_W'], 'L1_ffn_up_qa': _L1_ffn_in['up_qa'], 'L1_ffn_up_qb': _L1_ffn_in['up_qb'], 'L1_ffn_up_scale': _L1_ffn_in['up_scale'], 'L1_ffn_down_W': _L1_ffn_in['down_W'], 'L1_ffn_down_qa': _L1_ffn_in['down_qa'], 'L1_ffn_down_qb': _L1_ffn_in['down_qb'], 'L1_ffn_down_scale': _L1_ffn_in['down_scale'], 'L1_ffn_sh_gate_W': _L1_ffn_in['sh_gate_W'], 'L1_ffn_sh_up_W': _L1_ffn_in['sh_up_W'], 'L1_ffn_sh_down_W': _L1_ffn_in['sh_down_W'], 'L2_xattn_Wq': _L2_xattn_in['Wq'], 'L2_xattn_bq': _L2_xattn_in['bq'], 'L2_xattn_Wkv': _L2_xattn_in['Wkv'], 'L2_xattn_bkv': _L2_xattn_in['bkv'], 'L2_xattn_Wp': _L2_xattn_in['Wp'], 'L2_xattn_bp': _L2_xattn_in['bp'], 'L2_ffn_w1': _L2_ffn_in['w1'], 'L2_ffn_w2': _L2_ffn_in['w2'], 'L2_ffn_w3': _L2_ffn_in['w3'], 'L3_xattn_Wq': _L3_xattn_in['Wq'], 'L3_xattn_Wg': _L3_xattn_in['Wg'], 'L3_xattn_bg': _L3_xattn_in['bg'], 'L3_xattn_Wkv': _L3_xattn_in['Wkv'], 'L3_xattn_Wo': _L3_xattn_in['Wo'], 'L3_ffn_gate_w': _L3_ffn_in['gate_w'], 'L3_ffn_up_w': _L3_ffn_in['up_w'], 'L3_ffn_down_w': _L3_ffn_in['down_w']}

def reference(x, itok_BxS_13_99985, ctx_2048, L0_ffn_w1, L0_ffn_w3, L0_ffn_w2, L1_xattn_w, L1_xattn_u, L1_ffn_gate_weight, L1_ffn_inv_mapping, L1_ffn_mask_up_W, L1_ffn_gate_W, L1_ffn_gate_qa, L1_ffn_gate_qb, L1_ffn_gate_scale, L1_ffn_up_W, L1_ffn_up_qa, L1_ffn_up_qb, L1_ffn_up_scale, L1_ffn_down_W, L1_ffn_down_qa, L1_ffn_down_qb, L1_ffn_down_scale, L1_ffn_sh_gate_W, L1_ffn_sh_up_W, L1_ffn_sh_down_W, L2_xattn_Wq, L2_xattn_bq, L2_xattn_Wkv, L2_xattn_bkv, L2_xattn_Wp, L2_xattn_bp, L2_ffn_w1, L2_ffn_w2, L2_ffn_w3, L3_xattn_Wq, L3_xattn_Wg, L3_xattn_bg, L3_xattn_Wkv, L3_xattn_Wo, L3_ffn_gate_w, L3_ffn_up_w, L3_ffn_down_w):
    import jax
    import jax.numpy as jnp

    def _L0_xattn_ref(hidden_states, token_ids, Wg, Wu, Wd):
        import jax, jax.numpy as jnp
        import numpy as np
        B, S, D = (4, 512, 256)
        E = 4
        F = 1024 // E
        VOCAB = 12500
        tokens_per_expert = VOCAB // E
        tid = jnp.clip(token_ids, 0, VOCAB - 1)
        expert_ids = jnp.minimum(tid // tokens_per_expert, E - 1)
        out = jnp.zeros_like(hidden_states)
        for e in range(E):
            g = jax.nn.silu(jnp.einsum('bsd,fd->bsf', hidden_states, Wg[e]))
            u = jnp.einsum('bsd,fd->bsf', hidden_states, Wu[e])
            y = jnp.einsum('bsf,df->bsd', g * u, Wd[e])
            out = jnp.where((expert_ids == e)[..., None], y, out)
        return out

    def _L0_ffn_ref(x, w1, w3, w2):
        import jax, jax.numpy as jnp
        import numpy as np
        D_MODEL = 256
        HIDDEN = int(2 * D_MODEL * 4 / 3)

        def ternary_quant(w):
            s = jnp.mean(jnp.abs(w))
            q = jnp.clip(jnp.round(w / s), -1.0, 1.0) * s
            return w + jax.lax.stop_gradient(q - w)
        w1q = ternary_quant(w1)
        w3q = ternary_quant(w3)
        w2q = ternary_quant(w2)
        h1 = jnp.einsum('bsd,hd->bsh', x, w1q)
        h3 = jnp.einsum('bsd,hd->bsh', x, w3q)
        g = jax.nn.silu(h1) * h3
        return jnp.einsum('bsh,dh->bsd', g, w2q)

    def _L1_xattn_ref(B, T, C, w, u, k, v):
        import jax, jax.numpy as jnp
        import numpy as np
        B_DIM, T_DIM, C_DIM = (16, 128, 256)

        def _wkv(w, u, k, v):
            Bn, Tn, Cn = k.shape
            NEG_INF = jnp.float32(-1e+38)

            def step(carry, kv_t):
                p, q, o = carry
                kt, vt = kv_t
                no = jnp.maximum(o, u + kt)
                A = jnp.exp(o - no)
                E = jnp.exp(u + kt - no)
                y = (A * p + E * vt) / (A * q + E)
                no2 = jnp.maximum(w + o, kt)
                A2 = jnp.exp(w + o - no2)
                E2 = jnp.exp(kt - no2)
                return ((A2 * p + E2 * vt, A2 * q + E2, no2), y)
            init = (jnp.zeros((Bn, Cn), k.dtype), jnp.zeros((Bn, Cn), k.dtype), jnp.full((Bn, Cn), NEG_INF, k.dtype))
            kT = jnp.moveaxis(k, 1, 0)
            vT = jnp.moveaxis(v, 1, 0)
            _, yT = jax.lax.scan(step, init, (kT, vT))
            return jnp.moveaxis(yT, 0, 1)
        return _wkv(w, u, k, v)

    def _L1_ffn_ref(hidden_states, gate_weight, inv_mapping, mask_up_W, gate_W, gate_qa, gate_qb, gate_scale, up_W, up_qa, up_qb, up_scale, down_W, down_qa, down_qb, down_scale, sh_gate_W, sh_up_W, sh_down_W):
        import jax, jax.numpy as jnp
        import numpy as np
        B, S, H, I, E, F, K, R, TOPK = (1, 128, 256, 176, 64, 8, 8, 8, 6)
        ISH = 2 * I

        def _fused_linear(x, W, qa, qb, scale, w):
            out = x @ W.T
            a = jnp.einsum('th,krh->tkr', x, qa)
            b = jnp.einsum('tkr,khr->tkh', a, qb)
            mix = jnp.einsum('tkh,tk->th', b, w)
            return out + scale[None, :] * mix

        def _moe_forward(hidden_states, gate_weight, inv_mapping, mask_up_W, gate_W, gate_qa, gate_qb, gate_scale, up_W, up_qa, up_qb, up_scale, down_W, down_qa, down_qb, down_scale, sh_gate_W, sh_up_W, sh_down_W):
            b, s, h = hidden_states.shape
            x = hidden_states.reshape(-1, h)
            T = x.shape[0]
            scores = jax.nn.softmax(x @ gate_weight.T, axis=-1)
            topk_w, topk_idx = jax.lax.top_k(scores, TOPK)
            w_dense = jnp.zeros((T, E), x.dtype).at[jnp.arange(T)[:, None], topk_idx].add(topk_w)
            flat = w_dense[:, inv_mapping]
            scalar = flat.sum(-1)
            soft = jax.nn.softmax(jnp.where(flat == 0, -1000000000.0, flat), axis=-1)

            def expert(muW, gW, gqa, gqb, gs, uW, uqa, uqb, us, dW, dqa, dqb, ds, w):
                xe = x + w @ muW.T
                gate = jax.nn.silu(_fused_linear(xe, gW, gqa, gqb, gs, w))
                up = _fused_linear(xe, uW, uqa, uqb, us, w)
                return _fused_linear(gate * up, dW, dqa, dqb, ds, w)
            outs = jax.vmap(expert, in_axes=(0,) * 13 + (1,))(mask_up_W, gate_W, gate_qa, gate_qb, gate_scale, up_W, up_qa, up_qb, up_scale, down_W, down_qa, down_qb, down_scale, soft)
            y = jnp.einsum('fth,tf->th', outs, scalar).reshape(b, s, h)
            sh = jax.nn.silu(hidden_states @ sh_gate_W.T) * (hidden_states @ sh_up_W.T) @ sh_down_W.T
            return y + sh
        return _moe_forward(hidden_states, gate_weight, inv_mapping, mask_up_W, gate_W, gate_qa, gate_qb, gate_scale, up_W, up_qa, up_qb, up_scale, down_W, down_qa, down_qb, down_scale, sh_gate_W, sh_up_W, sh_down_W)

    def _L2_xattn_ref(x, cond, Wq, bq, Wkv, bkv, Wp, bp):
        import jax, jax.numpy as jnp
        import numpy as np
        D_MODEL = 256
        NUM_HEADS = 16
        HEAD_DIM = D_MODEL // NUM_HEADS

        def _fq_sym(x, axis):
            s = jnp.max(jnp.abs(x), axis=axis, keepdims=True) / 127.0
            s = jnp.maximum(s, 1e-08)
            q = jnp.clip(jnp.round(x / s), -127.0, 127.0) * s
            return x + jax.lax.stop_gradient(q - x)

        def _fq_unsigned(x, axis):
            s = jnp.max(x, axis=axis, keepdims=True) / 255.0
            s = jnp.maximum(s, 1e-08)
            q = jnp.clip(jnp.round(x / s), 0.0, 255.0) * s
            return x + jax.lax.stop_gradient(q - x)
        B, N, C = x.shape
        H, hd = (NUM_HEADS, HEAD_DIM)
        q = (x @ Wq + bq).reshape(1, B * N, H, hd)
        kv = (cond @ Wkv + bkv).reshape(1, -1, 2, H, hd)
        k, v = (kv[:, :, 0], kv[:, :, 1])
        scale = 1.0 / np.sqrt(hd).astype(np.float32)
        q = jnp.transpose(q * scale, (0, 2, 1, 3))
        k = jnp.transpose(k, (0, 2, 1, 3))
        v = jnp.transpose(v, (0, 2, 1, 3))
        q = _fq_sym(q, axis=-1)
        k = _fq_sym(k, axis=-1)
        v = _fq_sym(v, axis=2)
        attn = jnp.einsum('bhqd,bhkd->bhqk', q, k)
        attn = jax.nn.softmax(attn.astype(jnp.float32), axis=-1)
        attn = _fq_unsigned(attn, axis=-1)
        out = jnp.einsum('bhqk,bhkd->bhqd', attn, v)
        out = jnp.transpose(out, (0, 2, 1, 3)).reshape(B, N, C)
        return out @ Wp + bp

    def _L2_ffn_ref(x, w1, w2, w3):
        import jax, jax.numpy as jnp
        import numpy as np
        EPS = 1e-08

        def _quantize(w):
            gamma = jnp.mean(jnp.abs(w))
            return jnp.clip(jnp.round(w / (gamma + EPS)), -1.0, 1.0)

        def _bitlinear(x, w):
            return jnp.matmul(x, _quantize(w).T)
        x1 = _bitlinear(x, w1)
        x2 = _bitlinear(x, w2)
        hidden = jax.nn.sigmoid(x1) * x2
        return _bitlinear(hidden, w3)

    def _L3_xattn_ref(query, kv, Wq, Wg, bg, Wkv, Wo):
        import jax, jax.numpy as jnp
        import numpy as np
        EPS = 1e-06
        NUM_HEADS = 16

        def _feature_map(x):
            return jnp.where(x > 0, x + 1.0, jnp.exp(x))
        B, L, D = query.shape
        S = kv.shape[1]
        H = NUM_HEADS
        hd = D // H
        q = query @ Wq.T
        gate = jax.nn.sigmoid(query @ Wg.T + bg)
        kvp = kv @ Wkv.T
        k, v = jnp.split(kvp, 2, axis=-1)
        q = _feature_map(q.reshape(B, L, H, hd).transpose(0, 2, 1, 3))
        k = _feature_map(k.reshape(B, S, H, hd).transpose(0, 2, 1, 3))
        v = v.reshape(B, S, H, hd).transpose(0, 2, 1, 3)
        kv_summary = jnp.einsum('bhsd,bhse->bhde', k, v)
        k_sum = k.sum(axis=-2)
        z = 1.0 / (jnp.einsum('bhld,bhd->bhl', q, k_sum)[..., None] + EPS)
        attn = jnp.einsum('bhld,bhde->bhle', q, kv_summary) * z
        attn = attn.transpose(0, 2, 1, 3).reshape(B, L, D)
        out = attn * gate @ Wo.T
        return out

    def _L3_ffn_ref(x, gate_w, up_w, down_w):
        import jax, jax.numpy as jnp
        import numpy as np
        _FP8_MAX = 448.0
        _BLOCK = 32
        _EPS = 1e-30

        def _mx_dequant(t):
            rows, feat = t.shape
            blocks = t.reshape(rows, feat // _BLOCK, _BLOCK)
            max_abs = jnp.max(jnp.abs(blocks), axis=-1)
            scales = jnp.maximum(max_abs / _FP8_MAX, _EPS)
            q = (blocks / scales[..., None]).astype(jnp.float8_e4m3fn).astype(jnp.float32)
            return (q * scales[..., None]).reshape(rows, feat)

        def _mx_linear(x2d, w):
            return _mx_dequant(x2d) @ _mx_dequant(w).T
        B, S, H = x.shape
        x2d = x.reshape(B * S, H)
        gate = _mx_linear(x2d, gate_w)
        up = _mx_linear(x2d, up_w)
        h = jax.nn.silu(gate) * up
        out = _mx_linear(h, down_w)
        return out.reshape(B, S, H)
    x = x + _L0_xattn_ref(_layernorm(x, axis=-1), itok_BxS_13_99985, ctx_2048, ctx_2048, ctx_2048)
    x = x + _L0_ffn_ref(_layernorm(x, axis=-1), L0_ffn_w1, L0_ffn_w3, L0_ffn_w2)
    x = x + _L1_xattn_ref(4, 256, 256, L1_xattn_w, L1_xattn_u, _layernorm(x, axis=-1), ctx_2048)
    x = x + _L1_ffn_ref(_layernorm(x, axis=-1), L1_ffn_gate_weight, L1_ffn_inv_mapping, L1_ffn_mask_up_W, L1_ffn_gate_W, L1_ffn_gate_qa, L1_ffn_gate_qb, L1_ffn_gate_scale, L1_ffn_up_W, L1_ffn_up_qa, L1_ffn_up_qb, L1_ffn_up_scale, L1_ffn_down_W, L1_ffn_down_qa, L1_ffn_down_qb, L1_ffn_down_scale, L1_ffn_sh_gate_W, L1_ffn_sh_up_W, L1_ffn_sh_down_W)
    x = x + _L2_xattn_ref(_layernorm(x, axis=-1), ctx_2048, L2_xattn_Wq, L2_xattn_bq, L2_xattn_Wkv, L2_xattn_bkv, L2_xattn_Wp, L2_xattn_bp)
    x = x + _L2_ffn_ref(_layernorm(x, axis=-1), L2_ffn_w1, L2_ffn_w2, L2_ffn_w3)
    x = x + _L3_xattn_ref(_layernorm(x, axis=-1), ctx_2048, L3_xattn_Wq, L3_xattn_Wg, L3_xattn_bg, L3_xattn_Wkv, L3_xattn_Wo)
    x = x + _L3_ffn_ref(_layernorm(x, axis=-1), L3_ffn_gate_w, L3_ffn_up_w, L3_ffn_down_w)
    return x

_drawn_inputs = setup_inputs


def setup_inputs(seed=0):
    import zlib

    import numpy as np

    out = dict(_drawn_inputs(seed))
    spreads = {'L1_ffn_gate_scale': (0.10000000149011612, 0.6),
     'L1_ffn_up_scale': (0.10000000149011612, 0.6),
     'L1_ffn_down_scale': (0.10000000149011612, 0.6),
     'L2_xattn_bq': (0.0, 2.0),
     'L2_xattn_bkv': (0.0, 0.548),
     'L2_xattn_bp': (0.0, 0.414),
     'L3_xattn_bg': (1.0, 0.6)}
    factors = {'L1_xattn_w': 200.0,
     'L1_xattn_u': 8.0,
     'L1_ffn_gate_weight': 8.0,
     'L1_ffn_mask_up_W': 8.0,
     'L1_ffn_gate_W': 8.0,
     'L1_ffn_gate_qa': 8.0,
     'L1_ffn_gate_qb': 8.0,
     'L1_ffn_up_W': 8.0,
     'L1_ffn_up_qa': 8.0,
     'L1_ffn_up_qb': 8.0,
     'L1_ffn_down_W': 8.0,
     'L1_ffn_down_qa': 8.0,
     'L1_ffn_down_qb': 8.0,
     'L2_xattn_Wq': 64.0,
     'L2_xattn_Wkv': 64.0,
     'L3_xattn_Wq': 200.0,
     'L3_xattn_Wg': 64.0,
     'L3_xattn_Wkv': 64.0,
     'L3_xattn_Wo': 64.0,
     'L3_ffn_gate_w': 8.0,
     'L3_ffn_up_w': 8.0,
     'L3_ffn_down_w': 8.0,
     'L1_ffn_sh_gate_W': 7.046,
     'L1_ffn_sh_up_W': 6.905,
     'L1_ffn_sh_down_W': 6.916,
     'L2_xattn_Wp': 4.031}
    for name, (base, spread) in spreads.items():
        noise = np.random.default_rng([zlib.crc32(name.encode()), seed]).standard_normal(out[name].shape)
        drawn = base * np.exp(spread * noise) if base else spread * noise
        out[name] = jnp.asarray(drawn.astype(out[name].dtype))
    for name, factor in factors.items():
        out[name] = (out[name] * factor).astype(out[name].dtype)
    return out
```

```python
from contextlib import ExitStack
import math

import concourse.bass as bass
from concourse import mybir

ALU = mybir.AluOpType
ACT = mybir.ActivationFunctionType
AX = mybir.AxisListType
F32 = mybir.dt.float32
BF16 = mybir.dt.bfloat16
I32 = mybir.dt.int32

P = 128
D = 256
KC = D // P
BATCH = 4
SEQ = 256
TOK = BATCH * SEQ
TT = TOK // P
HALF = 512
TH = TOK // HALF

TOKENS_PER_EXPERT = 12500 // 4
NF = 8
NK = 8
NR = 8
NE = NF * NK
TOP = 6
INNER = 176
IC = 88
NI = INNER // IC
GATES = NE + NF
SLOT_LOADED = 16 * 15
HEADS = 16
HD = D // HEADS
ROUND = 1.5 * 2.0 ** 23
MX_BLOCK = 32
MX_MAX = 448.0
LN_EPS = 1e-5


def chunks(n):
    return [(a, min(P, n - a)) for a in range(0, n, P)]


def build(nc, a, out, stop=None):
    H0 = a["L0_ffn_w1"].shape[0]
    H1 = a["L1_ffn_sh_gate_W"].shape[0]
    H2 = a["L2_ffn_w1"].shape[0]
    H3 = a["L3_ffn_gate_w"].shape[0]

    with ExitStack() as ctx:
        def sb(name, shape, dt=F32):
            return ctx.enter_context(nc.sbuf_tensor(name, shape, dt))

        def sem(name):
            return ctx.enter_context(nc.semaphore(name))

        ps = ctx.enter_context(nc.psum_tensor("ps", [P, 8, 512], F32))
        x_t = sb("x_t", [P, KC, TOK])
        xn_t = sb("xn_t", [P, KC, TOK])
        xc = sb("xc", [P, TH, KC, HALF])
        sq = sb("sq", [P, KC, HALF])
        sd = sb("sd", [P, TH, HALF])
        ctx_t = sb("ctx_t", [P, KC, TOK])
        act_buf = sb("act_buf", [P, 2, HALF])
        hid_buf = sb("hid_buf", [P, 2, HALF])
        ident = sb("ident", [P, P])
        ident_b = sb("ident_b", [P, P], BF16)
        ones = sb("ones", [P, P])
        mean_w = sb("mean_w", [P, P])
        head_mask = sb("head_mask", [P, P])
        eps_col = sb("eps_col", [P, 1])

        arena = sb("arena", [P, 150 * 256])

        class Cut:
            def __init__(self, kb):
                self.at = int(kb * 256)

            def __call__(self, shape, dt=F32, parts=P):
                n = 1
                for s in shape:
                    n *= s
                words = n if dt in (F32, I32) else (n + 1) // 2
                v = arena[0:parts, self.at:self.at + words]
                self.at += words
                assert self.at <= 150 * 256, self.at / 256
                if dt != F32:
                    v = v.bitcast(dt)
                if len(shape) > 1:
                    names = "abcd"[:len(shape)]
                    v = v.rearrange(f"p ({' '.join(names)}) -> p {' '.join(names)}",
                                    **{c: s for c, s in zip(names[1:], shape[1:])})
                return v

        c = Cut(0)
        ctx_nat = c([TT, D])
        x_nat = c([TT, D])
        tid = c([TOK], I32)
        ge_mask = c([3, TOK], BF16)
        tok_mask = c([4, TOK], BF16)
        c = Cut(c.at / 256)
        w_l0 = [c([6, D]), c([6, D]), c([KC, H0])]
        wt_l0 = [c([KC, H0]), c([KC, H0]), c([6, D])]
        tern_tmp = c([6 * D])
        tern_s = c([32])
        assert c.at / 256 <= 75
        c = Cut(75)
        w_l1 = [c([3, D]), c([3, D]), c([KC, H1])]
        wt_l1 = [c([KC, H1]), c([KC, H1]), c([3, D])]
        gw_nat = c([D])
        gw_t = c([KC, NE])
        mu_nat = c([KC, NF, NK])
        mu_t = c([D])
        rep = c([P])
        sc_rep = c([P])
        group_mask = c([NF])
        inv_row = c([NE], I32)
        inv_f = c([3, NE])
        e_col = c([1])
        esel = c([NE])
        gates_t = c([TOK])
        gates_f = [c([TOK]) for _ in range(2)]
        moe_at = c.at / 256
        slots = []
        for _ in range(2):
            slots.append(dict(
                g=c([NI, D]), u=c([NI, D]), d=c([KC, INNER]), qa=c([D]), dqa=c([INNER]),
                qb=c([NI, P]), dqb=c([KC, NK * NR]), gs=c([NI]), us=c([NI]), ds=c([KC]),
                gT=c([KC, INNER]), uT=c([KC, INNER]), dT=c([NI, D]), qaT=c([KC, P]), dqbT=c([D]),
                dqaT=c([NI, NK * NR]), qbT=c([INNER])))
        c = Cut(0)
        wk = dict(w=c([KC]), u=c([KC]), wb=c([SEQ]), o=c([BATCH, SEQ + 1]), p=c([BATCH, SEQ + 1]),
                  q=c([BATCH, SEQ + 1]), e1=c([BATCH, SEQ]), e2=c([BATCH, SEQ]), ev=c([BATCH, SEQ]),
                  no=c([BATCH, SEQ]), e3=c([BATCH, SEQ]), e4=c([BATCH, SEQ]), num=c([BATCH, SEQ]),
                  den=c([BATCH, SEQ]))
        c = Cut(0)
        rt = dict(mx=c([TT]), sum=c([TT]), e=c([TT, NE]), sc=c([TT, NE + 2]), top=c([TT, 8]),
                  mr=c([TT, NE + 2]), wd=c([TT, NE]), wdT=c([TOK]), fl=c([TT, NE]), fm=c([TT, NE]),
                  gmx=c([TT * NF]), gt=c([TT, GATES]))
        moe = dict(xe=c([TH, KC, HALF]), wr=c([HALF]), sr=c([HALF]), aw=c([HALF]), awd=c([HALF]),
                   s=c([2, HALF]), h=c([NI, HALF]))
        assert c.at / 256 < 75
        c = Cut(0)
        q_s = c([HEADS, TOK], BF16)
        k_s = c([HEADS, TOK], BF16)
        v_tok = c([TT, D], BF16)
        q_tok = c([TT, D])
        k_tok = c([TT, D])
        at_q3 = c.at / 256
        q3 = c([TT, HEADS, 3, HD], BF16)
        k3 = c([TT, HEADS, 3, HD], BF16)
        v_t = c([KC, TOK])
        vn_t = c([KC, TOK], BF16)
        k_end = c.at / 256
        att_small = dict(amax=c([TT * HEADS]), inv=c([TT * HEADS]), sq=c([TT, HEADS]), sk=c([TT * HEADS]),
                         z=c([TT, HEADS]), rz=c([HEADS]), nm=c([2]), bias=c([2]), sv=c([KC]), vinv=c([KC]),
                         vmax=c([KC]), bvp=c([KC]), bpp=c([KC]), vout=c([KC]))
        bq_row = c([D], parts=1)
        bk_row = c([D], parts=1)
        wq2 = c([KC, D])
        wkv2 = c([KC, 2 * D])
        wp2 = c([KC, D])
        att_end = c.at / 256
        c2 = Cut(at_q3)
        att_e = c2([2, TOK])
        att_p = c2([2, TOK], BF16)
        att_pt = c2([2, TT, P], BF16)
        assert c2.at / 256 <= k_end
        o_tok, o_t = q_tok, k_tok.rearrange("p a b -> p (a b)").rearrange("p (k t) -> p k t", k=KC)
        q_tmp = v_t.rearrange("p k t -> p (k t)").rearrange("p (a b) -> p a b", a=TT)
        c = Cut(0)
        w_l2 = [c([6, D]), c([6, D]), c([KC, H2])]
        wt_l2 = [c([KC, H2]), c([KC, H2]), c([6, D])]
        tern_tmp2 = c([6 * D])
        tern_s2 = c([32])
        lx_nat = [c([KC, D]), c([KC, D]), c([KC, D]), c([4, D])]
        lx_t = [c([KC, D]), c([KC, D]), c([KC, D]), c([KC, 2 * D])]
        kf = c([TT, D])
        v1 = c([TT, KC, P + 1])
        lx_min = c([2, D])
        lx_exp = c([2, D])
        bd = c([BATCH, KC, P])
        dd = c([BATCH, KC, P])
        bg = c([KC])
        lx_qmin = c([KC, HALF])
        lx_q = c([KC, HALF])
        lx_gate = c([KC, HALF])
        lx_den = c([KC, HALF])
        lx_o = c([KC, HALF])
        c = Cut(0)
        w_l3 = [c([8, D]), c([8, D]), c([KC, H3])]
        wt_l3 = [c([KC, H3]), c([KC, H3]), c([8, D])]
        mxq = [c([8 * D]) for _ in range(3)]
        mx_s = [c([64]) for _ in range(3)]
        xn_tok = c([TT, D])
        xq_t = c([KC, TOK])
        h_tok = c([H3])
        h_act = c([H3])
        hq_t = c([8, P])
        x_tok = c([TT, D])
        res = c([2, D])

        dve_step, act_step, pool_step = sem("dve_step"), sem("act_step"), sem("pool_step")
        const_ready = sem("const_ready")
        load = {n: sem("load_" + n) for n in ("ctx", "x", "tid", "l0", "l1", "mu", "wku", "inv", "moe0", "moe1",
                                               "l2x", "l2", "l3x", "l3")}
        turned, evac_act, evac_dve = sem("turned"), sem("evac_act"), sem("evac_dve")
        weights_fixed = sem("weights_fixed")
        x_ready = sem("x_ready")
        ln_mean, ln_xc, ln_sq, ln_var, ln_sd, xn_ready = (sem(n) for n in (
            "ln_mean", "ln_xc", "ln_sq", "ln_var", "ln_sd", "xn_ready"))
        hid_ready, act_ready, gated, hid_used, y_ready = (sem(n) for n in (
            "hid_ready", "act_ready", "gated", "hid_used", "y_ready"))
        tern_part, tern_sum = sem("tern_part"), sem("tern_sum")
        exp_in, exp_out = sem("exp_in"), sem("exp_out")
        rt_logits, rt_wd, rt_wdt, rt_wdt_sb, rt_flat, rt_gt, rt_gatest, rt_gates_sb = (sem(n) for n in (
            "rt_logits", "rt_wd", "rt_wdt", "rt_wdt_sb", "rt_flat", "rt_gt", "rt_gatest", "rt_gates_sb"))
        moe_masked, moe_fixed, moe_turned, moe_ev_act, moe_ev_dve = (sem(n) for n in (
            "moe_masked", "moe_fixed", "moe_turned", "moe_ev_act", "moe_ev_dve"))
        moe_mu, moe_xe, moe_wr, moe_a, moe_aw, moe_h, moe_s, moe_sm, moe_hg, moe_ad, moe_awd, moe_y, moe_x = (
            sem(n) for n in ("moe_mu", "moe_xe", "moe_wr", "moe_a", "moe_aw", "moe_h", "moe_s", "moe_sm",
                             "moe_hg", "moe_ad", "moe_awd", "moe_y", "moe_x"))
        pj_ready, pj_used, v_ready, qk_split, head_turned, head_copied = (sem(n) for n in (
            "pj_ready", "pj_used", "v_ready", "qk_split", "head_turned", "head_copied"))
        vn_ready, vn_turned, v_copied = sem("vn_ready"), sem("vn_turned"), sem("v_copied")
        att_s, att_max, att_bias, att_exp, att_round, att_t, att_eva, att_evd, att_o, att_o_used = (sem(n) for n in (
            "att_s", "att_max", "att_bias", "att_exp", "att_round", "att_t", "att_eva", "att_evd", "att_o",
            "att_o_used"))
        att_rz = sem("att_rz")
        round_starts = sem("round_starts")
        ot_turned, ot_copied, att_done = sem("ot_turned"), sem("ot_copied"), sem("att_done")
        lx_kv, lx_min_r, lx_exp_r, lx_kf, lx_v, lx_sum, lx_bd = (sem(n) for n in (
            "lx_kv", "lx_min_r", "lx_exp_r", "lx_kf", "lx_v", "lx_sum", "lx_bd"))
        lx_qg, lx_qmin_r, lx_act, lx_qf, lx_att, lx_or = (sem(n) for n in (
            "lx_qg", "lx_qmin_r", "lx_act", "lx_qf", "lx_att", "lx_or"))
        xt_turned, xt_copied, xq_ready, xq_turned, xq_copied = (sem(n) for n in (
            "xt_turned", "xt_copied", "xq_ready", "xq_turned", "xq_copied"))
        m_gu, m_act, m_h, m_ht, m_htc, m_o, m_res = (sem(n) for n in (
            "m_gu", "m_act", "m_h", "m_ht", "m_htc", "m_o", "m_res"))
        stored = [sem("stored_even"), sem("stored_odd")]

        groups = []

        def turn_in(rows, nat, dst, wait, fixed):
            full = rows // P
            todo = [(r, 2) for r in range(0, full - 1, 2)]
            if full % 2:
                todo.append((full - 1, 1))
            todo = [(r * P, [P] * n) for r, n in todo]
            if rows % P:
                todo.append((full * P, [rows % P]))
            for r0, ws in todo:
                turns = [(P, w, k * 256 + j * P, nat[0:w, r0 // P + j, k * P:(k + 1) * P])
                         for k in range(KC) for j, w in enumerate(ws)]
                n = sum(ws)
                groups.append((turns, [(dst[:, :, r0:r0 + n], P, 0, 256, n)], wait, fixed))

        def turn_out(cols, nat, dst, wait, fixed):
            full = cols // P
            for c0 in range(0, full, 2):
                n = min(2, full - c0)
                turns = [(P, P, j * 256 + r * P, nat[:, r, (c0 + j) * P:(c0 + j + 1) * P])
                         for j in range(n) for r in range(KC)]
                groups.append((turns, [(dst[:, c0:c0 + n, :], P, 0, 256, 256)], wait, fixed))
            if cols % P:
                w = cols % P
                turns = [(w, P, r * P, nat[:, r, full * P:cols]) for r in range(KC)]
                groups.append((turns, [(dst[0:w, full:full + 1, :], w, 0, 256, 256)], wait, fixed))

        marks = {}

        def mark(name, f):
            first = len(groups)
            f()
            marks[name] = (first, len(groups))

        def tokens_turned(nat, dst, wait):
            for h in range(TH):
                for k in range(KC):
                    turns = [(P, P, j * P, nat[:, 4 * h + j, k * P:(k + 1) * P]) for j in range(4)]
                    groups.append((turns, [(dst[:, k, h * HALF:(h + 1) * HALF].unsqueeze(1), P, 0, 512, 512)],
                                   wait, 0))

        mark("x", lambda: tokens_turned(x_nat, x_t, (load["x"], 16)))
        mark("ctx", lambda: tokens_turned(ctx_nat, ctx_t, (load["ctx"], 16)))

        def three(ws, wts, h, wait, fixed):
            turn_in(h, ws[0], wts[0], wait, fixed)
            turn_in(h, ws[1], wts[1], wait, fixed)
            turn_out(h, ws[2], wts[2], wait, fixed)
        mark("l0", lambda: three(w_l0, wt_l0, H0, None, 1))
        mark("l1", lambda: three(w_l1, wt_l1, H1, (load["l1"], 16 * 5), 0))

        def small():
            turns = [(P, NE, k * NE, gw_nat[0:NE, k * P:(k + 1) * P]) for k in range(KC)]
            groups.append((turns, [(gw_t[:, :, :], P, 0, NE, NE)], (load["mu"], 16 * 3), 0))
            turns = [(NE, P, k * P, mu_nat[:, k, :, :].rearrange("p f k -> p (f k)")) for k in range(KC)]
            groups.append((turns, [(mu_t[0:NE, :].unsqueeze(1), NE, 0, 256, 256)], (load["mu"], 16 * 3), 0))
        mark("small", small)
        mark("l2", lambda: three(w_l2, wt_l2, H2, None, 2))

        def lx():
            turn_in(D, lx_nat[0], lx_t[0], (load["l3x"], 16 * 5), 0)
            turn_in(D, lx_nat[1], lx_t[1], (load["l3x"], 16 * 5), 0)
            turn_in(D, lx_nat[2], lx_t[2], (load["l3x"], 16 * 5), 0)
            turn_in(2 * D, lx_nat[3], lx_t[3], (load["l3x"], 16 * 5), 0)
        mark("lx", lx)
        mark("l3", lambda: three(w_l3, wt_l3, H3, None, 3))

        def evacuated(eng, upto):
            eng.wait_ge(evac_act, (upto + 1) // 2)
            if upto // 2:
                eng.wait_ge(evac_dve, upto // 2)

        def pe_turn(pe, name):
            for g in range(*marks[name]):
                turns, _, wait, fixed = groups[g]
                if g >= 2:
                    pe.wait_ge(evac_dve if g % 2 else evac_act, g // 2)
                if wait:
                    pe.wait_ge(*wait)
                if fixed:
                    pe.wait_ge(weights_fixed, fixed)
                for m, w, col, src in turns:
                    last = pe.transpose(ps[0:m, 6 + g % 2, col:col + w], src, ident[0:src.shape[0], 0:src.shape[0]])
                last.then_inc(turned, 1)

        def copy_out(eng, name, parity):
            for g in range(*marks[name]):
                if g % 2 != parity:
                    continue
                eng.wait_ge(turned, g + 1)
                for dst, m, col, step, n in groups[g][1]:
                    k = dst.shape[1]
                    src = ps[0:m, 6 + g % 2, col:col + k * step].rearrange("p (k n) -> p k n", k=k)[:, :, 0:n]
                    if parity:
                        last = eng.tensor_copy(dst, src)
                    else:
                        last = eng.activation(dst, src, ACT.Copy)
                last.then_inc(evac_dve if parity else evac_act, 1)

        def std_ffn(name, wts, h):
            ch = chunks(h)
            return dict(name=name, n=len(ch), rows=[w for _, w in ch],
                        w1=lambda k, i: wts[0][:, k, ch[i][0]:ch[i][0] + ch[i][1]],
                        w3=lambda k, i: wts[1][:, k, ch[i][0]:ch[i][0] + ch[i][1]],
                        w2=lambda i, o: wts[2][0:ch[i][1], i, o * P:(o + 1) * P])

        l0x = dict(name="l0x", n=4 * KC, rows=[P] * 4 * KC,
                   w1=lambda k, i: ctx_t[:, k, i * P:(i + 1) * P], w3=None,
                   w2=lambda i, o: ctx_t[:, i % KC, (i // KC) * SEQ + o * P:(i // KC) * SEQ + (o + 1) * P])
        l0 = std_ffn("l0", wt_l0, H0)
        l1 = std_ffn("l1", wt_l1, H1)
        l2 = std_ffn("l2", wt_l2, H2)
        unit = 0
        halves = 0
        for s in (l0x, l0, l1, l2):
            s["u0"], s["y0"] = unit, halves
            unit += TH * s["n"]
            halves += TH
        LN = dict(l0x=0, l0=1, wkv=2, l1=3, l2x=4, l2=5, l3x=6, l3=7)

        def tok(h):
            return slice(h * HALF, (h + 1) * HALF)

        block = ctx.enter_context(nc.Block())

        @block.sync
        def _(sp):
            sp.dma_start(x_nat, a["x"].rearrange("b (c p) d -> p (b c) d", p=P)).then_inc(load["x"], 16)
            sp.dma_start(ctx_nat, a["ctx_2048"].rearrange("b (c p) d -> p (b c) d", p=P)).then_inc(load["ctx"], 16)
            sp.dma_start(tid, a["itok_BxS_13_99985"].rearrange("b s -> (b s)").partition_broadcast(P)
                         ).then_inc(load["tid"], 16)

            def rows_in(dst, src, s):
                full = src.shape[0] // P
                sp.dma_start(dst[:, 0:full, :], src[0:full * P, :].rearrange("(c p) d -> p c d", p=P)).then_inc(s, 16)
                if src.shape[0] % P:
                    sp.dma_start(dst[0:src.shape[0] % P, full, :], src[full * P:, :]).then_inc(s, 16)

            for w, n in zip(w_l0, ("L0_ffn_w1", "L0_ffn_w3", "L0_ffn_w2")):
                rows_in(w, a[n], load["l0"])
            for w, n in zip(w_l1, ("L1_ffn_sh_gate_W", "L1_ffn_sh_up_W", "L1_ffn_sh_down_W")):
                rows_in(w, a[n], load["l1"])
            sp.dma_start(gw_nat[0:NE, :], a["L1_ffn_gate_weight"]).then_inc(load["mu"], 16)
            for k in range(KC):
                sp.dma_start(mu_nat[:, k], a["L1_ffn_mask_up_W"][:, k * P:(k + 1) * P, :].rearrange("f p k -> p f k")
                             ).then_inc(load["mu"], 16)
            sp.dma_start(inv_row[0:NE], a["L1_ffn_inv_mapping"].rearrange("f k -> (f k)").partition_broadcast(NE)
                         ).then_inc(load["inv"], 16)

            def load_slot(f, s):
                b = slots[s]
                done = load[f"moe{s}"]
                f1 = bass.ds(f, 1)

                def go(dst, src, columns=False):
                    sp.dma_start(dst, src, allow_slow_non_contiguous=columns).then_inc(done, 16)
                go(b["g"][0:IC], a["L1_ffn_gate_W"][f1].rearrange("f (c p) d -> p (f c) d", p=IC))
                go(b["u"][0:IC], a["L1_ffn_up_W"][f1].rearrange("f (c p) d -> p (f c) d", p=IC))
                go(b["d"], a["L1_ffn_down_W"][f1].rearrange("f (c p) d -> p (f c) d", p=P))
                go(b["qa"][0:64], a["L1_ffn_gate_qa"][f1].rearrange("f k r d -> (f k r) d"))
                go(b["qa"][64:128], a["L1_ffn_up_qa"][f1].rearrange("f k r d -> (f k r) d"))
                go(b["dqa"][0:64], a["L1_ffn_down_qa"][f1].rearrange("f k r d -> (f k r) d"))
                for i in range(NI):
                    for j, n in enumerate(("L1_ffn_gate_qb", "L1_ffn_up_qb")):
                        go(b["qb"][0:IC, i, 64 * j:64 * j + 64].rearrange("p (k r) -> p k r", k=NK),
                           a[n][f1, :, i * IC:(i + 1) * IC, :].rearrange("f k p r -> p (f k) r"))
                for i in range(KC):
                    go(b["dqb"][:, i, :].rearrange("p (k r) -> p k r", k=NK),
                       a["L1_ffn_down_qb"][f1, :, i * P:(i + 1) * P, :].rearrange("f k p r -> p (f k) r"))
                go(b["gs"][0:IC], a["L1_ffn_gate_scale"][f1].rearrange("f (c p) -> p (f c)", p=IC), True)
                go(b["us"][0:IC], a["L1_ffn_up_scale"][f1].rearrange("f (c p) -> p (f c)", p=IC), True)
                go(b["ds"], a["L1_ffn_down_scale"][f1].rearrange("f (c p) -> p (f c)", p=P), True)

            load_slot(0, 0)
            load_slot(1, 1)
            sp.wait_ge(x_ready, 2 * LN["wkv"] + 2)
            for n, d in (("L1_xattn_w", wk["w"]), ("L1_xattn_u", wk["u"])):
                sp.dma_start(d, a[n].rearrange("(k p) -> p k", p=P),
                             allow_slow_non_contiguous=True).then_inc(load["wku"], 16)
            with sp.Fori(1, NF // 2) as pair:
                for s in range(2):
                    sp.wait_ge(moe_turned, pair * 10 + (5 * s - 5))
                    load_slot(pair * 2 + s, s)
            sp.wait_ge(x_ready, 2 * LN["l2x"] + 2)
            for d, s in ((wq2, a["L2_xattn_Wq"]), (wkv2, a["L2_xattn_Wkv"]), (wp2, a["L2_xattn_Wp"])):
                sp.dma_start(d, s.rearrange("(k p) n -> p k n", p=P)).then_inc(load["l2x"], 16)
            bkv = a["L2_xattn_bkv"]
            sp.dma_start(bq_row, a["L2_xattn_bq"].unsqueeze(0)).then_inc(load["l2x"], 16)
            sp.dma_start(bk_row, bkv[0:D].unsqueeze(0)).then_inc(load["l2x"], 16)
            sp.dma_start(att_small["bvp"], bkv[D:2 * D].rearrange("(k p) -> p k", p=P),
                             allow_slow_non_contiguous=True).then_inc(load["l2x"], 16)
            sp.dma_start(att_small["bpp"], a["L2_xattn_bp"].rearrange("(k p) -> p k", p=P),
                             allow_slow_non_contiguous=True).then_inc(load["l2x"], 16)
            sp.wait_ge(x_ready, 2 * LN["l2"] + 2)
            for w, n in zip(w_l2, ("L2_ffn_w1", "L2_ffn_w2", "L2_ffn_w3")):
                rows_in(w, a[n], load["l2"])
            for w, n in zip(lx_nat, ("L3_xattn_Wq", "L3_xattn_Wg", "L3_xattn_Wo", "L3_xattn_Wkv")):
                rows_in(w, a[n], load["l3x"])
            sp.dma_start(bg, a["L3_xattn_bg"].rearrange("(k p) -> p k", p=P),
                             allow_slow_non_contiguous=True).then_inc(load["l3x"], 16)
            sp.wait_ge(x_ready, 2 * LN["l3"] + 2)
            for w, n in zip(w_l3, ("L3_ffn_gate_w", "L3_ffn_up_w", "L3_ffn_down_w")):
                rows_in(w, a[n], load["l3"])
            rows = out.rearrange("b (c p) d -> (b c) p d", p=P)
            for t in range(TT):
                sp.wait_ge(m_res, t + 1)
                sp.dma_start(rows[t], res[:, t % 2, :]).then_inc(stored[t % 2], 16)
            for s in stored:
                sp.wait_ge(s, 16 * TT // 2)

        @block.gpsimd
        def _(pool):
            made = 0

            def step(ins):
                nonlocal made
                made += 1
                ins.then_inc(pool_step, 1)
                pool.wait_ge(pool_step, made)

            step(pool.memset(ones[:, :], 1.0))
            step(pool.memset(mean_w[:, :], 1.0 / D))
            step(pool.memset(eps_col[:, :], LN_EPS))
            step(pool.affine_select(out=ident[:, :], in_=ones[:, :], compare_op=ALU.is_equal, fill=0.0, base=0,
                                    pattern=[[-1, P]], channel_multiplier=1))
            step(pool.tensor_copy(ident_b[:, :], ident[:, :]))
            hm = head_mask[:, :].rearrange("p (a b) -> p a b", a=P // HD)
            on = ones[:, :].rearrange("p (a b) -> p a b", a=P // HD)
            step(pool.affine_select(out=hm, in_=on, compare_op=ALU.is_ge, fill=0.0, base=0,
                                    pattern=[[-HD, P // HD], [0, HD]], channel_multiplier=1))
            step(pool.affine_select(out=hm, in_=hm, compare_op=ALU.is_ge, fill=0.0, base=HD - 1,
                                    pattern=[[HD, P // HD], [0, HD]], channel_multiplier=-1))
            g0 = group_mask[0:NE, :]
            step(pool.memset(group_mask, 1.0))
            step(pool.affine_select(out=g0, in_=g0, compare_op=ALU.is_ge, fill=0.0, base=0,
                                    pattern=[[-NK, NF]], channel_multiplier=1))
            step(pool.affine_select(out=g0, in_=g0, compare_op=ALU.is_ge, fill=0.0, base=NK - 1,
                                    pattern=[[NK, NF]], channel_multiplier=-1))
            g1 = group_mask[NE:GATES, :]
            step(pool.affine_select(out=g1, in_=g1, compare_op=ALU.is_equal, fill=0.0, base=0,
                                    pattern=[[-1, NF]], channel_multiplier=1))
            step(pool.memset(sc_rep[0:NE, :], 0.0))
            step(pool.memset(sc_rep[NE:GATES, :], 1.0))
            step(pool.memset(rep[0:NE, :], 0.0))
            step(pool.memset(rep[NE:GATES, :], 0.0))
            rp = rep[0:NE, :].rearrange("p (a k r) -> p a k r", a=2, k=NK)
            for m in range(NF):
                step(pool.affine_select(out=rp, in_=rp, compare_op=ALU.not_equal, fill=1.0, base=-NK * m,
                                        pattern=[[0, 2], [-1, NK], [0, NR]], channel_multiplier=1))
            step(pool.iota(e_col[0:NE, :], pattern=[[0, 1]], base=0, channel_multiplier=1,
                           allow_small_or_imprecise_dtypes=True))
            step(pool.memset(mu_t[NE:GATES, :], 0.0))
            pool.sem_inc(const_ready, 1)

            with pool.Fori(0, TT) as t:
                for h in range(HEADS):
                    pool.wait_ge(att_exp, t * HEADS + (h + 1))
                    if h >= 2:
                        pool.wait_ge(att_t, t * HEADS + (h - 1))
                    pool.sem_inc(round_starts, 1)
                    pool.tensor_scalar(att_p[:, h % 2, :], att_e[:, h % 2, :], ROUND, ROUND, ALU.add,
                                       ALU.subtract).then_inc(att_round, 1)

        @block.tensor
        def _(pe):
            def mm(o, l, r, start, stop):
                return pe.matmul(o, l, r, start=start, stop=stop)

            def layer_norm(name):
                L = LN[name]
                pe.wait_ge(x_ready, 2 * L + 2)
                for h in range(TH):
                    n = 2 * L + h
                    if h:
                        pe.wait_ge(ln_xc, n)
                    for k in range(KC):
                        last = mm(ps[:, 4, :], mean_w[:, :], x_t[:, k, tok(h)], k == 0, k == KC - 1)
                    last.then_inc(ln_mean, 1)
                for h in range(TH):
                    n = 2 * L + h
                    pe.wait_ge(ln_sq, n + 1)
                    if h:
                        pe.wait_ge(ln_sd, n)
                    for k in range(KC):
                        last = mm(ps[:, 5, :], mean_w[:, :], sq[:, k, :], k == 0, k == KC - 1)
                    last.then_inc(ln_var, 1)

            def ffn(s):
                L = LN[s["name"]]
                for h in range(TH):
                    pe.wait_ge(xn_ready, 2 * L + h + 1)

                    def down(i):
                        u = s["u0"] + h * s["n"] + i
                        pe.wait_ge(gated, u + 1)
                        if i == 0:
                            pe.wait_ge(xn_ready, 2 * L + 2)
                            if h:
                                pe.wait_ge(x_ready, 2 * (L + 1) + 1)
                        r = s["rows"][i]
                        for o in range(KC):
                            last = mm(ps[:, 4 + o, :], s["w2"](i, o), hid_buf[0:r, u % 2, :], i == 0, i == s["n"] - 1)
                        last.then_inc(hid_used, 1)

                    for i in range(s["n"]):
                        u = s["u0"] + h * s["n"] + i
                        if u >= 2:
                            pe.wait_ge(gated, u - 1)
                        r = s["rows"][i]
                        b = 2 * (u % 2)
                        for j, w in enumerate([s["w1"], s["w3"]] if s["w3"] else [s["w1"]]):
                            for k in range(KC):
                                last = mm(ps[0:r, b + j, :], w(k, i), xn_t[:, k, tok(h)], k == 0, k == KC - 1)
                        last.then_inc(hid_ready, 1)
                        if i:
                            down(i - 1)
                    down(s["n"] - 1)

            def ternary(n):
                pe.wait_ge(tern_part, n)
                st = tern_s if n == 1 else tern_s2
                mm(ps[:, 4, 0:6], ones[:, :], st[:, 0:6], True, True).then_inc(tern_sum, 1)

            pe.wait_ge(const_ready, 1)
            pe_turn(pe, "x")
            pe_turn(pe, "ctx")
            evacuated(pe, marks["ctx"][1])
            layer_norm("l0x")
            ffn(l0x)
            pe.wait_ge(x_ready, 4)
            ternary(1)
            pe_turn(pe, "l0")
            evacuated(pe, marks["l0"][1])
            layer_norm("l0")
            ffn(l0)
            layer_norm("wkv")
            pe_turn(pe, "l1")
            pe_turn(pe, "small")
            evacuated(pe, marks["small"][1])
            layer_norm("l1")
            pe.wait_ge(xn_ready, 2 * LN["l1"] + 2)
            for t in range(TT):
                for k in range(KC):
                    last = mm(ps[:, 0, t * NE:(t + 1) * NE], xn_t[:, k, t * P:(t + 1) * P], gw_t[:, k, :],
                              k == 0, k == KC - 1)
            last.then_inc(rt_logits, 1)
            pe.wait_ge(rt_wd, 1)
            for t in range(TT):
                last = pe.transpose(ps[0:NE, 1 + t // 4, (t % 4) * P:(t % 4 + 1) * P], rt["wd"][:, t, :], ident[:, :])
            last.then_inc(rt_wdt, 1)
            pe.wait_ge(rt_wdt_sb, 1)
            for t in range(TT):
                last = mm(ps[:, 3, t * NE:(t + 1) * NE], rt["wdT"][0:NE, t * P:(t + 1) * P], esel[0:NE, :], True, True)
            last.then_inc(rt_flat, 1)
            pe.wait_ge(rt_gt, 1)
            for t in range(TT):
                last = pe.transpose(ps[0:GATES, 1 + t // 4, (t % 4) * P:(t % 4 + 1) * P], rt["gt"][:, t, :], ident[:, :])
            last.then_inc(rt_gatest, 1)
            pe.wait_ge(rt_gates_sb, 1)

            def turn_slot(pair, s):
                b, f = slots[s], pair * 2 + s
                pe.wait_ge(load[f"moe{s}"], pair * SLOT_LOADED + SLOT_LOADED)
                pe.wait_ge(moe_fixed, f + 1)

                def bank(g):
                    return 6 + (g + s) % 2

                def turn(m, g, col, src):
                    n = src.shape[0]
                    w = src.shape[0]
                    return pe.transpose(ps[0:m, bank(g), col:col + w], src, ident[0:n, 0:n])
                pe.wait_ge(moe_ev_dve, f * 2 + 1)
                for k in range(KC):
                    for i in range(NI):
                        last = turn(P, 0, k * 256 + i * IC, b["g"][0:IC, i, k * P:(k + 1) * P])
                last.then_inc(moe_turned, 1)
                pe.wait_ge(moe_ev_act, f * 3 + 1)
                for k in range(KC):
                    for i in range(NI):
                        last = turn(P, 1, k * 256 + i * IC, b["u"][0:IC, i, k * P:(k + 1) * P])
                last.then_inc(moe_turned, 1)
                pe.wait_ge(moe_ev_act, f * 3 + 2)
                for i in range(NI):
                    for r in range(KC):
                        last = turn(IC, 2, i * 256 + r * P, b["d"][:, r, i * IC:(i + 1) * IC])
                last.then_inc(moe_turned, 1)
                pe.wait_ge(moe_ev_dve, f * 2 + 2)
                for k in range(KC):
                    turn(P, 3, k * P, b["qa"][:, k * P:(k + 1) * P])
                for r in range(KC):
                    last = turn(64, 3, 256 + r * P, b["dqb"][:, r, :])
                last.then_inc(moe_turned, 1)
                pe.wait_ge(moe_ev_act, f * 3 + 3)
                for i in range(NI):
                    turn(P, 4, 256 + i * IC, b["qb"][0:IC, i, :])
                for i in range(NI):
                    last = turn(IC, 4, i * 64, b["dqa"][0:64, i * IC:(i + 1) * IC])
                last.then_inc(moe_turned, 1)
                pe.wait_ge(moe_ev_act, f * 3 + 4)
                pe.wait_ge(moe_ev_dve, f * 2 + 3)

            def expert(f, s):
                b = slots[s]
                pe.wait_ge(moe_masked, f + 1)
                for h in range(TH):
                    n = f * 2 + h
                    g = gates_f[s][0:GATES, tok(h)]
                    for o in range(KC):
                        mm(ps[:, o, :], mu_t[0:GATES, o * P:(o + 1) * P], g, True, True)
                    mm(ps[:, 2, :], rep[0:GATES, :], g, True, True)
                    mm(ps[:, 3, :], sc_rep[0:GATES, :], g, True, True).then_inc(moe_mu, 1)
                    pe.wait_ge(moe_xe, n + 1)
                    xe = moe["xe"][:, h]
                    for k in range(KC):
                        last = mm(ps[:, 0, :], b["qaT"][:, k, :], xe[:, k, :], k == 0, k == KC - 1)
                    last.then_inc(moe_a, 1)
                    for i in range(NI):
                        ba, bb = ((1, 2), (3, 0))[i]
                        pe.wait_ge(moe_wr, n * 2 + (1 + i))
                        if i:
                            pe.wait_ge(moe_aw, n + 1)
                        cs = slice(i * IC, (i + 1) * IC)
                        for k in range(KC):
                            mm(ps[0:IC, ba, :], b["gT"][:, k, cs], xe[:, k, :], k == 0, False)
                        for k in range(KC):
                            mm(ps[0:IC, bb, :], b["uT"][:, k, cs], xe[:, k, :], k == 0, False)
                        if i == 0:
                            pe.wait_ge(moe_aw, n + 1)
                        mm(ps[0:IC, ba, :], b["qbT"][0:64, cs], moe["aw"][0:64, :], False, True)
                        mm(ps[0:IC, bb, :], b["qbT"][64:128, cs], moe["aw"][64:128, :], False, True
                           ).then_inc(moe_h, 1)
                    for i in range(NI):
                        pe.wait_ge(moe_hg, n * 2 + (1 + i))
                        last = mm(ps[0:64, 1, :], b["dqaT"][0:IC, i, :], moe["h"][0:IC, i, :], i == 0, i == NI - 1)
                    last.then_inc(moe_ad, 1)
                    pe.wait_ge(moe_x, n + 1)
                    for o in range(KC):
                        for i in range(NI):
                            mm(ps[:, 4 + o, :], b["dT"][0:IC, i, o * P:(o + 1) * P], moe["h"][0:IC, i, :], i == 0, False)
                    pe.wait_ge(moe_awd, n + 1)
                    for o in range(KC):
                        last = mm(ps[:, 4 + o, :], b["dqbT"][0:64, o * P:(o + 1) * P], moe["awd"][0:64, :], False, True)
                    last.then_inc(moe_y, 1)

            with pe.Fori(0, NF // 2) as pair:
                for s in range(2):
                    turn_slot(pair, s)
                    expert(pair * 2 + s, s)
            pe.wait_ge(moe_x, 2 * NF + 1)
            ffn(l1)

            layer_norm("l2x")
            pe.wait_ge(xn_ready, 2 * LN["l2x"] + 2)
            pe.wait_ge(load["l2x"], 16 * 7)
            for t in range(TT):
                for j, (src, w, row) in enumerate(((xn_t, wq2, bq_row), (ctx_t, wkv2, bk_row))):
                    n = 2 * t + j
                    if n >= 4:
                        pe.wait_ge(pj_used, n - 3)
                    o = ps[:, n % 4, 0:D]
                    for k in range(KC):
                        mm(o, src[:, k, t * P:(t + 1) * P], w[:, k, 0:D], k == 0, False)
                    mm(o, ones[0:1, :], row, False, True).then_inc(pj_ready, 1)
            for h in range(TH):
                for o in range(KC):
                    n = 2 * h + o
                    bnk = (4, 5, 6, 7)[n]
                    for k in range(KC):
                        last = mm(ps[:, bnk, :], wkv2[:, k, D + o * P:D + (o + 1) * P], ctx_t[:, k, tok(h)],
                                  k == 0, k == KC - 1)
                    last.then_inc(v_ready, 1)
            for n in range(2 * HEADS):
                src = (q3, k3)[n // HEADS]
                if n % HEADS == 0:
                    pe.wait_ge(qk_split, 1 + n // HEADS)
                if n >= 2:
                    pe.wait_ge(head_copied, n - 1)
                o = ps[:, n % 2, :].bitcast(BF16)
                for t in range(TT):
                    last = pe.transpose(o[0:3 * HD, t * P:(t + 1) * P],
                                        src[:, t, n % HEADS].rearrange("p a b -> p (a b)"), ident_b[:, :])
                last.then_inc(head_turned, 1)
            pe.wait_ge(vn_ready, 1)
            for k in range(KC):
                o = ps[:, 2 + k, :].bitcast(BF16)
                for t in range(TT):
                    last = pe.transpose(o[:, t * P:(t + 1) * P], vn_t[:, k, t * P:(t + 1) * P], ident_b[:, :])
                last.then_inc(vn_turned, 1)
            pe.wait_ge(head_copied, 2 * HEADS)
            pe.wait_ge(v_copied, KC)
            with pe.Fori(0, TT) as t:
                for i in range(HEADS + 2):
                    if i < HEADS:
                        if i >= 2:
                            pe.wait_ge(att_exp, t * HEADS + (i - 1))
                        for kh in range(2):
                            last = mm(ps[:, 2 * (i % 2) + kh, :], q_s[0:3 * HD, i, bass.ds(t * P, P)],
                                      k_s[0:3 * HD, i, kh * 512:(kh + 1) * 512], True, True)
                        last.then_inc(att_s, 1)
                    if 1 <= i <= HEADS:
                        j = i - 1
                        pe.wait_ge(att_round, t * HEADS + (j + 1))
                        if j >= 2:
                            pe.wait_ge(att_evd if j % 2 else att_eva, t * (HEADS // 2) + j // 2)
                        o = ps[:, 4 + j % 2, :].bitcast(BF16)
                        for k in range(TT):
                            last = pe.transpose(o[:, k * P:(k + 1) * P], att_p[:, j % 2, k * P:(k + 1) * P],
                                                ident_b[:, :])
                        last.then_inc(att_t, 1)
                    if i >= 2:
                        j = i - 2
                        pe.wait_ge(att_evd if j % 2 else att_eva, t * (HEADS // 2) + (j // 2 + 1))
                        if j == 0:
                            pe.wait_ge(att_o_used, t + 1)
                        for k in range(TT):
                            last = mm(ps[:, 6, j * HD:(j + 1) * HD], att_pt[:, j % 2, k, :],
                                      v_tok[:, k, j * HD:(j + 1) * HD], k == 0, k == TT - 1)
                        if j == HEADS - 1:
                            last.then_inc(att_o, 1)
            pe.wait_ge(att_o_used, TT + 1)
            for h in range(TH):
                for k in range(KC):
                    for j in range(4):
                        last = pe.transpose(ps[:, 2 * h + k, j * P:(j + 1) * P],
                                            o_tok[:, 4 * h + j, k * P:(k + 1) * P], ident[:, :])
                    last.then_inc(ot_turned, 1)
            for h in range(TH):
                pe.wait_ge(ot_copied, 2 * h + 2)
                for o in range(KC):
                    for k in range(KC):
                        last = mm(ps[:, 4 + 2 * h + o, :], wp2[:, k, o * P:(o + 1) * P], o_t[:, k, tok(h)],
                                  k == 0, k == KC - 1)
                last.then_inc(att_done, 1)
            pe.wait_ge(x_ready, 2 * LN["l2"] + 2)
            ternary(2)
            pe_turn(pe, "l2")
            evacuated(pe, marks["l2"][1])
            layer_norm("l2")
            ffn(l2)
            pe_turn(pe, "lx")
            evacuated(pe, marks["lx"][1])
            layer_norm("l3x")
            for t in range(TT):
                if t >= 2:
                    pe.wait_ge(lx_kf, t - 1)
                    pe.wait_ge(lx_v, t - 1)
                for j in range(2):
                    for k in range(KC):
                        last = mm(ps[:, 2 * j + t % 2, 0:D], ctx_t[:, k, t * P:(t + 1) * P],
                                  lx_t[3][:, k, j * D:(j + 1) * D], k == 0, k == KC - 1)
                    last.then_inc(lx_kv, 1)
            pe.wait_ge(lx_kf, TT)
            pe.wait_ge(lx_v, TT)
            for b in range(BATCH):
                for m in range(KC):
                    for j in range(2):
                        t = 2 * b + j
                        last = mm(ps[:, b, m * (P + 1):(m + 1) * (P + 1)], kf[:, t, m * P:(m + 1) * P], v1[:, t, m, :],
                                  j == 0, j == 1)
                last.then_inc(lx_sum, 1)
            pe.wait_ge(xn_ready, 2 * LN["l3x"] + 2)
            pe.wait_ge(lx_bd, 1)
            for h in range(TH):
                for j in range(2):
                    for o in range(KC):
                        for k in range(KC):
                            last = mm(ps[:, 2 * j + o, :], lx_t[j][:, k, o * P:(o + 1) * P], xn_t[:, k, tok(h)],
                                      k == 0, k == KC - 1)
                    last.then_inc(lx_qg, 1)
                pe.wait_ge(lx_qf, h + 1)
                for j, w in enumerate((bd, dd)):
                    for m in range(KC):
                        for b in range(2):
                            last = mm(ps[:, 4 + 2 * j + m, b * SEQ:(b + 1) * SEQ], w[:, 2 * h + b, m, :],
                                      lx_q[:, m, b * SEQ:(b + 1) * SEQ], True, True)
                last.then_inc(lx_att, 1)
                pe.wait_ge(lx_or, h + 1)
                for o in range(KC):
                    for k in range(KC):
                        last = mm(ps[:, o, :], lx_t[2][:, k, o * P:(o + 1) * P], lx_o[:, k, :], k == 0, k == KC - 1)
                last.then_inc(y_ready, 1)
                pe.wait_ge(x_ready, 2 * LN["l3x"] + 2 + h + 1)
            layer_norm("l3")
            pe.wait_ge(xn_ready, 2 * LN["l3"] + 2)
            for h in range(TH):
                for k in range(KC):
                    n = 2 * h + k
                    for j in range(4):
                        t = 4 * h + j
                        last = pe.transpose(ps[:, n, j * P:(j + 1) * P], xn_t[:, k, t * P:(t + 1) * P], ident[:, :])
                    last.then_inc(xt_turned, 1)
            for h in range(TH):
                for k in range(KC):
                    n = 2 * h + k
                    pe.wait_ge(xt_copied, n + 1)
                    for j in range(4):
                        t = 4 * h + j
                        last = pe.transpose(ps[:, n, j * P:(j + 1) * P], x_t[:, k, t * P:(t + 1) * P], ident[:, :])
                    last.then_inc(xt_turned, 1)
            pe.wait_ge(xq_ready, 1)
            pe.wait_ge(xt_copied, 8)
            for h in range(TH):
                for k in range(KC):
                    n = 2 * h + k
                    for j in range(4):
                        t = 4 * h + j
                        last = pe.transpose(ps[:, n, j * P:(j + 1) * P], xn_tok[:, t, k * P:(k + 1) * P], ident[:, :])
                    last.then_inc(xq_turned, 1)
            pe_turn(pe, "l3")
            evacuated(pe, marks["l3"][1])
            pe.wait_ge(xq_copied, 4)
            for t in range(TT):
                if t:
                    pe.wait_ge(m_h, t)
                for j in range(2):
                    for c2_ in range(2):
                        for k in range(KC):
                            last = mm(ps[:, 2 * j + c2_, :], xq_t[:, k, t * P:(t + 1) * P],
                                      wt_l3[j][:, k, c2_ * 512:(c2_ + 1) * 512], k == 0, k == KC - 1)
                    last.then_inc(m_gu, 1)
                pe.wait_ge(m_h, TT * 0 + t + 1)
                pe.wait_ge(m_res, t) if t else None
                for k in range(8):
                    last = pe.transpose(ps[:, 4 + k // 4, (k % 4) * P:(k % 4 + 1) * P], h_tok[:, k * P:(k + 1) * P],
                                        ident[:, :])
                last.then_inc(m_ht, 1)
                pe.wait_ge(m_htc, t + 1)
                for k in range(8):
                    last = mm(ps[:, 6, 0:D], hq_t[:, k, :], wt_l3[2][:, k, :], k == 0, k == 7)
                last.then_inc(m_o, 1)

        @block.scalar
        def _(act):
            def layer_norm(name):
                L = LN[name]
                for h in range(TH):
                    n = 2 * L + h
                    act.wait_ge(ln_xc, n + 1)
                    if n:
                        act.wait_ge(ln_var, n)
                    act.activation(sq[:, :, :], xc[:, h], ACT.Square).then_inc(ln_sq, 1)
                    act.wait_ge(ln_var, n + 1)
                    act.activation(sd[:, h, :], ps[:, 5, :], ACT.Sqrt, bias=eps_col[:, :]).then_inc(ln_sd, 1)

            def ffn(s, func, scale=None):
                for h in range(TH):
                    for i in range(s["n"]):
                        u = s["u0"] + h * s["n"] + i
                        r = s["rows"][i]
                        act.wait_ge(hid_ready, u + 1)
                        if u >= 2:
                            act.wait_ge(gated, u - 1)
                        act.activation(act_buf[0:r, u % 2, :], ps[0:r, 2 * (u % 2), :], func,
                                       scale=1.0 if scale is None else scale[0:r, :]).then_inc(act_ready, 1)

            act.wait_ge(const_ready, 1)
            copy_out(act, "x", 0)
            copy_out(act, "ctx", 0)
            layer_norm("l0x")
            ffn(l0x, ACT.Silu)
            copy_out(act, "l0", 0)
            layer_norm("l0")
            ffn(l0, ACT.Silu, tern_s[:, 8:9])
            layer_norm("wkv")
            for k in range(KC):
                for j, names in enumerate((("e1", "e2"), ("e3", "e4"))):
                    for i, nm in enumerate(names):
                        n = 4 * k + 2 * j + i
                        act.wait_ge(exp_in, n + 1)
                        act.activation(wk[nm], wk[nm], ACT.Exp).then_inc(exp_out, 1)
            copy_out(act, "l1", 0)
            copy_out(act, "small", 0)
            layer_norm("l1")
            act.wait_ge(exp_in, 9)
            act.activation(rt["e"], rt["e"], ACT.Exp).then_inc(exp_out, 1)
            act.wait_ge(rt_wdt, 1)
            act.activation(rt["wdT"][0:NE, :].rearrange("p (a b) -> p a b", a=2), ps[0:NE, 1:3, :], ACT.Copy
                           ).then_inc(rt_wdt_sb, 1)
            act.wait_ge(exp_in, 10)
            act.activation(rt["fm"], rt["fm"], ACT.Exp).then_inc(exp_out, 1)
            act.wait_ge(rt_gatest, 1)
            act.activation(gates_t[0:GATES, :].rearrange("p (a b) -> p a b", a=2), ps[0:GATES, 1:3, :], ACT.Copy
                           ).then_inc(rt_gates_sb, 1)

            def turn_slot(pair, s):
                b, f = slots[s], pair * 2 + s
                act.wait_ge(moe_turned, f * 5 + 1)
                act.activation(b["gT"], ps[:, 6 + s % 2, :].rearrange("p (k n) -> p k n", k=KC)[:, :, 0:INNER],
                               ACT.Copy).then_inc(moe_ev_act, 1)
                act.wait_ge(moe_turned, f * 5 + 3)
                act.activation(b["dT"][0:IC], ps[0:IC, 6 + s % 2, :].rearrange("p (k n) -> p k n", k=NI),
                               ACT.Copy).then_inc(moe_ev_act, 1)
                act.wait_ge(moe_turned, f * 5 + 5)
                act.activation(b["dqaT"][0:IC], ps[0:IC, 6 + s % 2, 0:NI * 64].rearrange("p (k n) -> p k n", k=NI),
                               ACT.Copy)
                act.activation(b["qbT"], ps[:, 6 + s % 2, 256:256 + INNER], ACT.Copy).then_inc(moe_ev_act, 1)

            def expert(f, s):
                for h in range(TH):
                    n = f * 2 + h
                    act.wait_ge(moe_mu, n + 1)
                    act.activation(moe["wr"], ps[:, 2, :], ACT.Copy).then_inc(moe_wr, 1)
                    act.activation(moe["sr"], ps[:, 3, :], ACT.Copy).then_inc(moe_wr, 1)
                    for i in range(NI):
                        act.wait_ge(moe_h, n * 2 + (1 + i))
                        act.activation(moe["s"][0:IC, i, :], ps[0:IC, (1, 3)[i], :], ACT.Silu).then_inc(moe_s, 1)

            act.sem_inc(moe_ev_act, 1)
            with act.Fori(0, NF // 2) as pair:
                for s in range(2):
                    turn_slot(pair, s)
                    expert(pair * 2 + s, s)
            ffn(l1, ACT.Silu)

            layer_norm("l2x")
            for n in range(2 * HEADS):
                if n % 2 == 0:
                    act.wait_ge(head_turned, n + 1)
                    if n:
                        act.wait_ge(head_copied, n)
                    dst = (q_s, k_s)[n // HEADS]
                    act.activation(dst[0:3 * HD, n % HEADS, :], ps[0:3 * HD, n % 2, :].bitcast(BF16), ACT.Copy
                                   ).then_inc(head_copied, 1)
            with act.Fori(0, TT) as t:
                for i in range(HEADS + 1):
                    if i < HEADS:
                        act.wait_ge(att_bias, t * HEADS + (i + 1))
                        if i >= 2:
                            act.wait_ge(att_round, t * HEADS + (i - 1))
                        act.activation(att_e[:, i % 2, :].rearrange("p (a b) -> p a b", a=2),
                                       ps[:, 2 * (i % 2):2 * (i % 2) + 2, :], ACT.Exp,
                                       bias=att_small["bias"][:, i % 2:i % 2 + 1],
                                       scale=att_small["sq"][:, bass.ds(t, 1), i],
                                       accum_out=att_small["z"][:, bass.ds(t, 1), i]).then_inc(att_exp, 1)
                    j = i - 1
                    if j >= 0 and j % 2 == 0:
                        act.wait_ge(att_t, t * HEADS + (j + 1))
                        act.activation(att_pt[:, 0].rearrange("p a b -> p (a b)"), ps[:, 4, :].bitcast(BF16),
                                       ACT.Copy).then_inc(att_eva, 1)
            copy_out(act, "l2", 0)
            layer_norm("l2")
            ffn(l2, ACT.Sigmoid)
            copy_out(act, "lx", 0)
            layer_norm("l3x")
            for t in range(TT):
                act.wait_ge(lx_kv, 2 * t + 2)
                act.activation(v1[:, t, :, 0:P], ps[:, 2 + t % 2, 0:D].rearrange("p (m n) -> p m n", m=KC), ACT.Copy
                               ).then_inc(lx_v, 1)
                act.wait_ge(lx_min_r, t + 1)
                if t >= 2:
                    act.wait_ge(lx_kf, t - 1)
                act.activation(lx_exp[:, t % 2, :], lx_min[:, t % 2, :], ACT.Exp).then_inc(lx_exp_r, 1)
            for h in range(TH):
                act.wait_ge(lx_qmin_r, h + 1)
                act.activation(lx_qmin, lx_qmin, ACT.Exp).then_inc(lx_act, 1)
                act.wait_ge(lx_qg, 2 * h + 2)
                if h:
                    act.wait_ge(lx_or, h)
                for o in range(KC):
                    last = act.activation(lx_gate[:, o, :], ps[:, 2 + o, :], ACT.Sigmoid, bias=bg[:, o:o + 1])
                    last.then_inc(lx_act, 1)
            layer_norm("l3")
            copy_out(act, "l3", 0)
            for t in range(TT):
                act.wait_ge(m_gu, 2 * t + 1)
                if t:
                    act.wait_ge(m_ht, t)
                act.activation(h_act.rearrange("p (a b) -> p a b", a=2), ps[:, 0:2, :], ACT.Silu).then_inc(m_act, 1)
                act.wait_ge(m_ht, t + 1)
                if t:
                    act.wait_ge(m_o, t)
                act.activation(hq_t.rearrange("p a b -> p (a b)").rearrange("p (a b) -> p a b", a=2), ps[:, 4:6, :],
                               ACT.Copy).then_inc(m_htc, 1)

        @block.vector
        def _(dve):
            made = 0

            def step(ins):
                nonlocal made
                made += 1
                ins.then_inc(dve_step, 1)
                dve.wait_ge(dve_step, made)

            TS, TTN, STT = dve.tensor_scalar, dve.tensor_tensor, dve.scalar_tensor_tensor

            def layer_norm(name):
                L = LN[name]
                for h in range(TH):
                    n = 2 * L + h
                    dve.wait_ge(ln_mean, n + 1)
                    TTN(xc[:, h], x_t[:, :, tok(h)], ps[:, 4:5, :].to_broadcast([P, KC, HALF]), ALU.subtract
                        ).then_inc(ln_xc, 1)
                for h in range(TH):
                    n = 2 * L + h
                    dve.wait_ge(ln_sd, n + 1)
                    step(dve.reciprocal(sd[:, h, :], sd[:, h, :]))
                    TTN(xn_t[:, :, tok(h)], xc[:, h], sd[:, h:h + 1, :].to_broadcast([P, KC, HALF]), ALU.mult
                        ).then_inc(xn_ready, 1)

            def add_y(h, scalar=None):
                y = ps[:, 4:6, :]
                if scalar is None:
                    return TTN(x_t[:, :, tok(h)], y, x_t[:, :, tok(h)], ALU.add)
                return STT(x_t[:, :, tok(h)], y, scalar, x_t[:, :, tok(h)], ALU.mult, ALU.add)

            def ffn(s, gate, y_scale=None):
                for h in range(TH):
                    for i in range(s["n"]):
                        u = s["u0"] + h * s["n"] + i
                        r = s["rows"][i]
                        dve.wait_ge(act_ready, u + 1)
                        if u >= 2:
                            dve.wait_ge(hid_used, u - 1)
                        gate(h, i, r, act_buf[0:r, u % 2, :], ps[0:r, 2 * (u % 2), :], ps[0:r, 2 * (u % 2) + 1, :],
                             hid_buf[0:r, u % 2, :]).then_inc(gated, 1)
                    dve.wait_ge(hid_used, s["u0"] + (h + 1) * s["n"])
                    add_y(h, y_scale).then_inc(x_ready, 1)

            def ternary(ws, h, tmp, st, wait, use_scale):
                dve.wait_ge(*wait)
                full = h // P
                parts = [(ws[i][:, 0:full, :], P, 2 * i) for i in range(2)]
                parts += [(ws[i][0:h % P, full, :], h % P, 2 * i + 1) for i in range(2)]
                parts += [(ws[2], P, 4)]
                step(dve.memset(st, 0.0))
                for w, r, col in parts:
                    last = dve.tensor_reduce(st[0:r, col:col + 1], w, AX.XY if len(w.shape) == 3 else AX.X, ALU.add,
                                             apply_absolute_value=True)
                    step(last)
                dve.sem_inc(tern_part, 1)
                dve.wait_ge(tern_sum, 1 if use_scale else 2)
                step(dve.tensor_reduce(st[:, 8:11], ps[:, 4, 0:6].rearrange("p (a b) -> p a b", b=2), AX.X, ALU.add))
                step(TS(st[:, 8:11], st[:, 8:11], 1.0 / (h * D), None, ALU.mult))
                if not use_scale:
                    step(TS(st[:, 8:11], st[:, 8:11], 1e-8, None, ALU.add))
                step(TS(st[:, 12:15], st[:, 8:11], 0.5, None, ALU.mult))
                step(TS(st[:, 16:19], st[:, 8:11], -0.5, None, ALU.mult))
                step(TTN(st[:, 20:21], st[:, 9:10], st[:, 10:11], ALU.mult))
                for w, r, col in parts:
                    i = col // 2
                    t = tmp[0:r, 0:w.free_size() if callable(w.free_size) else w.free_size]
                    if len(w.shape) == 3:
                        t = t.rearrange("p (a b) -> p a b", a=w.shape[1])
                    step(TS(t, w, st[0:r, 16 + i:17 + i], None, ALU.is_lt))
                    step(STT(w, w, st[0:r, 12 + i:13 + i], t, ALU.is_gt, ALU.subtract))
                dve.sem_inc(weights_fixed, 1)

            copy_out(dve, "x", 1)
            copy_out(dve, "ctx", 1)
            dve.wait_ge(evac_act, 2)
            dve.wait_ge(evac_dve, 2)
            dve.sem_inc(x_ready, 2)
            dve.wait_ge(load["tid"], 16)
            for e in range(1, 4):
                step(TS(ge_mask[:, e - 1, :], tid, float(e * TOKENS_PER_EXPERT), None, ALU.is_ge))
            step(TS(tok_mask[:, 0, :], ge_mask[:, 0, :], -1.0, 1.0, ALU.mult, ALU.add))
            step(TTN(tok_mask[:, 1, :], ge_mask[:, 0, :], ge_mask[:, 1, :], ALU.subtract))
            step(TTN(tok_mask[:, 2, :], ge_mask[:, 1, :], ge_mask[:, 2, :], ALU.subtract))
            step(dve.tensor_copy(tok_mask[:, 3, :], ge_mask[:, 2, :]))
            layer_norm("l0x")

            def gate_l0x(h, i, r, s, ga, up, hid):
                step(TTN(hid, ga, s, ALU.mult))
                return TTN(hid, hid, tok_mask[:, i // KC, tok(h)], ALU.mult)
            ffn(l0x, gate_l0x)
            ternary(w_l0, H0, tern_tmp, tern_s, (load["l0"], 16 * 5), True)
            copy_out(dve, "l0", 1)
            layer_norm("l0")

            def gate_l0(h, i, r, s, ga, up, hid):
                return STT(hid, up, tern_s[0:r, 20:21], s, ALU.mult, ALU.mult)
            ffn(l0, gate_l0)

            layer_norm("wkv")
            dve.wait_ge(load["wku"], 32)
            W = wk
            for k in range(KC):
                kk = xn_t[:, k, :].rearrange("p (b s) -> p b s", b=BATCH)
                vv = ctx_t[:, k, :].rearrange("p (b s) -> p b s", b=BATCH)
                xx = x_t[:, k, :].rearrange("p (b s) -> p b s", b=BATCH)
                w, u = W["w"][:, k:k + 1], W["u"][:, k:k + 1]
                o0, o1 = W["o"][:, :, 0:SEQ], W["o"][:, :, 1:SEQ + 1]
                p0, q0 = W["p"][:, :, 0:SEQ], W["q"][:, :, 0:SEQ]
                step(dve.memset(W["wb"], 0.0))
                step(TS(W["wb"], W["wb"], w, None, ALU.add))
                step(dve.memset(W["o"][:, :, 0:1], -1e38))
                step(dve.memset(W["p"][:, :, 0:1], 0.0))
                step(dve.memset(W["q"][:, :, 0:1], 0.0))
                for b in range(BATCH):
                    step(dve.tensor_tensor_scan(o1[:, b, :], W["wb"], kk[:, b, :], -1e38, ALU.add, ALU.max))
                TTN(W["e2"], kk, o1, ALU.subtract).then_inc(dve_step, 1)
                made += 1
                dve.wait_ge(dve_step, made)
                step(STT(W["e1"], o0, w, o1, ALU.add, ALU.subtract))
                dve.sem_inc(exp_in, 2)
                step(STT(W["no"], kk, u, o0, ALU.add, ALU.max))
                step(TTN(W["e3"], o0, W["no"], ALU.subtract))
                step(STT(W["e4"], kk, u, W["no"], ALU.add, ALU.subtract))
                dve.sem_inc(exp_in, 2)
                dve.wait_ge(exp_out, 4 * k + 2)
                step(TTN(W["ev"], W["e2"], vv, ALU.mult))
                for b in range(BATCH):
                    step(dve.tensor_tensor_scan(W["p"][:, b, 1:], W["e1"][:, b, :], W["ev"][:, b, :], 0.0,
                                                ALU.mult, ALU.add))
                    step(dve.tensor_tensor_scan(W["q"][:, b, 1:], W["e1"][:, b, :], W["e2"][:, b, :], 0.0,
                                                ALU.mult, ALU.add))
                dve.wait_ge(exp_out, 4 * k + 4)
                step(TTN(W["num"], W["e3"], p0, ALU.mult))
                step(TTN(W["den"], W["e3"], q0, ALU.mult))
                step(TTN(W["ev"], W["e4"], vv, ALU.mult))
                step(TTN(W["num"], W["num"], W["ev"], ALU.add))
                step(TTN(W["den"], W["den"], W["e4"], ALU.add))
                step(dve.reciprocal(W["den"], W["den"]))
                step(TTN(W["num"], W["num"], W["den"], ALU.mult))
                TTN(xx, xx, W["num"], ALU.add).then_inc(x_ready, 1)
            copy_out(dve, "l1", 1)
            copy_out(dve, "small", 1)
            layer_norm("l1")

            dve.wait_ge(load["inv"], 16)
            iv = inv_f[0:NE]
            step(dve.tensor_copy(iv[:, 0, :], inv_row[0:NE]))
            step(TS(iv[:, 1, :], iv[:, 0, :], 0.0, float(NE), ALU.is_lt, ALU.mult))
            step(TTN(iv[:, 0, :], iv[:, 0, :], iv[:, 1, :], ALU.add))
            step(TS(iv[:, 2, :], iv[:, 0, :], 0.0, float(NE - 1), ALU.max, ALU.min))
            dve.wait_ge(const_ready, 1)
            step(TS(esel[0:NE, :], iv[:, 2, :], e_col[0:NE, :], None, ALU.is_equal))
            dve.wait_ge(rt_logits, 1)
            lg = ps[:, 0, :].rearrange("p (t e) -> p t e", e=NE)
            R = rt

            def b3(v, n):
                return v.unsqueeze(2).to_broadcast([P, v.shape[1], n])
            step(dve.tensor_reduce(R["mx"], lg, AX.X, ALU.max))
            step(TTN(R["e"], lg, b3(R["mx"], NE), ALU.subtract))
            dve.sem_inc(exp_in, 1)
            dve.wait_ge(exp_out, 9)
            step(dve.tensor_reduce(R["sum"], R["e"], AX.X, ALU.add))
            step(dve.reciprocal(R["sum"], R["sum"]))
            step(TTN(R["sc"][:, :, 0:NE], R["e"], b3(R["sum"], NE), ALU.mult))
            step(dve.memset(R["sc"][:, :, NE:NE + 2], -1.0))
            for t in range(TT):
                step(dve.max(R["top"][:, t, :], R["sc"][:, t, 0:NE]))
            step(dve.memset(R["top"][:, :, TOP:8], -1.0))
            for t in range(TT):
                step(dve.match_replace(R["mr"][:, t, :], R["top"][:, t, :], R["sc"][:, t, :], -2.0))
            STT(R["wd"], R["mr"][:, :, 0:NE], -2.0, R["sc"][:, :, 0:NE], ALU.is_equal, ALU.mult).then_inc(rt_wd, 1)
            dve.wait_ge(rt_flat, 1)
            fl, fm = (R[n].rearrange("p t (f k) -> p (t f) k", k=NK) for n in ("fl", "fm"))
            step(dve.tensor_copy(R["fl"], ps[:, 3, :].rearrange("p (t e) -> p t e", e=NE)))
            step(dve.tensor_reduce(R["gt"][:, :, NE:GATES], R["fl"].rearrange("p t (f k) -> p t f k", k=NK), AX.X, ALU.add))
            step(TS(R["fm"], R["fl"], 0.0, -1e9, ALU.is_equal, ALU.mult))
            step(TTN(R["fm"], R["fm"], R["fl"], ALU.add))
            step(dve.tensor_reduce(R["gmx"], fm, AX.X, ALU.max))
            step(TTN(fm, fm, b3(R["gmx"], NK), ALU.subtract))
            dve.sem_inc(exp_in, 1)
            dve.wait_ge(exp_out, 10)
            step(dve.tensor_reduce(R["gmx"], fm, AX.X, ALU.add))
            step(dve.reciprocal(R["gmx"], R["gmx"]))
            TTN(R["gt"][:, :, 0:NE].rearrange("p t (f k) -> p t f k", k=NK),
                R["fm"].rearrange("p t (f k) -> p t f k", k=NK),
                R["gmx"].rearrange("p (t f) -> p t f", f=NF).unsqueeze(3).to_broadcast([P, TT, NF, NK]),
                ALU.mult).then_inc(rt_gt, 1)
            dve.wait_ge(rt_gates_sb, 1)

            def turn_slot(pair, s):
                b, f = slots[s], pair * 2 + s
                dve.wait_ge(load[f"moe{s}"], pair * SLOT_LOADED + SLOT_LOADED)
                TS(gates_f[s][0:GATES, :], gates_t[0:GATES, :], group_mask[0:GATES, bass.ds(f, 1)], None, ALU.mult
                   ).then_inc(moe_masked, 1)
                for j, n in enumerate(("gs", "us")):
                    v = b["qb"][0:IC, :, 64 * j:64 * j + 64]
                    TTN(v, v, b[n][0:IC, :].unsqueeze(2).to_broadcast([IC, NI, 64]), ALU.mult)
                TTN(b["dqb"], b["dqb"], b["ds"].unsqueeze(2).to_broadcast([P, KC, 64]), ALU.mult).then_inc(moe_fixed, 1)
                dve.wait_ge(moe_turned, f * 5 + 2)
                dve.tensor_copy(b["uT"], ps[:, 6 + (1 + s) % 2, :].rearrange("p (k n) -> p k n", k=KC)[:, :, 0:INNER]
                                ).then_inc(moe_ev_dve, 1)
                dve.wait_ge(moe_turned, f * 5 + 4)
                bk = 6 + (1 + s) % 2
                dve.tensor_copy(b["qaT"], ps[:, bk, 0:256].rearrange("p (k n) -> p k n", k=KC))
                dve.tensor_copy(b["dqbT"][0:64, :], ps[0:64, bk, 256:512]).then_inc(moe_ev_dve, 1)

            def expert(f, s):
                M = moe
                for h in range(TH):
                    n = f * 2 + h
                    dve.wait_ge(moe_mu, n + 1)
                    TTN(M["xe"][:, h], ps[:, 0:2, :], xn_t[:, :, tok(h)], ALU.add).then_inc(moe_xe, 1)
                    dve.wait_ge(moe_a, n + 1)
                    dve.wait_ge(moe_wr, n * 2 + 2)
                    TTN(M["aw"], ps[:, 0, :], M["wr"], ALU.mult).then_inc(moe_aw, 1)
                    for i in range(NI):
                        dve.wait_ge(moe_s, n * 2 + (1 + i))
                        TTN(M["s"][0:IC, i, :], M["s"][0:IC, i, :], M["sr"][0:IC, :], ALU.mult).then_inc(moe_sm, 1)
                        dve.wait_ge(moe_sm, n * 2 + (1 + i))
                        TTN(M["h"][0:IC, i, :], ps[0:IC, (2, 0)[i], :], M["s"][0:IC, i, :], ALU.mult
                            ).then_inc(moe_hg, 1)
                    dve.wait_ge(moe_ad, n + 1)
                    TTN(M["awd"][0:64, :], ps[0:64, 1, :], M["wr"][0:64, :], ALU.mult).then_inc(moe_awd, 1)
                    dve.wait_ge(moe_y, n + 1)
                    add_y(h).then_inc(moe_x, 1)

            dve.sem_inc(moe_ev_dve, 1)
            dve.sem_inc(moe_x, 1)
            with dve.Fori(0, NF // 2) as pair:
                for s in range(2):
                    turn_slot(pair, s)
                    expert(pair * 2 + s, s)

            def gate_std(h, i, r, s, ga, up, hid):
                return TTN(hid, up, s, ALU.mult)
            dve.wait_ge(moe_x, 2 * NF + 1)
            ffn(l1, gate_std)

            layer_norm("l2x")
            A = att_small
            for t in range(TT):
                for j in range(2):
                    n = 2 * t + j
                    dve.wait_ge(pj_ready, n + 1)
                    if j:
                        dve.tensor_copy(k_tok[:, t, :], ps[:, n % 4, 0:D]).then_inc(pj_used, 1)
                    else:
                        TS(q_tok[:, t, :], ps[:, n % 4, 0:D], 1.0 / math.sqrt(HD), None, ALU.mult
                           ).then_inc(pj_used, 1)
            for h in range(TH):
                for o in range(KC):
                    dve.wait_ge(v_ready, 2 * h + o + 1)
                    step(TS(v_t[:, o, tok(h)], ps[:, 4 + 2 * h + o, :], A["bvp"][:, o:o + 1], None, ALU.add))
            step(dve.tensor_reduce(A["vmax"], v_t, AX.X, ALU.max, apply_absolute_value=True))
            step(TS(A["sv"], A["vmax"], 1.0 / 127.0, 1e-8, ALU.mult, ALU.max))
            step(dve.reciprocal(A["vinv"], A["sv"]))
            for o in range(KC):
                step(TS(v_t[:, o, :], v_t[:, o, :], A["vinv"][:, o:o + 1], ROUND, ALU.mult, ALU.add))
            TS(vn_t, v_t, ROUND, None, ALU.subtract).then_inc(vn_ready, 1)
            dve.wait_ge(vn_ready, 1)
            dve.wait_ge(pj_used, 2 * TT)
            for j, (src, s_, three_) in enumerate(((q_tok, A["sq"].rearrange("p t h -> p (t h)"), q3),
                                                   (k_tok, A["sk"], k3))):
                v = src.rearrange("p t (h d) -> p (t h) d", d=HD)
                tmp = q_tmp.rearrange("p t (h d) -> p (t h) d", d=HD)
                o = three_.rearrange("p t h c d -> p (t h) c d")
                step(dve.tensor_reduce(A["amax"], v, AX.X, ALU.max, apply_absolute_value=True))
                step(TS(s_, A["amax"], 1.0 / 127.0, 1e-8, ALU.mult, ALU.max))
                step(dve.reciprocal(A["inv"], s_))
                step(TTN(tmp, v, b3(A["inv"], HD), ALU.mult))
                if j == 0:
                    step(TS(tmp, tmp, ROUND, None, ALU.add))
                    for c_ in range(3):
                        last = TS(o[:, :, c_, :], tmp, ROUND, None, ALU.subtract)
                    last.then_inc(qk_split, 1)
                    dve.wait_ge(qk_split, 1)
                else:
                    step(TS(tmp, tmp, ROUND, ROUND, ALU.add, ALU.subtract))
                    step(TTN(tmp, tmp, b3(s_, HD), ALU.mult))
                    step(dve.tensor_copy(o[:, :, 0, :], tmp))
                    step(TTN(tmp, tmp, o[:, :, 0, :], ALU.subtract))
                    step(dve.tensor_copy(o[:, :, 1, :], tmp))
                    TTN(o[:, :, 2, :], tmp, o[:, :, 1, :], ALU.subtract).then_inc(qk_split, 1)
            for n in range(2 * HEADS):
                if n % 2:
                    dve.wait_ge(head_turned, n + 1)
                    dve.wait_ge(head_copied, n)
                    dst = (q_s, k_s)[n // HEADS]
                    dve.tensor_copy(dst[0:3 * HD, n % HEADS, :], ps[0:3 * HD, n % 2, :].bitcast(BF16)
                                    ).then_inc(head_copied, 1)
            for k in range(KC):
                dve.wait_ge(vn_turned, k + 1)
                dve.tensor_copy(v_tok[:, :, k * P:(k + 1) * P],
                                ps[:, 2 + k, :].bitcast(BF16).rearrange("p (t d) -> p t d", t=TT)).then_inc(v_copied, 1)
            dve.sem_inc(att_o_used, 1)
            with dve.Fori(0, TT) as t:
                for i in range(HEADS + 1):
                    if i < HEADS:
                        b = i % 2
                        dve.wait_ge(att_s, t * HEADS + (i + 1))
                        dve.tensor_reduce(A["nm"][:, b:b + 1], ps[:, 2 * b:2 * b + 2, :], AX.XY, ALU.max, negate=True
                                          ).then_inc(att_max, 1)
                        dve.wait_ge(att_max, t * HEADS + (i + 1))
                        TS(A["bias"][:, b:b + 1], A["nm"][:, b:b + 1], A["sq"][:, bass.ds(t, 1), i], math.log(255.0),
                           ALU.mult, ALU.add).then_inc(att_bias, 1)
                    j = i - 1
                    if j >= 0 and j % 2:
                        dve.wait_ge(att_t, t * HEADS + (j + 1))
                        dve.tensor_copy(att_pt[:, 1].rearrange("p a b -> p (a b)"), ps[:, 5, :].bitcast(BF16)
                                        ).then_inc(att_evd, 1)
                dve.wait_ge(att_o, t + 1)
                dve.wait_ge(att_exp, t * HEADS + HEADS)
                dve.reciprocal(A["rz"], A["z"][:, bass.ds(t, 1), :].rearrange("p a h -> p (a h)")).then_inc(att_rz, 1)
                dve.wait_ge(att_rz, t + 1)
                TTN(o_tok[:, bass.ds(t, 1), :].rearrange("p a (h d) -> p (a h) d", d=HD),
                    ps[:, 6, 0:D].rearrange("p (h d) -> p h d", d=HD), b3(A["rz"], HD), ALU.mult
                    ).then_inc(att_o_used, 1)
            for n in range(4):
                h, k = divmod(n, 2)
                dve.wait_ge(ot_turned, n + 1)
                TS(o_t[:, k, tok(h)], ps[:, n, :], A["sv"][:, k:k + 1], None, ALU.mult).then_inc(ot_copied, 1)
            for h in range(TH):
                dve.wait_ge(att_done, h + 1)
                for o in range(KC):
                    last = STT(x_t[:, o, tok(h)], ps[:, 4 + 2 * h + o, :], A["bpp"][:, o:o + 1], x_t[:, o, tok(h)],
                               ALU.add, ALU.add)
                    if o == 0:
                        step(last)
                last.then_inc(x_ready, 1)

            ternary(w_l2, H2, tern_tmp2, tern_s2, (load["l2"], 16 * 5), False)
            copy_out(dve, "l2", 1)
            layer_norm("l2")
            ffn(l2, gate_std)

            copy_out(dve, "lx", 1)
            layer_norm("l3x")
            step(dve.memset(v1[:, :, :, P:P + 1], 1.0))
            for t in range(TT):
                dve.wait_ge(lx_kv, 2 * t + 1)
                if t >= 2:
                    dve.wait_ge(lx_exp_r, t - 1)
                TS(lx_min[:, t % 2, :], ps[:, t % 2, 0:D], 0.0, None, ALU.min).then_inc(lx_min_r, 1)
                dve.wait_ge(lx_exp_r, t + 1)
                STT(kf[:, t, :], ps[:, t % 2, 0:D], 0.0, lx_exp[:, t % 2, :], ALU.max, ALU.add).then_inc(lx_kf, 1)
            for b in range(BATCH):
                dve.wait_ge(lx_sum, b + 1)
                for m in range(KC):
                    c0 = m * (P + 1)
                    step(TTN(bd[:, b, m, :], ps[:, b, c0:c0 + P], head_mask[:, :], ALU.mult))
                    step(TS(dd[:, b, m, :], head_mask[:, :], ps[:, b, c0 + P:c0 + P + 1], None, ALU.mult))
            dve.sem_inc(lx_bd, 1)
            for h in range(TH):
                dve.wait_ge(lx_qg, 2 * h + 1)
                TS(lx_qmin, ps[:, 0:2, :], 0.0, None, ALU.min).then_inc(lx_qmin_r, 1)
                dve.wait_ge(lx_act, 3 * h + 1)
                STT(lx_q, ps[:, 0:2, :], 0.0, lx_qmin, ALU.max, ALU.add).then_inc(lx_qf, 1)
                dve.wait_ge(lx_att, h + 1)
                step(TS(lx_den, ps[:, 6:8, :], 1e-6, None, ALU.add))
                step(dve.reciprocal(lx_den, lx_den))
                step(TTN(lx_den, ps[:, 4:6, :], lx_den, ALU.mult))
                dve.wait_ge(lx_act, 3 * h + 3)
                TTN(lx_o, lx_den, lx_gate, ALU.mult).then_inc(lx_or, 1)
                dve.wait_ge(y_ready, h + 1)
                TTN(x_t[:, :, tok(h)], ps[:, 0:2, :], x_t[:, :, tok(h)], ALU.add).then_inc(x_ready, 1)

            def mx_quant(v, q, s, n):
                qf = q.rearrange("p (a b) -> p a b", b=MX_BLOCK)
                sc_ = s[:, 0:n]
                step(dve.tensor_reduce(sc_, v, AX.X, ALU.max, apply_absolute_value=True))
                step(TS(sc_, sc_, 1.0 / MX_MAX, 1e-30, ALU.mult, ALU.max))
                step(dve.reciprocal(s2[:, 0:n], sc_))
                step(TTN(v, v, b3(s2[:, 0:n], MX_BLOCK), ALU.mult))
                step(TS(q.bitcast(I32), v.rearrange("p a b -> p (a b)").bitcast(I32), 0x7F800000, None,
                        ALU.bitwise_and))
                step(TS(qf, qf, 2.0 ** -6, 1.5 * 2.0 ** 20, ALU.max, ALU.mult))
                step(TTN(v, v, qf, ALU.add))
                step(TTN(v, v, qf, ALU.subtract))
                return TTN(v, v, b3(sc_, MX_BLOCK), ALU.mult)
            s2 = mx_s[2]
            layer_norm("l3")
            for n in range(8):
                h, k = divmod(n % 4, 2)
                dve.wait_ge(xt_turned, n + 1)
                dst = (xn_tok, x_tok)[n // 4]
                dve.tensor_copy(dst[:, 4 * h:4 * h + 4, k * P:(k + 1) * P],
                                ps[:, n % 4, :].rearrange("p (t d) -> p t d", t=4)).then_inc(xt_copied, 1)
            dve.wait_ge(xt_copied, 8)
            mx_quant(xn_tok.rearrange("p t (a b) -> p (t a) b", b=MX_BLOCK), mxq[0], mx_s[0], 64).then_inc(xq_ready, 1)
            for n in range(4):
                h, k = divmod(n, 2)
                dve.wait_ge(xq_turned, n + 1)
                dve.tensor_copy(xq_t[:, k, tok(h)], ps[:, n, :]).then_inc(xq_copied, 1)
            dve.wait_ge(load["l3"], 16 * 3)
            for i in range(3):
                v = w_l3[i].rearrange("p c (a b) -> p (c a) b", b=MX_BLOCK)
                ins = mx_quant(v, mxq[0], mx_s[0], 64)
                if i < 2:
                    step(ins)
            ins.then_inc(weights_fixed, 1)
            copy_out(dve, "l3", 1)
            for t in range(TT):
                dve.wait_ge(m_act, t + 1)
                dve.wait_ge(m_gu, 2 * t + 2)
                if t:
                    dve.wait_ge(m_ht, t)
                step(TTN(h_tok.rearrange("p (a b) -> p a b", a=2), ps[:, 2:4, :],
                         h_act.rearrange("p (a b) -> p a b", a=2), ALU.mult))
                mx_quant(h_tok.rearrange("p (a b) -> p a b", b=MX_BLOCK), mxq[0][:, 0:H3], mx_s[0], 32
                         ).then_inc(m_h, 1)
                dve.wait_ge(m_o, t + 1)
                if t >= 2:
                    dve.wait_ge(stored[t % 2], 16 * (t // 2))
                TTN(res[:, t % 2, :], ps[:, 6, 0:D], x_tok[:, t, :], ALU.add).then_inc(m_res, 1)


_INS = ['x', 'itok_BxS_13_99985', 'ctx_2048', 'L0_ffn_w1', 'L0_ffn_w3', 'L0_ffn_w2', 'L1_xattn_w', 'L1_xattn_u',
        'L1_ffn_gate_weight', 'L1_ffn_inv_mapping', 'L1_ffn_mask_up_W', 'L1_ffn_gate_W', 'L1_ffn_gate_qa',
        'L1_ffn_gate_qb', 'L1_ffn_gate_scale', 'L1_ffn_up_W', 'L1_ffn_up_qa', 'L1_ffn_up_qb', 'L1_ffn_up_scale',
        'L1_ffn_down_W', 'L1_ffn_down_qa', 'L1_ffn_down_qb', 'L1_ffn_down_scale', 'L1_ffn_sh_gate_W',
        'L1_ffn_sh_up_W', 'L1_ffn_sh_down_W', 'L2_xattn_Wq', 'L2_xattn_bq', 'L2_xattn_Wkv', 'L2_xattn_bkv',
        'L2_xattn_Wp', 'L2_xattn_bp', 'L2_ffn_w1', 'L2_ffn_w2', 'L2_ffn_w3', 'L3_xattn_Wq', 'L3_xattn_Wg',
        'L3_xattn_bg', 'L3_xattn_Wkv', 'L3_xattn_Wo', 'L3_ffn_gate_w', 'L3_ffn_up_w', 'L3_ffn_down_w']


def kernel(**inputs):
    import numpy as _np
    import concourse.bacc as _bacc
    from concourse import mybir as _mybir
    from concourse.bass_utils import run_bass_kernel_spmd as _run

    nc = _bacc.Bacc("TRN2", target_bir_lowering=False, num_devices=1)
    arrays, args = {}, {}
    for name in _INS:
        v = _np.ascontiguousarray(inputs[name])
        arrays[f"in_{name}"] = v
        args[name] = nc.dram_tensor(f"in_{name}", v.shape, _mybir.dt.from_np(v.dtype), kind="ExternalInput").ap()
    out = nc.dram_tensor("out_0", (BATCH, SEQ, D), F32, kind="ExternalOutput").ap()
    build(nc, args, out)
    r = _run(nc, [arrays], core_ids=[0])
    return r.results[0]["out_0"]
```

```python
from contextlib import ExitStack
import math

import concourse.bass as bass
from concourse import mybir

ALU = mybir.AluOpType
ACT = mybir.ActivationFunctionType
AX = mybir.AxisListType
F32 = mybir.dt.float32
BF16 = mybir.dt.bfloat16
I32 = mybir.dt.int32

P = 128
D = 256
KC = D // P
BATCH = 4
SEQ = 256
TOK = BATCH * SEQ
TT = TOK // P
HALF = 512
TH = TOK // HALF

TOKENS_PER_EXPERT = 12500 // 4
NF = 8
NK = 8
NR = 8
NE = NF * NK
TOP = 6
INNER = 176
REST = INNER - P
PACK = 64 + REST
GATES = NE + NF
SLOT_LOADED = 16 * 21
HEADS = 16
HD = D // HEADS
ROUND = 1.5 * 2.0 ** 23
MX_BLOCK = 32
MX_MAX = 448.0
LN_EPS = 1e-5


def chunks(n):
    return [(a, min(P, n - a)) for a in range(0, n, P)]


def build(nc, a, out, stop=None):
    H0 = a["L0_ffn_w1"].shape[0]
    H1 = a["L1_ffn_sh_gate_W"].shape[0]
    H2 = a["L2_ffn_w1"].shape[0]
    H3 = a["L3_ffn_gate_w"].shape[0]

    with ExitStack() as ctx:
        def sb(name, shape, dt=F32):
            return ctx.enter_context(nc.sbuf_tensor(name, shape, dt))

        def sem(name):
            return ctx.enter_context(nc.semaphore(name))

        ps = ctx.enter_context(nc.psum_tensor("ps", [P, 8, 512], F32))
        x_t = sb("x_t", [P, KC, TOK])
        xn_t = sb("xn_t", [P, KC, TOK])
        xc = sb("xc", [P, TH, KC, HALF])
        sq = sb("sq", [P, KC, HALF])
        sd = sb("sd", [P, TH, HALF])
        ctx_t = sb("ctx_t", [P, KC, TOK])
        act_buf = sb("act_buf", [P, 2, HALF])
        hid_buf = sb("hid_buf", [P, 2, HALF])
        ident = sb("ident", [P, P])
        ident_b = sb("ident_b", [P, P], BF16)
        ones = sb("ones", [P, P])
        mean_w = sb("mean_w", [P, P])
        head_mask = sb("head_mask", [P, P])
        eps_col = sb("eps_col", [P, 1])

        arena = sb("arena", [P, 150 * 256])

        class Cut:
            def __init__(self, kb):
                self.at = int(kb * 256)

            def __call__(self, shape, dt=F32, parts=P):
                n = 1
                for s in shape:
                    n *= s
                words = n if dt in (F32, I32) else (n + 1) // 2
                v = arena[0:parts, self.at:self.at + words]
                self.at += words
                assert self.at <= 150 * 256, self.at / 256
                if dt != F32:
                    v = v.bitcast(dt)
                if len(shape) > 1:
                    names = "abcd"[:len(shape)]
                    v = v.rearrange(f"p ({' '.join(names)}) -> p {' '.join(names)}",
                                    **{c: s for c, s in zip(names[1:], shape[1:])})
                return v

        c = Cut(0)
        ctx_nat = c([TT, D])
        x_nat = c([TT, D])
        tid = c([TOK], I32)
        ge_mask = c([3, TOK], BF16)
        tok_mask = c([4, TOK], BF16)
        c = Cut(c.at / 256)
        w_l0 = [c([6, D]), c([6, D]), c([KC, H0])]
        wt_l0 = [c([KC, H0]), c([KC, H0]), c([6, D])]
        tern_tmp = c([6 * D])
        tern_s = c([32])
        assert c.at / 256 <= 75
        c = Cut(75)
        w_l1 = [c([3, D]), c([3, D]), c([KC, H1])]
        wt_l1 = [c([KC, H1]), c([KC, H1]), c([3, D])]
        gw_nat = c([D])
        gw_t = c([KC, NE])
        mu_nat = c([KC, NF, NK])
        mu_t = c([D])
        rep = c([P])
        sc_rep = c([P])
        group_mask = c([NF])
        inv_row = c([NE], I32)
        inv_f = c([3, NE])
        e_col = c([1])
        esel = c([NE])
        gates_t = c([TOK])
        gates_f = [c([TOK]) for _ in range(2)]
        moe_at = c.at / 256
        slots = []
        for _ in range(2):
            slots.append(dict(
                main=c([2, D]), rest=c([D]), qa=c([D]),
                d=c([KC, PACK + P]), dqa=c([PACK + P]), qb=c([P]), qb_rest=c([P]),
                s_main=c([2]), s_rest=c([1]), s_down=c([KC]),
                mainT=c([2, KC, P]), restT=c([KC, PACK]), qaT=c([KC, P]), qbT=c([P]), qb_restT=c([PACK]),
                dqaT=c([64]), dqa_restT=c([64]), dT=c([D]), packT=c([D])))
        c = Cut(0)
        wk = dict(w=c([KC]), u=c([KC]), wb=c([SEQ]), o=c([BATCH, SEQ + 1]), p=c([BATCH, SEQ + 1]),
                  q=c([BATCH, SEQ + 1]), e1=c([BATCH, SEQ]), e2=c([BATCH, SEQ]), ev=c([BATCH, SEQ]),
                  no=c([BATCH, SEQ]), e3=c([BATCH, SEQ]), e4=c([BATCH, SEQ]), num=c([BATCH, SEQ]),
                  den=c([BATCH, SEQ]))
        c = Cut(0)
        rt = dict(mx=c([TT]), sum=c([TT]), e=c([TT, NE]), sc=c([TT, NE + 2]), top=c([TT, 8]),
                  mr=c([TT, NE + 2]), wd=c([TT, NE]), wdT=c([TOK]), fl=c([TT, NE]), fm=c([TT, NE]),
                  gmx=c([TT * NF]), gt=c([TT, GATES]))
        moe = dict(xe=c([TH, KC, HALF]), wr=c([TH, HALF]), sr=c([TH, HALF]), aw=c([HALF]),
                   s=c([2, HALF]), h=c([HALF]), pack=c([HALF]))
        assert c.at / 256 < 75
        c = Cut(0)
        q_s = c([HEADS, TOK], BF16)
        k_s = c([HEADS, TOK], BF16)
        v_tok = c([TT, D], BF16)
        q_tok = c([TT, D])
        k_tok = c([TT, D])
        at_q3 = c.at / 256
        q3 = c([TT, HEADS, 3, HD], BF16)
        k3 = c([TT, HEADS, 3, HD], BF16)
        v_t = c([KC, TOK])
        vn_t = c([KC, TOK], BF16)
        k_end = c.at / 256
        att_small = dict(amax=c([TT * HEADS]), inv=c([TT * HEADS]), sq=c([TT, HEADS]), sk=c([TT * HEADS]),
                         z=c([TT, HEADS]), rz=c([HEADS]), nm=c([2]), bias=c([2]), sv=c([KC]), vinv=c([KC]),
                         vmax=c([KC]), bvp=c([KC]), bpp=c([KC]), vout=c([KC]))
        bq_row = c([D], parts=1)
        bk_row = c([D], parts=1)
        wq2 = c([KC, D])
        wkv2 = c([KC, 2 * D])
        wp2 = c([KC, D])
        att_end = c.at / 256
        c2 = Cut(at_q3)
        att_e = c2([2, TOK])
        att_p = c2([2, TOK], BF16)
        att_pt = c2([4, TT, P], BF16)
        assert c2.at / 256 <= k_end
        o_tok, o_t = q_tok, k_tok.rearrange("p a b -> p (a b)").rearrange("p (k t) -> p k t", k=KC)
        q_tmp = v_t.rearrange("p k t -> p (k t)").rearrange("p (a b) -> p a b", a=TT)
        c = Cut(0)
        w_l2 = [c([6, D]), c([6, D]), c([KC, H2])]
        wt_l2 = [c([KC, H2]), c([KC, H2]), c([6, D])]
        tern_tmp2 = c([6 * D])
        tern_s2 = c([32])
        lx_nat = [c([KC, D]), c([KC, D]), c([KC, D]), c([4, D])]
        lx_t = [c([KC, D]), c([KC, D]), c([KC, D]), c([KC, 2 * D])]
        kf = c([TT, D])
        v1 = c([TT, KC, P + 1])
        lx_min = c([2, D])
        lx_exp = c([2, D])
        bd = c([BATCH, KC, P])
        dd = c([BATCH, KC, P])
        bg = c([KC])
        lx_qmin = c([KC, HALF])
        lx_q = c([KC, HALF])
        lx_gate = c([KC, HALF])
        lx_den = c([KC, HALF])
        lx_o = c([KC, HALF])
        c = Cut(0)
        w_l3 = [c([8, D]), c([8, D]), c([KC, H3])]
        wt_l3 = [c([KC, H3]), c([KC, H3]), c([8, D])]
        mxq = [c([8 * D]) for _ in range(3)]
        mx_s = [c([64]) for _ in range(3)]
        xn_tok = c([TT, D])
        xq_t = c([KC, TOK])
        h_tok = c([H3])
        h_act = c([H3])
        hq_t = c([8, P])
        x_tok = c([TT, D])
        res = c([2, D])

        dve_step, act_step, pool_step = sem("dve_step"), sem("act_step"), sem("pool_step")
        const_ready = sem("const_ready")
        load = {n: sem("load_" + n) for n in ("ctx", "x", "tid", "l0", "l1", "mu", "wku", "inv", "moe0", "moe1",
                                               "l2x", "l2", "l3x", "l3")}
        turned, evac_act, evac_dve = sem("turned"), sem("evac_act"), sem("evac_dve")
        weights_fixed = sem("weights_fixed")
        x_ready = sem("x_ready")
        ln_mean, ln_xc, ln_sq, ln_var, ln_sd, xn_ready = (sem(n) for n in (
            "ln_mean", "ln_xc", "ln_sq", "ln_var", "ln_sd", "xn_ready"))
        hid_ready, act_ready, gated, hid_used, y_ready = (sem(n) for n in (
            "hid_ready", "act_ready", "gated", "hid_used", "y_ready"))
        tern_part, tern_sum = sem("tern_part"), sem("tern_sum")
        exp_in, exp_out = sem("exp_in"), sem("exp_out")
        rt_logits, rt_wd, rt_wdt, rt_wdt_sb, rt_flat, rt_gt, rt_gatest, rt_gates_sb = (sem(n) for n in (
            "rt_logits", "rt_wd", "rt_wdt", "rt_wdt_sb", "rt_flat", "rt_gt", "rt_gatest", "rt_gates_sb"))
        moe_masked, moe_fixed, moe_turn_a, moe_turn_d, moe_ev_act, moe_ev_dve, slots_clear = (sem(n) for n in (
            "moe_masked", "moe_fixed", "moe_turn_a", "moe_turn_d", "moe_ev_act", "moe_ev_dve", "slots_clear"))
        (moe_mu, moe_wrm, moe_srm, moe_xe, moe_wr, moe_sr, moe_a, moe_aw, moe_h, moe_s, moe_sm, moe_hg, moe_ad,
         moe_awd, moe_y, moe_x) = (sem(n) for n in (
             "moe_mu", "moe_wrm", "moe_srm", "moe_xe", "moe_wr", "moe_sr", "moe_a", "moe_aw", "moe_h", "moe_s",
             "moe_sm", "moe_hg", "moe_ad", "moe_awd", "moe_y", "moe_x"))
        pj_ready, pj_used, v_ready, qk_split, head_turned, head_copied = (sem(n) for n in (
            "pj_ready", "pj_used", "v_ready", "qk_split", "head_turned", "head_copied"))
        vn_ready, vn_turned, v_copied = sem("vn_ready"), sem("vn_turned"), sem("v_copied")
        att_s, att_max, att_bias, att_exp, att_round, att_t, att_copied, att_o, att_o_used = (sem(n) for n in (
            "att_s", "att_max", "att_bias", "att_exp", "att_round", "att_t", "att_copied", "att_o",
            "att_o_used"))
        att_rz = sem("att_rz")
        ot_turned, ot_copied, att_done = sem("ot_turned"), sem("ot_copied"), sem("att_done")
        lx_kv, lx_min_r, lx_exp_r, lx_kf, lx_v, lx_sum, lx_bd = (sem(n) for n in (
            "lx_kv", "lx_min_r", "lx_exp_r", "lx_kf", "lx_v", "lx_sum", "lx_bd"))
        lx_qg, lx_qmin_r, lx_act, lx_qf, lx_att, lx_or = (sem(n) for n in (
            "lx_qg", "lx_qmin_r", "lx_act", "lx_qf", "lx_att", "lx_or"))
        xt_turned, xt_copied, xq_ready, xq_turned, xq_copied = (sem(n) for n in (
            "xt_turned", "xt_copied", "xq_ready", "xq_turned", "xq_copied"))
        m_gu, m_act, m_h, m_ht, m_htc, m_o, m_res = (sem(n) for n in (
            "m_gu", "m_act", "m_h", "m_ht", "m_htc", "m_o", "m_res"))
        stored = [sem("stored_even"), sem("stored_odd")]

        groups = []

        def turn_in(rows, nat, dst, wait, fixed):
            full = rows // P
            todo = [(r, 2) for r in range(0, full - 1, 2)]
            if full % 2:
                todo.append((full - 1, 1))
            todo = [(r * P, [P] * n) for r, n in todo]
            if rows % P:
                todo.append((full * P, [rows % P]))
            for r0, ws in todo:
                turns = [(P, w, k * 256 + j * P, nat[0:w, r0 // P + j, k * P:(k + 1) * P])
                         for k in range(KC) for j, w in enumerate(ws)]
                n = sum(ws)
                groups.append((turns, [(dst[:, :, r0:r0 + n], P, 0, 256, n)], wait, fixed))

        def turn_out(cols, nat, dst, wait, fixed):
            full = cols // P
            for c0 in range(0, full, 2):
                n = min(2, full - c0)
                turns = [(P, P, j * 256 + r * P, nat[:, r, (c0 + j) * P:(c0 + j + 1) * P])
                         for j in range(n) for r in range(KC)]
                groups.append((turns, [(dst[:, c0:c0 + n, :], P, 0, 256, 256)], wait, fixed))
            if cols % P:
                w = cols % P
                turns = [(w, P, r * P, nat[:, r, full * P:cols]) for r in range(KC)]
                groups.append((turns, [(dst[0:w, full:full + 1, :], w, 0, 256, 256)], wait, fixed))

        marks = {}

        def mark(name, f):
            first = len(groups)
            f()
            marks[name] = (first, len(groups))

        def tokens_turned(nat, dst, wait):
            for h in range(TH):
                for k in range(KC):
                    turns = [(P, P, j * P, nat[:, 4 * h + j, k * P:(k + 1) * P]) for j in range(4)]
                    groups.append((turns, [(dst[:, k, h * HALF:(h + 1) * HALF].unsqueeze(1), P, 0, 512, 512)],
                                   wait, 0))

        mark("x", lambda: tokens_turned(x_nat, x_t, (load["x"], 16)))
        mark("ctx", lambda: tokens_turned(ctx_nat, ctx_t, (load["ctx"], 16)))

        def three(ws, wts, h, wait, fixed):
            turn_in(h, ws[0], wts[0], wait, fixed)
            turn_in(h, ws[1], wts[1], wait, fixed)
            turn_out(h, ws[2], wts[2], wait, fixed)
        mark("l0", lambda: three(w_l0, wt_l0, H0, None, 1))
        mark("l1", lambda: three(w_l1, wt_l1, H1, (load["l1"], 16 * 5), 0))

        def small():
            turns = [(P, NE, k * NE, gw_nat[0:NE, k * P:(k + 1) * P]) for k in range(KC)]
            groups.append((turns, [(gw_t[:, :, :], P, 0, NE, NE)], (load["mu"], 16 * 3), 0))
            turns = [(NE, P, k * P, mu_nat[:, k, :, :].rearrange("p f k -> p (f k)")) for k in range(KC)]
            groups.append((turns, [(mu_t[0:NE, :].unsqueeze(1), NE, 0, 256, 256)], (load["mu"], 16 * 3), 0))
        mark("small", small)
        mark("l2", lambda: three(w_l2, wt_l2, H2, None, 2))

        def lx():
            turn_in(D, lx_nat[0], lx_t[0], (load["l3x"], 16 * 5), 0)
            turn_in(D, lx_nat[1], lx_t[1], (load["l3x"], 16 * 5), 0)
            turn_in(D, lx_nat[2], lx_t[2], (load["l3x"], 16 * 5), 0)
            turn_in(2 * D, lx_nat[3], lx_t[3], (load["l3x"], 16 * 5), 0)
        mark("lx", lx)
        mark("l3", lambda: three(w_l3, wt_l3, H3, None, 3))

        def evacuated(eng, upto):
            eng.wait_ge(evac_act, (upto + 1) // 2)
            if upto // 2:
                eng.wait_ge(evac_dve, upto // 2)

        def pe_turn(pe, name):
            for g in range(*marks[name]):
                turns, _, wait, fixed = groups[g]
                if g >= 2:
                    pe.wait_ge(evac_dve if g % 2 else evac_act, g // 2)
                if wait:
                    pe.wait_ge(*wait)
                if fixed:
                    pe.wait_ge(weights_fixed, fixed)
                for m, w, col, src in turns:
                    last = pe.transpose(ps[0:m, 6 + g % 2, col:col + w], src, ident[0:src.shape[0], 0:src.shape[0]])
                last.then_inc(turned, 1)

        def copy_out(eng, name, parity):
            for g in range(*marks[name]):
                if g % 2 != parity:
                    continue
                eng.wait_ge(turned, g + 1)
                for dst, m, col, step, n in groups[g][1]:
                    k = dst.shape[1]
                    src = ps[0:m, 6 + g % 2, col:col + k * step].rearrange("p (k n) -> p k n", k=k)[:, :, 0:n]
                    if parity:
                        last = eng.tensor_copy(dst, src)
                    else:
                        last = eng.activation(dst, src, ACT.Copy)
                last.then_inc(evac_dve if parity else evac_act, 1)

        def std_ffn(name, wts, h):
            ch = chunks(h)
            return dict(name=name, n=len(ch), rows=[w for _, w in ch],
                        w1=lambda k, i: wts[0][:, k, ch[i][0]:ch[i][0] + ch[i][1]],
                        w3=lambda k, i: wts[1][:, k, ch[i][0]:ch[i][0] + ch[i][1]],
                        w2=lambda i, o: wts[2][0:ch[i][1], i, o * P:(o + 1) * P])

        l0x = dict(name="l0x", n=4 * KC, rows=[P] * 4 * KC,
                   w1=lambda k, i: ctx_t[:, k, i * P:(i + 1) * P], w3=None,
                   w2=lambda i, o: ctx_t[:, i % KC, (i // KC) * SEQ + o * P:(i // KC) * SEQ + (o + 1) * P])
        l0 = std_ffn("l0", wt_l0, H0)
        l1 = std_ffn("l1", wt_l1, H1)
        l2 = std_ffn("l2", wt_l2, H2)
        unit = 0
        halves = 0
        for s in (l0x, l0, l1, l2):
            s["u0"], s["y0"] = unit, halves
            unit += TH * s["n"]
            halves += TH
        LN = dict(l0x=0, l0=1, wkv=2, l1=3, l2x=4, l2=5, l3x=6, l3=7)

        def tok(h):
            return slice(h * HALF, (h + 1) * HALF)

        block = ctx.enter_context(nc.Block())

        @block.sync
        def _(sp):
            sp.dma_start(x_nat, a["x"].rearrange("b (c p) d -> p (b c) d", p=P)).then_inc(load["x"], 16)
            sp.dma_start(ctx_nat, a["ctx_2048"].rearrange("b (c p) d -> p (b c) d", p=P)).then_inc(load["ctx"], 16)
            sp.dma_start(tid, a["itok_BxS_13_99985"].rearrange("b s -> (b s)").partition_broadcast(P)
                         ).then_inc(load["tid"], 16)

            def rows_in(dst, src, s):
                full = src.shape[0] // P
                sp.dma_start(dst[:, 0:full, :], src[0:full * P, :].rearrange("(c p) d -> p c d", p=P)).then_inc(s, 16)
                if src.shape[0] % P:
                    sp.dma_start(dst[0:src.shape[0] % P, full, :], src[full * P:, :]).then_inc(s, 16)

            for w, n in zip(w_l0, ("L0_ffn_w1", "L0_ffn_w3", "L0_ffn_w2")):
                rows_in(w, a[n], load["l0"])
            for w, n in zip(w_l1, ("L1_ffn_sh_gate_W", "L1_ffn_sh_up_W", "L1_ffn_sh_down_W")):
                rows_in(w, a[n], load["l1"])
            sp.dma_start(gw_nat[0:NE, :], a["L1_ffn_gate_weight"]).then_inc(load["mu"], 16)
            for k in range(KC):
                sp.dma_start(mu_nat[:, k], a["L1_ffn_mask_up_W"][:, k * P:(k + 1) * P, :].rearrange("f p k -> p f k")
                             ).then_inc(load["mu"], 16)
            sp.dma_start(inv_row[0:NE], a["L1_ffn_inv_mapping"].rearrange("f k -> (f k)").partition_broadcast(NE)
                         ).then_inc(load["inv"], 16)

            def load_slot(f, s):
                b = slots[s]
                done = load[f"moe{s}"]
                f1 = bass.ds(f, 1)

                def go(dst, src, columns=False):
                    sp.dma_start(dst, src, allow_slow_non_contiguous=columns).then_inc(done, 16)
                for j, (w, qb, qa, sc) in enumerate((
                        ("L1_ffn_gate_W", "L1_ffn_gate_qb", "L1_ffn_gate_qa", "L1_ffn_gate_scale"),
                        ("L1_ffn_up_W", "L1_ffn_up_qb", "L1_ffn_up_qa", "L1_ffn_up_scale"))):
                    r0 = 64 * j
                    go(b["main"][:, j, :], a[w][f1, 0:P].rearrange("f p d -> p (f d)"))
                    go(b["rest"][r0:r0 + REST], a[w][f1, P:INNER].rearrange("f p d -> p (f d)"))
                    go(b["qa"][r0:r0 + 64], a[qa][f1].rearrange("f k r d -> (f k r) d"))
                    go(b["qb"][:, r0:r0 + 64].rearrange("p (k r) -> p k r", k=NK),
                       a[qb][f1, :, 0:P, :].rearrange("f k p r -> p (f k) r"))
                    go(b["qb_rest"][r0:r0 + REST, r0:r0 + 64].rearrange("p (k r) -> p k r", k=NK),
                       a[qb][f1, :, P:INNER, :].rearrange("f k p r -> p (f k) r"))
                    go(b["s_main"][:, j:j + 1], a[sc][f1, 0:P].rearrange("f p -> p f"), True)
                    go(b["s_rest"][r0:r0 + REST], a[sc][f1, P:INNER].rearrange("f p -> p f"), True)
                down = a["L1_ffn_down_W"][f1].rearrange("f (c p) d -> p (f c) d", p=P)
                go(b["d"][:, :, PACK:], down[:, :, 0:P])
                go(b["d"][:, :, 64:PACK], down[:, :, P:INNER])
                dqa = a["L1_ffn_down_qa"][f1].rearrange("f k r d -> (f k r) d")
                go(b["dqa"][0:64, PACK:], dqa[:, 0:P])
                go(b["dqa"][0:64, 64:PACK], dqa[:, P:INNER])
                for i in range(KC):
                    go(b["d"][:, i, 0:64].rearrange("p (k r) -> p k r", k=NK),
                       a["L1_ffn_down_qb"][f1, :, i * P:(i + 1) * P, :].rearrange("f k p r -> p (f k) r"))
                go(b["s_down"], a["L1_ffn_down_scale"][f1].rearrange("f (c p) -> p (f c)", p=P), True)

            sp.wait_ge(slots_clear, 1)
            load_slot(0, 0)
            load_slot(1, 1)
            sp.wait_ge(x_ready, 2 * LN["wkv"] + 2)
            for n, d in (("L1_xattn_w", wk["w"]), ("L1_xattn_u", wk["u"])):
                sp.dma_start(d, a[n].rearrange("(k p) -> p k", p=P),
                             allow_slow_non_contiguous=True).then_inc(load["wku"], 16)
            with sp.Fori(1, NF // 2) as pair:
                for s in range(2):
                    sp.wait_ge(moe_turn_a, pair * 4 + (2 * s - 2))
                    sp.wait_ge(moe_turn_d, pair * 4 + (2 * s - 2))
                    load_slot(pair * 2 + s, s)
            sp.wait_ge(x_ready, 2 * LN["l2x"] + 2)
            for d, s in ((wq2, a["L2_xattn_Wq"]), (wkv2, a["L2_xattn_Wkv"]), (wp2, a["L2_xattn_Wp"])):
                sp.dma_start(d, s.rearrange("(k p) n -> p k n", p=P)).then_inc(load["l2x"], 16)
            bkv = a["L2_xattn_bkv"]
            sp.dma_start(bq_row, a["L2_xattn_bq"].unsqueeze(0)).then_inc(load["l2x"], 16)
            sp.dma_start(bk_row, bkv[0:D].unsqueeze(0)).then_inc(load["l2x"], 16)
            sp.dma_start(att_small["bvp"], bkv[D:2 * D].rearrange("(k p) -> p k", p=P),
                             allow_slow_non_contiguous=True).then_inc(load["l2x"], 16)
            sp.dma_start(att_small["bpp"], a["L2_xattn_bp"].rearrange("(k p) -> p k", p=P),
                             allow_slow_non_contiguous=True).then_inc(load["l2x"], 16)
            sp.wait_ge(x_ready, 2 * LN["l2"] + 2)
            for w, n in zip(w_l2, ("L2_ffn_w1", "L2_ffn_w2", "L2_ffn_w3")):
                rows_in(w, a[n], load["l2"])
            for w, n in zip(lx_nat, ("L3_xattn_Wq", "L3_xattn_Wg", "L3_xattn_Wo", "L3_xattn_Wkv")):
                rows_in(w, a[n], load["l3x"])
            sp.dma_start(bg, a["L3_xattn_bg"].rearrange("(k p) -> p k", p=P),
                             allow_slow_non_contiguous=True).then_inc(load["l3x"], 16)
            sp.wait_ge(x_ready, 2 * LN["l3"] + 2)
            for w, n in zip(w_l3, ("L3_ffn_gate_w", "L3_ffn_up_w", "L3_ffn_down_w")):
                rows_in(w, a[n], load["l3"])
            rows = out.rearrange("b (c p) d -> (b c) p d", p=P)
            for t in range(TT):
                sp.wait_ge(m_res, t + 1)
                sp.dma_start(rows[t], res[:, t % 2, :]).then_inc(stored[t % 2], 16)
            for s in stored:
                sp.wait_ge(s, 16 * TT // 2)

        @block.gpsimd
        def _(pool):
            made = 0

            def step(ins):
                nonlocal made
                made += 1
                ins.then_inc(pool_step, 1)
                pool.wait_ge(pool_step, made)

            for b in slots:
                step(pool.memset(b["rest"], 0.0))
                step(pool.memset(b["qb_rest"], 0.0))
                step(pool.memset(b["dqa"], 0.0))
                step(pool.memset(b["s_rest"], 0.0))
            pool.sem_inc(slots_clear, 1)
            step(pool.memset(ones[:, :], 1.0))
            step(pool.memset(mean_w[:, :], 1.0 / D))
            step(pool.memset(eps_col[:, :], LN_EPS))
            step(pool.affine_select(out=ident[:, :], in_=ones[:, :], compare_op=ALU.is_equal, fill=0.0, base=0,
                                    pattern=[[-1, P]], channel_multiplier=1))
            step(pool.tensor_copy(ident_b[:, :], ident[:, :]))
            hm = head_mask[:, :].rearrange("p (a b) -> p a b", a=P // HD)
            on = ones[:, :].rearrange("p (a b) -> p a b", a=P // HD)
            step(pool.affine_select(out=hm, in_=on, compare_op=ALU.is_ge, fill=0.0, base=0,
                                    pattern=[[-HD, P // HD], [0, HD]], channel_multiplier=1))
            step(pool.affine_select(out=hm, in_=hm, compare_op=ALU.is_ge, fill=0.0, base=HD - 1,
                                    pattern=[[HD, P // HD], [0, HD]], channel_multiplier=-1))
            g0 = group_mask[0:NE, :]
            step(pool.memset(group_mask, 1.0))
            step(pool.affine_select(out=g0, in_=g0, compare_op=ALU.is_ge, fill=0.0, base=0,
                                    pattern=[[-NK, NF]], channel_multiplier=1))
            step(pool.affine_select(out=g0, in_=g0, compare_op=ALU.is_ge, fill=0.0, base=NK - 1,
                                    pattern=[[NK, NF]], channel_multiplier=-1))
            g1 = group_mask[NE:GATES, :]
            step(pool.affine_select(out=g1, in_=g1, compare_op=ALU.is_equal, fill=0.0, base=0,
                                    pattern=[[-1, NF]], channel_multiplier=1))
            step(pool.memset(sc_rep[0:NE, :], 0.0))
            step(pool.memset(sc_rep[NE:GATES, :], 1.0))
            step(pool.memset(rep[0:NE, :], 0.0))
            step(pool.memset(rep[NE:GATES, :], 0.0))
            rp = rep[0:NE, :].rearrange("p (a k r) -> p a k r", a=2, k=NK)
            for m in range(NF):
                step(pool.affine_select(out=rp, in_=rp, compare_op=ALU.not_equal, fill=1.0, base=-NK * m,
                                        pattern=[[0, 2], [-1, NK], [0, NR]], channel_multiplier=1))
            step(pool.iota(e_col[0:NE, :], pattern=[[0, 1]], base=0, channel_multiplier=1,
                           allow_small_or_imprecise_dtypes=True))
            step(pool.memset(mu_t[NE:GATES, :], 0.0))
            pool.sem_inc(const_ready, 1)

        @block.tensor
        def _(pe):
            def mm(o, l, r, start, stop):
                return pe.matmul(o, l, r, start=start, stop=stop)

            def layer_norm(name):
                L = LN[name]
                pe.wait_ge(x_ready, 2 * L + 2)
                for h in range(TH):
                    n = 2 * L + h
                    if h:
                        pe.wait_ge(ln_xc, n)
                    for k in range(KC):
                        last = mm(ps[:, 4, :], mean_w[:, :], x_t[:, k, tok(h)], k == 0, k == KC - 1)
                    last.then_inc(ln_mean, 1)
                for h in range(TH):
                    n = 2 * L + h
                    pe.wait_ge(ln_sq, n + 1)
                    if h:
                        pe.wait_ge(ln_sd, n)
                    for k in range(KC):
                        last = mm(ps[:, 5, :], mean_w[:, :], sq[:, k, :], k == 0, k == KC - 1)
                    last.then_inc(ln_var, 1)

            def ffn(s):
                L = LN[s["name"]]
                for h in range(TH):
                    pe.wait_ge(xn_ready, 2 * L + h + 1)

                    def down(i):
                        u = s["u0"] + h * s["n"] + i
                        pe.wait_ge(gated, u + 1)
                        if i == 0:
                            pe.wait_ge(xn_ready, 2 * L + 2)
                            if h:
                                pe.wait_ge(x_ready, 2 * (L + 1) + 1)
                        r = s["rows"][i]
                        for o in range(KC):
                            last = mm(ps[:, 4 + o, :], s["w2"](i, o), hid_buf[0:r, u % 2, :], i == 0, i == s["n"] - 1)
                        last.then_inc(hid_used, 1)

                    for i in range(s["n"]):
                        u = s["u0"] + h * s["n"] + i
                        if u >= 2:
                            pe.wait_ge(gated, u - 1)
                        r = s["rows"][i]
                        b = 2 * (u % 2)
                        for j, w in enumerate([s["w1"], s["w3"]] if s["w3"] else [s["w1"]]):
                            for k in range(KC):
                                last = mm(ps[0:r, b + j, :], w(k, i), xn_t[:, k, tok(h)], k == 0, k == KC - 1)
                        last.then_inc(hid_ready, 1)
                        if i:
                            down(i - 1)
                    down(s["n"] - 1)

            def ternary(n):
                pe.wait_ge(tern_part, n)
                st = tern_s if n == 1 else tern_s2
                mm(ps[:, 4, 0:6], ones[:, :], st[:, 0:6], True, True).then_inc(tern_sum, 1)

            pe.wait_ge(const_ready, 1)
            pe_turn(pe, "x")
            pe_turn(pe, "ctx")
            evacuated(pe, marks["ctx"][1])
            layer_norm("l0x")
            ffn(l0x)
            pe.wait_ge(x_ready, 4)
            ternary(1)
            pe_turn(pe, "l0")
            evacuated(pe, marks["l0"][1])
            layer_norm("l0")
            ffn(l0)
            layer_norm("wkv")
            pe_turn(pe, "l1")
            pe_turn(pe, "small")
            evacuated(pe, marks["small"][1])
            layer_norm("l1")
            pe.wait_ge(xn_ready, 2 * LN["l1"] + 2)
            for t in range(TT):
                for k in range(KC):
                    last = mm(ps[:, 0, t * NE:(t + 1) * NE], xn_t[:, k, t * P:(t + 1) * P], gw_t[:, k, :],
                              k == 0, k == KC - 1)
            last.then_inc(rt_logits, 1)
            pe.wait_ge(rt_wd, 1)
            for t in range(TT):
                last = pe.transpose(ps[0:NE, 1 + t // 4, (t % 4) * P:(t % 4 + 1) * P], rt["wd"][:, t, :], ident[:, :])
            last.then_inc(rt_wdt, 1)
            pe.wait_ge(rt_wdt_sb, 1)
            for t in range(TT):
                last = mm(ps[:, 3, t * NE:(t + 1) * NE], rt["wdT"][0:NE, t * P:(t + 1) * P], esel[0:NE, :], True, True)
            last.then_inc(rt_flat, 1)
            pe.wait_ge(rt_gt, 1)
            for t in range(TT):
                last = pe.transpose(ps[0:GATES, 1 + t // 4, (t % 4) * P:(t % 4 + 1) * P], rt["gt"][:, t, :], ident[:, :])
            last.then_inc(rt_gatest, 1)
            pe.wait_ge(rt_gates_sb, 1)

            def turned(m, bank, col, src):
                n = src.shape[0]
                return pe.transpose(ps[0:m, bank, col:col + n], src, ident[0:n, 0:n])

            def turn_first(f, s):
                b = slots[s]
                pe.wait_ge(moe_fixed, f + 1)
                for k in range(KC):
                    turned(P, 1, k * P, b["qa"][:, k * P:(k + 1) * P])
                turned(PACK, 1, 320, b["dqa"][0:64, 0:PACK])
                turned(P, 1, 256, b["dqa"][0:64, PACK:]).then_inc(moe_turn_a, 1)
                for j in range(2):
                    for k in range(KC):
                        last = turned(P, 3, (2 * j + k) * P, b["main"][:, j, k * P:(k + 1) * P])
                last.then_inc(moe_turn_d, 1)

            def turn_second(f, s):
                b = slots[s]
                for k in range(KC):
                    turned(P, 1, k * PACK, b["rest"][0:PACK, k * P:(k + 1) * P])
                turned(P, 1, 256, b["qb"])
                turned(P, 1, 384, b["qb_rest"][0:PACK]).then_inc(moe_turn_a, 1)
                for k in range(KC):
                    turned(P, 3, k * P, b["d"][:, k, PACK:])
                for k in range(KC):
                    last = turned(PACK, 3, 256 + k * P, b["d"][:, k, 0:PACK])
                last.then_inc(moe_turn_d, 1)

            def correction(f, s, h):
                n = f * 2 + h
                g = gates_f[s][0:GATES, tok(h)]
                if h == 0:
                    pe.wait_ge(moe_masked, f + 1)
                    pe.wait_ge(moe_ev_act, f * 2 + 1)
                if not (isinstance(f, int) and n == 0):
                    pe.wait_ge(moe_sr, n)
                mm(ps[:, 7, :], rep[0:GATES, :], g, True, True).then_inc(moe_wrm, 1)
                for o in range(KC):
                    last = mm(ps[:, o, :], mu_t[0:GATES, o * P:(o + 1) * P], g, True, True)
                last.then_inc(moe_mu, 1)
                pe.wait_ge(moe_wr, n + 1)
                mm(ps[:, 7, :], sc_rep[0:GATES, :], g, True, True).then_inc(moe_srm, 1)

            def codes(f, s, h):
                n = f * 2 + h
                if h == 0:
                    pe.wait_ge(moe_ev_act, f * 2 + 1)
                pe.wait_ge(moe_xe, n + 1)
                for k in range(KC):
                    last = mm(ps[:, 0, :], slots[s]["qaT"][:, k, :], moe["xe"][:, h, k, :], k == 0, k == KC - 1)
                last.then_inc(moe_a, 1)

            def inner(f, s, h, last_expert):
                n = f * 2 + h
                b, xe, aw = slots[s], moe["xe"][:, h], moe["aw"]
                if h == 0:
                    pe.wait_ge(moe_ev_act, f * 2 + 2)
                if h == 0:
                    pe.wait_ge(moe_ev_dve, f * 2 + 2)
                elif not last_expert:
                    pe.wait_ge(moe_ev_dve, f * 2 + 3)
                for k in range(KC):
                    mm(ps[:, 2, :], b["mainT"][:, 0, k, :], xe[:, k, :], k == 0, False)
                for k in range(KC):
                    mm(ps[0:PACK, 4, :], b["restT"][:, k, :], xe[:, k, :], k == 0, False)
                for k in range(KC):
                    mm(ps[:, 3, :], b["mainT"][:, 1, k, :], xe[:, k, :], k == 0, False)
                pe.wait_ge(moe_aw, n + 1)
                mm(ps[:, 2, :], b["qbT"][0:64, :], aw[0:64, :], False, True).then_inc(moe_h, 1)
                mm(ps[:, 3, :], b["qbT"][64:128, :], aw[64:128, :], False, True).then_inc(moe_h, 1)
                mm(ps[0:PACK, 4, :], b["qb_restT"], aw, False, True).then_inc(moe_h, 1)

            def down_codes(f, s, h):
                n = f * 2 + h
                pe.wait_ge(moe_hg, n * 2 + 2)
                mm(ps[0:64, 2, :], slots[s]["dqaT"], moe["h"], True, False)
                mm(ps[0:64, 2, :], slots[s]["dqa_restT"][64:PACK, :], moe["pack"][64:PACK, :], False, True
                   ).then_inc(moe_ad, 1)

            def result(f, s, h):
                n = f * 2 + h
                pe.wait_ge(moe_x, n + 1)
                for o in range(KC):
                    mm(ps[:, 5 + o, :], slots[s]["dT"][:, o * P:(o + 1) * P], moe["h"], True, False)
                pe.wait_ge(moe_awd, n + 1)
                for o in range(KC):
                    last = mm(ps[:, 5 + o, :], slots[s]["packT"][0:PACK, o * P:(o + 1) * P], moe["pack"][0:PACK, :],
                              False, True)
                last.then_inc(moe_y, 1)

            def unit(f, s, h, final):
                ahead = (f, s, 1) if h == 0 else (f + 1, 1 - s, 0)
                inner(f, s, h, final)
                if not final or h == 0:
                    correction(*ahead)
                down_codes(f, s, h)
                if not final or h == 0:
                    codes(*ahead)
                if not final:
                    (turn_first, turn_second)[h](f + 1, 1 - s)
                result(f, s, h)

            turn_first(0, 0)
            pe.wait_ge(moe_ev_act, 1)
            pe.wait_ge(moe_ev_dve, 1)
            turn_second(0, 0)
            pe.wait_ge(moe_ev_act, 2)
            pe.wait_ge(moe_ev_dve, 2)
            correction(0, 0, 0)
            codes(0, 0, 0)
            with pe.Fori(0, NF // 2 - 1) as pair:
                for s in range(2):
                    for h in range(TH):
                        unit(pair * 2 + s, s, h, False)
            for f in (NF - 2, NF - 1):
                for h in range(TH):
                    unit(f, f % 2, h, f == NF - 1)
            pe.wait_ge(moe_x, 2 * NF + 1)
            ffn(l1)

            layer_norm("l2x")
            pe.wait_ge(xn_ready, 2 * LN["l2x"] + 2)
            pe.wait_ge(load["l2x"], 16 * 7)
            for t in range(TT):
                for j, (src, w, row) in enumerate(((xn_t, wq2, bq_row), (ctx_t, wkv2, bk_row))):
                    n = 2 * t + j
                    if n >= 4:
                        pe.wait_ge(pj_used, n - 3)
                    o = ps[:, n % 4, 0:D]
                    for k in range(KC):
                        mm(o, src[:, k, t * P:(t + 1) * P], w[:, k, 0:D], k == 0, False)
                    mm(o, ones[0:1, :], row, False, True).then_inc(pj_ready, 1)
            for h in range(TH):
                for o in range(KC):
                    n = 2 * h + o
                    bnk = (4, 5, 6, 7)[n]
                    for k in range(KC):
                        last = mm(ps[:, bnk, :], wkv2[:, k, D + o * P:D + (o + 1) * P], ctx_t[:, k, tok(h)],
                                  k == 0, k == KC - 1)
                    last.then_inc(v_ready, 1)
            for n in range(2 * HEADS):
                src = (q3, k3)[n // HEADS]
                if n % HEADS == 0:
                    pe.wait_ge(qk_split, 1 + n // HEADS)
                if n >= 2:
                    pe.wait_ge(head_copied, n - 1)
                o = ps[:, n % 2, :].bitcast(BF16)
                for t in range(TT):
                    last = pe.transpose(o[0:3 * HD, t * P:(t + 1) * P],
                                        src[:, t, n % HEADS].rearrange("p a b -> p (a b)"), ident_b[:, :])
                last.then_inc(head_turned, 1)
            pe.wait_ge(vn_ready, 1)
            for k in range(KC):
                o = ps[:, 2 + k, :].bitcast(BF16)
                for t in range(TT):
                    last = pe.transpose(o[:, t * P:(t + 1) * P], vn_t[:, k, t * P:(t + 1) * P], ident_b[:, :])
                last.then_inc(vn_turned, 1)
            pe.wait_ge(head_copied, 2 * HEADS)
            pe.wait_ge(v_copied, KC)
            def scores(t, i):
                t, i = t + i // HEADS, i % HEADS
                for kh in range(2):
                    last = mm(ps[:, 2 * (i % 2) + kh, :], q_s[0:3 * HD, i, bass.ds(t * P, P)],
                              k_s[0:3 * HD, i, kh * 512:(kh + 1) * 512], True, True)
                last.then_inc(att_s, 1)

            def turn_probs(t, j):
                pe.wait_ge(att_round, t * HEADS + (j + 1))
                if not (isinstance(t, int) and t * HEADS + j < 2):
                    pe.wait_ge(att_copied, t * HEADS + (j - 1))
                o = ps[:, 4 + j % 2, :].bitcast(BF16)
                for k in range(TT):
                    last = pe.transpose(o[:, k * P:(k + 1) * P], att_p[:, j % 2, k * P:(k + 1) * P], ident_b[:, :])
                last.then_inc(att_t, 1)

            def values(t, j):
                pe.wait_ge(att_copied, t * HEADS + (j + 1))
                if j == 0:
                    pe.wait_ge(att_o_used, t + 1)
                for k in range(TT):
                    last = mm(ps[:, 6, j * HD:(j + 1) * HD], att_pt[:, j % 4, k, :],
                              v_tok[:, k, j * HD:(j + 1) * HD], k == 0, k == TT - 1)
                if j == HEADS - 1:
                    last.then_inc(att_o, 1)

            def query_tile(t, final):
                for i in range(4, HEADS + 4):
                    if i < HEADS or not final:
                        pe.wait_ge(att_exp, t * HEADS + (i - 1))
                        scores(t, i)
                    values(t, i - 4)
                    if i - 2 < HEADS or not final:
                        turn_probs(t, i - 2)

            scores(0, 0)
            scores(0, 1)
            pe.wait_ge(att_exp, 1)
            scores(0, 2)
            turn_probs(0, 0)
            pe.wait_ge(att_exp, 2)
            scores(0, 3)
            turn_probs(0, 1)
            with pe.Fori(0, TT - 1) as t:
                query_tile(t, False)
            query_tile(TT - 1, True)
            pe.wait_ge(att_o_used, TT + 1)
            for h in range(TH):
                for k in range(KC):
                    for j in range(4):
                        last = pe.transpose(ps[:, 2 * h + k, j * P:(j + 1) * P],
                                            o_tok[:, 4 * h + j, k * P:(k + 1) * P], ident[:, :])
                    last.then_inc(ot_turned, 1)
            for h in range(TH):
                pe.wait_ge(ot_copied, 2 * h + 2)
                for o in range(KC):
                    for k in range(KC):
                        last = mm(ps[:, 4 + 2 * h + o, :], wp2[:, k, o * P:(o + 1) * P], o_t[:, k, tok(h)],
                                  k == 0, k == KC - 1)
                last.then_inc(att_done, 1)
            pe.wait_ge(x_ready, 2 * LN["l2"] + 2)
            ternary(2)
            pe_turn(pe, "l2")
            evacuated(pe, marks["l2"][1])
            layer_norm("l2")
            ffn(l2)
            pe_turn(pe, "lx")
            evacuated(pe, marks["lx"][1])
            layer_norm("l3x")
            for t in range(TT):
                if t >= 2:
                    pe.wait_ge(lx_kf, t - 1)
                    pe.wait_ge(lx_v, t - 1)
                for j in range(2):
                    for k in range(KC):
                        last = mm(ps[:, 2 * j + t % 2, 0:D], ctx_t[:, k, t * P:(t + 1) * P],
                                  lx_t[3][:, k, j * D:(j + 1) * D], k == 0, k == KC - 1)
                    last.then_inc(lx_kv, 1)
            pe.wait_ge(lx_kf, TT)
            pe.wait_ge(lx_v, TT)
            for b in range(BATCH):
                for m in range(KC):
                    for j in range(2):
                        t = 2 * b + j
                        last = mm(ps[:, b, m * (P + 1):(m + 1) * (P + 1)], kf[:, t, m * P:(m + 1) * P], v1[:, t, m, :],
                                  j == 0, j == 1)
                last.then_inc(lx_sum, 1)
            pe.wait_ge(xn_ready, 2 * LN["l3x"] + 2)
            pe.wait_ge(lx_bd, 1)
            for h in range(TH):
                for j in range(2):
                    for o in range(KC):
                        for k in range(KC):
                            last = mm(ps[:, 2 * j + o, :], lx_t[j][:, k, o * P:(o + 1) * P], xn_t[:, k, tok(h)],
                                      k == 0, k == KC - 1)
                    last.then_inc(lx_qg, 1)
                pe.wait_ge(lx_qf, h + 1)
                for j, w in enumerate((bd, dd)):
                    for m in range(KC):
                        for b in range(2):
                            last = mm(ps[:, 4 + 2 * j + m, b * SEQ:(b + 1) * SEQ], w[:, 2 * h + b, m, :],
                                      lx_q[:, m, b * SEQ:(b + 1) * SEQ], True, True)
                last.then_inc(lx_att, 1)
                pe.wait_ge(lx_or, h + 1)
                for o in range(KC):
                    for k in range(KC):
                        last = mm(ps[:, o, :], lx_t[2][:, k, o * P:(o + 1) * P], lx_o[:, k, :], k == 0, k == KC - 1)
                last.then_inc(y_ready, 1)
                pe.wait_ge(x_ready, 2 * LN["l3x"] + 2 + h + 1)
            layer_norm("l3")
            pe.wait_ge(xn_ready, 2 * LN["l3"] + 2)
            for h in range(TH):
                for k in range(KC):
                    n = 2 * h + k
                    for j in range(4):
                        t = 4 * h + j
                        last = pe.transpose(ps[:, n, j * P:(j + 1) * P], xn_t[:, k, t * P:(t + 1) * P], ident[:, :])
                    last.then_inc(xt_turned, 1)
            for h in range(TH):
                for k in range(KC):
                    n = 2 * h + k
                    pe.wait_ge(xt_copied, n + 1)
                    for j in range(4):
                        t = 4 * h + j
                        last = pe.transpose(ps[:, n, j * P:(j + 1) * P], x_t[:, k, t * P:(t + 1) * P], ident[:, :])
                    last.then_inc(xt_turned, 1)
            pe.wait_ge(xq_ready, 1)
            pe.wait_ge(xt_copied, 8)
            for h in range(TH):
                for k in range(KC):
                    n = 2 * h + k
                    for j in range(4):
                        t = 4 * h + j
                        last = pe.transpose(ps[:, n, j * P:(j + 1) * P], xn_tok[:, t, k * P:(k + 1) * P], ident[:, :])
                    last.then_inc(xq_turned, 1)
            pe_turn(pe, "l3")
            evacuated(pe, marks["l3"][1])
            pe.wait_ge(xq_copied, 4)
            for t in range(TT):
                if t:
                    pe.wait_ge(m_h, t)
                for j in range(2):
                    for c2_ in range(2):
                        for k in range(KC):
                            last = mm(ps[:, 2 * j + c2_, :], xq_t[:, k, t * P:(t + 1) * P],
                                      wt_l3[j][:, k, c2_ * 512:(c2_ + 1) * 512], k == 0, k == KC - 1)
                    last.then_inc(m_gu, 1)
                pe.wait_ge(m_h, TT * 0 + t + 1)
                pe.wait_ge(m_res, t) if t else None
                for k in range(8):
                    last = pe.transpose(ps[:, 4 + k // 4, (k % 4) * P:(k % 4 + 1) * P], h_tok[:, k * P:(k + 1) * P],
                                        ident[:, :])
                last.then_inc(m_ht, 1)
                pe.wait_ge(m_htc, t + 1)
                for k in range(8):
                    last = mm(ps[:, 6, 0:D], hq_t[:, k, :], wt_l3[2][:, k, :], k == 0, k == 7)
                last.then_inc(m_o, 1)

        @block.scalar
        def _(act):
            def layer_norm(name):
                L = LN[name]
                for h in range(TH):
                    n = 2 * L + h
                    act.wait_ge(ln_xc, n + 1)
                    if n:
                        act.wait_ge(ln_var, n)
                    act.activation(sq[:, :, :], xc[:, h], ACT.Square).then_inc(ln_sq, 1)
                    act.wait_ge(ln_var, n + 1)
                    act.activation(sd[:, h, :], ps[:, 5, :], ACT.Sqrt, bias=eps_col[:, :]).then_inc(ln_sd, 1)

            def ffn(s, func, scale=None):
                for h in range(TH):
                    for i in range(s["n"]):
                        u = s["u0"] + h * s["n"] + i
                        r = s["rows"][i]
                        act.wait_ge(hid_ready, u + 1)
                        if u >= 2:
                            act.wait_ge(gated, u - 1)
                        act.activation(act_buf[0:r, u % 2, :], ps[0:r, 2 * (u % 2), :], func,
                                       scale=1.0 if scale is None else scale[0:r, :]).then_inc(act_ready, 1)

            act.wait_ge(const_ready, 1)
            copy_out(act, "x", 0)
            copy_out(act, "ctx", 0)
            layer_norm("l0x")
            ffn(l0x, ACT.Silu)
            copy_out(act, "l0", 0)
            layer_norm("l0")
            ffn(l0, ACT.Silu, tern_s[:, 8:9])
            layer_norm("wkv")
            for k in range(KC):
                for j, names in enumerate((("e1", "e2"), ("e3", "e4"))):
                    for i, nm in enumerate(names):
                        n = 4 * k + 2 * j + i
                        act.wait_ge(exp_in, n + 1)
                        act.activation(wk[nm], wk[nm], ACT.Exp).then_inc(exp_out, 1)
            copy_out(act, "l1", 0)
            copy_out(act, "small", 0)
            layer_norm("l1")
            act.wait_ge(exp_in, 9)
            act.activation(rt["e"], rt["e"], ACT.Exp).then_inc(exp_out, 1)
            act.wait_ge(rt_wdt, 1)
            act.activation(rt["wdT"][0:NE, :].rearrange("p (a b) -> p a b", a=2), ps[0:NE, 1:3, :], ACT.Copy
                           ).then_inc(rt_wdt_sb, 1)
            act.wait_ge(exp_in, 10)
            act.activation(rt["fm"], rt["fm"], ACT.Exp).then_inc(exp_out, 1)
            act.wait_ge(rt_gatest, 1)
            act.activation(gates_t[0:GATES, :].rearrange("p (a b) -> p a b", a=2), ps[0:GATES, 1:3, :], ACT.Copy
                           ).then_inc(rt_gates_sb, 1)

            def copy_first(f, s):
                b = slots[s]
                act.wait_ge(moe_turn_a, f * 2 + 1)
                act.activation(b["qaT"], ps[:, 1, 0:256].rearrange("p (k n) -> p k n", k=KC), ACT.Copy)
                act.activation(b["dqa_restT"][0:PACK], ps[0:PACK, 1, 320:384], ACT.Copy)
                act.activation(b["dqaT"], ps[:, 1, 256:320], ACT.Copy).then_inc(moe_ev_act, 1)

            def copy_second(f, s):
                b = slots[s]
                act.wait_ge(moe_turn_a, f * 2 + 2)
                act.activation(b["restT"], ps[:, 1, 0:KC * PACK].rearrange("p (k n) -> p k n", k=KC), ACT.Copy)
                act.activation(b["qbT"], ps[:, 1, 256:384], ACT.Copy)
                act.activation(b["qb_restT"], ps[:, 1, 384:384 + PACK], ACT.Copy).then_inc(moe_ev_act, 1)

            def spread(f, s, h):
                n = f * 2 + h
                act.wait_ge(moe_wrm, n + 1)
                act.activation(moe["wr"][:, h, :], ps[:, 7, :], ACT.Copy).then_inc(moe_wr, 1)
                act.wait_ge(moe_srm, n + 1)
                act.activation(moe["sr"][:, h, :], ps[:, 7, :], ACT.Copy).then_inc(moe_sr, 1)

            def unit(f, s, h, final):
                n = f * 2 + h
                act.wait_ge(moe_h, n * 3 + 1)
                act.activation(moe["s"][:, 0, :], ps[:, 2, :], ACT.Silu).then_inc(moe_s, 1)
                act.wait_ge(moe_h, n * 3 + 3)
                act.activation(moe["s"][64:PACK, 1, :], ps[0:REST, 4, :], ACT.Silu).then_inc(moe_s, 1)
                if not final or h == 0:
                    spread(*((f, s, 1) if h == 0 else (f + 1, 1 - s, 0)))
                if not final:
                    (copy_first, copy_second)[h](f + 1, 1 - s)

            copy_first(0, 0)
            copy_second(0, 0)
            spread(0, 0, 0)
            with act.Fori(0, NF // 2 - 1) as pair:
                for s in range(2):
                    for h in range(TH):
                        unit(pair * 2 + s, s, h, False)
            for f in (NF - 2, NF - 1):
                for h in range(TH):
                    unit(f, f % 2, h, f == NF - 1)
            ffn(l1, ACT.Silu)

            layer_norm("l2x")
            for n in range(2 * HEADS):
                if n % 2 == 0:
                    act.wait_ge(head_turned, n + 1)
                    if n:
                        act.wait_ge(head_copied, n)
                    dst = (q_s, k_s)[n // HEADS]
                    act.activation(dst[0:3 * HD, n % HEADS, :], ps[0:3 * HD, n % 2, :].bitcast(BF16), ACT.Copy
                                   ).then_inc(head_copied, 1)
            def exponentials(t, i):
                act.wait_ge(att_bias, t * HEADS + (i + 1))
                if not (isinstance(t, int) and t * HEADS + i < 2):
                    act.wait_ge(att_round, t * HEADS + (i - 1))
                t, i = t + i // HEADS, i % HEADS
                act.activation(att_e[:, i % 2, :].rearrange("p (a b) -> p a b", a=2),
                               ps[:, 2 * (i % 2):2 * (i % 2) + 2, :], ACT.Exp,
                               bias=att_small["bias"][:, i % 2:i % 2 + 1],
                               scale=att_small["sq"][:, bass.ds(t, 1), i],
                               accum_out=att_small["z"][:, bass.ds(t, 1), i]).then_inc(att_exp, 1)

            def probs_copy(t, j):
                act.wait_ge(att_t, t * HEADS + (j + 1))
                act.activation(att_pt[:, j % 4].rearrange("p a b -> p (a b)"),
                               ps[:, 4 + j % 2, :].bitcast(BF16), ACT.Copy).then_inc(att_copied, 1)

            def query_tile(t, final):
                for i in range(4, HEADS + 2 if final else HEADS + 4):
                    if i < HEADS or not final:
                        exponentials(t, i)
                    probs_copy(t, i - 2)

            exponentials(0, 0)
            exponentials(0, 1)
            exponentials(0, 2)
            probs_copy(0, 0)
            exponentials(0, 3)
            probs_copy(0, 1)
            with act.Fori(0, TT - 1) as t:
                query_tile(t, False)
            query_tile(TT - 1, True)
            copy_out(act, "l2", 0)
            layer_norm("l2")
            ffn(l2, ACT.Sigmoid)
            copy_out(act, "lx", 0)
            layer_norm("l3x")
            for t in range(TT):
                act.wait_ge(lx_kv, 2 * t + 2)
                act.activation(v1[:, t, :, 0:P], ps[:, 2 + t % 2, 0:D].rearrange("p (m n) -> p m n", m=KC), ACT.Copy
                               ).then_inc(lx_v, 1)
                act.wait_ge(lx_min_r, t + 1)
                if t >= 2:
                    act.wait_ge(lx_kf, t - 1)
                act.activation(lx_exp[:, t % 2, :], lx_min[:, t % 2, :], ACT.Exp).then_inc(lx_exp_r, 1)
            for h in range(TH):
                act.wait_ge(lx_qmin_r, h + 1)
                act.activation(lx_qmin, lx_qmin, ACT.Exp).then_inc(lx_act, 1)
                act.wait_ge(lx_qg, 2 * h + 2)
                if h:
                    act.wait_ge(lx_or, h)
                for o in range(KC):
                    last = act.activation(lx_gate[:, o, :], ps[:, 2 + o, :], ACT.Sigmoid, bias=bg[:, o:o + 1])
                    last.then_inc(lx_act, 1)
            layer_norm("l3")
            copy_out(act, "l3", 0)
            for t in range(TT):
                act.wait_ge(m_gu, 2 * t + 1)
                if t:
                    act.wait_ge(m_ht, t)
                act.activation(h_act.rearrange("p (a b) -> p a b", a=2), ps[:, 0:2, :], ACT.Silu).then_inc(m_act, 1)
                act.wait_ge(m_ht, t + 1)
                if t:
                    act.wait_ge(m_o, t)
                act.activation(hq_t.rearrange("p a b -> p (a b)").rearrange("p (a b) -> p a b", a=2), ps[:, 4:6, :],
                               ACT.Copy).then_inc(m_htc, 1)

        @block.vector
        def _(dve):
            made = 0

            def step(ins):
                nonlocal made
                made += 1
                ins.then_inc(dve_step, 1)
                dve.wait_ge(dve_step, made)

            TS, TTN, STT = dve.tensor_scalar, dve.tensor_tensor, dve.scalar_tensor_tensor

            def layer_norm(name):
                L = LN[name]
                for h in range(TH):
                    n = 2 * L + h
                    dve.wait_ge(ln_mean, n + 1)
                    TTN(xc[:, h], x_t[:, :, tok(h)], ps[:, 4:5, :].to_broadcast([P, KC, HALF]), ALU.subtract
                        ).then_inc(ln_xc, 1)
                for h in range(TH):
                    n = 2 * L + h
                    dve.wait_ge(ln_sd, n + 1)
                    step(dve.reciprocal(sd[:, h, :], sd[:, h, :]))
                    TTN(xn_t[:, :, tok(h)], xc[:, h], sd[:, h:h + 1, :].to_broadcast([P, KC, HALF]), ALU.mult
                        ).then_inc(xn_ready, 1)

            def add_y(h, scalar=None):
                y = ps[:, 4:6, :]
                if scalar is None:
                    return TTN(x_t[:, :, tok(h)], y, x_t[:, :, tok(h)], ALU.add)
                return STT(x_t[:, :, tok(h)], y, scalar, x_t[:, :, tok(h)], ALU.mult, ALU.add)

            def ffn(s, gate, y_scale=None):
                for h in range(TH):
                    for i in range(s["n"]):
                        u = s["u0"] + h * s["n"] + i
                        r = s["rows"][i]
                        dve.wait_ge(act_ready, u + 1)
                        if u >= 2:
                            dve.wait_ge(hid_used, u - 1)
                        gate(h, i, r, act_buf[0:r, u % 2, :], ps[0:r, 2 * (u % 2), :], ps[0:r, 2 * (u % 2) + 1, :],
                             hid_buf[0:r, u % 2, :]).then_inc(gated, 1)
                    dve.wait_ge(hid_used, s["u0"] + (h + 1) * s["n"])
                    add_y(h, y_scale).then_inc(x_ready, 1)

            def ternary(ws, h, tmp, st, wait, use_scale):
                dve.wait_ge(*wait)
                full = h // P
                parts = [(ws[i][:, 0:full, :], P, 2 * i) for i in range(2)]
                parts += [(ws[i][0:h % P, full, :], h % P, 2 * i + 1) for i in range(2)]
                parts += [(ws[2], P, 4)]
                step(dve.memset(st, 0.0))
                for w, r, col in parts:
                    last = dve.tensor_reduce(st[0:r, col:col + 1], w, AX.XY if len(w.shape) == 3 else AX.X, ALU.add,
                                             apply_absolute_value=True)
                    step(last)
                dve.sem_inc(tern_part, 1)
                dve.wait_ge(tern_sum, 1 if use_scale else 2)
                step(dve.tensor_reduce(st[:, 8:11], ps[:, 4, 0:6].rearrange("p (a b) -> p a b", b=2), AX.X, ALU.add))
                step(TS(st[:, 8:11], st[:, 8:11], 1.0 / (h * D), None, ALU.mult))
                if not use_scale:
                    step(TS(st[:, 8:11], st[:, 8:11], 1e-8, None, ALU.add))
                step(TS(st[:, 12:15], st[:, 8:11], 0.5, None, ALU.mult))
                step(TS(st[:, 16:19], st[:, 8:11], -0.5, None, ALU.mult))
                step(TTN(st[:, 20:21], st[:, 9:10], st[:, 10:11], ALU.mult))
                for w, r, col in parts:
                    i = col // 2
                    t = tmp[0:r, 0:w.free_size() if callable(w.free_size) else w.free_size]
                    if len(w.shape) == 3:
                        t = t.rearrange("p (a b) -> p a b", a=w.shape[1])
                    step(TS(t, w, st[0:r, 16 + i:17 + i], None, ALU.is_lt))
                    step(STT(w, w, st[0:r, 12 + i:13 + i], t, ALU.is_gt, ALU.subtract))
                dve.sem_inc(weights_fixed, 1)

            copy_out(dve, "x", 1)
            copy_out(dve, "ctx", 1)
            dve.wait_ge(evac_act, 2)
            dve.wait_ge(evac_dve, 2)
            dve.sem_inc(x_ready, 2)
            dve.wait_ge(load["tid"], 16)
            for e in range(1, 4):
                step(TS(ge_mask[:, e - 1, :], tid, float(e * TOKENS_PER_EXPERT), None, ALU.is_ge))
            step(TS(tok_mask[:, 0, :], ge_mask[:, 0, :], -1.0, 1.0, ALU.mult, ALU.add))
            step(TTN(tok_mask[:, 1, :], ge_mask[:, 0, :], ge_mask[:, 1, :], ALU.subtract))
            step(TTN(tok_mask[:, 2, :], ge_mask[:, 1, :], ge_mask[:, 2, :], ALU.subtract))
            step(dve.tensor_copy(tok_mask[:, 3, :], ge_mask[:, 2, :]))
            layer_norm("l0x")

            def gate_l0x(h, i, r, s, ga, up, hid):
                step(TTN(hid, ga, s, ALU.mult))
                return TTN(hid, hid, tok_mask[:, i // KC, tok(h)], ALU.mult)
            ffn(l0x, gate_l0x)
            ternary(w_l0, H0, tern_tmp, tern_s, (load["l0"], 16 * 5), True)
            copy_out(dve, "l0", 1)
            layer_norm("l0")

            def gate_l0(h, i, r, s, ga, up, hid):
                return STT(hid, up, tern_s[0:r, 20:21], s, ALU.mult, ALU.mult)
            ffn(l0, gate_l0)

            layer_norm("wkv")
            dve.wait_ge(load["wku"], 32)
            W = wk
            for k in range(KC):
                kk = xn_t[:, k, :].rearrange("p (b s) -> p b s", b=BATCH)
                vv = ctx_t[:, k, :].rearrange("p (b s) -> p b s", b=BATCH)
                xx = x_t[:, k, :].rearrange("p (b s) -> p b s", b=BATCH)
                w, u = W["w"][:, k:k + 1], W["u"][:, k:k + 1]
                o0, o1 = W["o"][:, :, 0:SEQ], W["o"][:, :, 1:SEQ + 1]
                p0, q0 = W["p"][:, :, 0:SEQ], W["q"][:, :, 0:SEQ]
                step(dve.memset(W["wb"], 0.0))
                step(TS(W["wb"], W["wb"], w, None, ALU.add))
                step(dve.memset(W["o"][:, :, 0:1], -1e38))
                step(dve.memset(W["p"][:, :, 0:1], 0.0))
                step(dve.memset(W["q"][:, :, 0:1], 0.0))
                for b in range(BATCH):
                    step(dve.tensor_tensor_scan(o1[:, b, :], W["wb"], kk[:, b, :], -1e38, ALU.add, ALU.max))
                TTN(W["e2"], kk, o1, ALU.subtract).then_inc(dve_step, 1)
                made += 1
                dve.wait_ge(dve_step, made)
                step(STT(W["e1"], o0, w, o1, ALU.add, ALU.subtract))
                dve.sem_inc(exp_in, 2)
                step(STT(W["no"], kk, u, o0, ALU.add, ALU.max))
                step(TTN(W["e3"], o0, W["no"], ALU.subtract))
                step(STT(W["e4"], kk, u, W["no"], ALU.add, ALU.subtract))
                dve.sem_inc(exp_in, 2)
                dve.wait_ge(exp_out, 4 * k + 2)
                step(TTN(W["ev"], W["e2"], vv, ALU.mult))
                for b in range(BATCH):
                    step(dve.tensor_tensor_scan(W["p"][:, b, 1:], W["e1"][:, b, :], W["ev"][:, b, :], 0.0,
                                                ALU.mult, ALU.add))
                    step(dve.tensor_tensor_scan(W["q"][:, b, 1:], W["e1"][:, b, :], W["e2"][:, b, :], 0.0,
                                                ALU.mult, ALU.add))
                dve.wait_ge(exp_out, 4 * k + 4)
                step(TTN(W["num"], W["e3"], p0, ALU.mult))
                step(TTN(W["den"], W["e3"], q0, ALU.mult))
                step(TTN(W["ev"], W["e4"], vv, ALU.mult))
                step(TTN(W["num"], W["num"], W["ev"], ALU.add))
                step(TTN(W["den"], W["den"], W["e4"], ALU.add))
                step(dve.reciprocal(W["den"], W["den"]))
                step(TTN(W["num"], W["num"], W["den"], ALU.mult))
                TTN(xx, xx, W["num"], ALU.add).then_inc(x_ready, 1)
            copy_out(dve, "l1", 1)
            copy_out(dve, "small", 1)
            layer_norm("l1")

            dve.wait_ge(load["inv"], 16)
            iv = inv_f[0:NE]
            step(dve.tensor_copy(iv[:, 0, :], inv_row[0:NE]))
            step(TS(iv[:, 1, :], iv[:, 0, :], 0.0, float(NE), ALU.is_lt, ALU.mult))
            step(TTN(iv[:, 0, :], iv[:, 0, :], iv[:, 1, :], ALU.add))
            step(TS(iv[:, 2, :], iv[:, 0, :], 0.0, float(NE - 1), ALU.max, ALU.min))
            dve.wait_ge(const_ready, 1)
            step(TS(esel[0:NE, :], iv[:, 2, :], e_col[0:NE, :], None, ALU.is_equal))
            dve.wait_ge(rt_logits, 1)
            lg = ps[:, 0, :].rearrange("p (t e) -> p t e", e=NE)
            R = rt

            def b3(v, n):
                return v.unsqueeze(2).to_broadcast([P, v.shape[1], n])
            step(dve.tensor_reduce(R["mx"], lg, AX.X, ALU.max))
            step(TTN(R["e"], lg, b3(R["mx"], NE), ALU.subtract))
            dve.sem_inc(exp_in, 1)
            dve.wait_ge(exp_out, 9)
            step(dve.tensor_reduce(R["sum"], R["e"], AX.X, ALU.add))
            step(dve.reciprocal(R["sum"], R["sum"]))
            step(TTN(R["sc"][:, :, 0:NE], R["e"], b3(R["sum"], NE), ALU.mult))
            step(dve.memset(R["sc"][:, :, NE:NE + 2], -1.0))
            for t in range(TT):
                step(dve.max(R["top"][:, t, :], R["sc"][:, t, 0:NE]))
            step(dve.memset(R["top"][:, :, TOP:8], -1.0))
            for t in range(TT):
                step(dve.match_replace(R["mr"][:, t, :], R["top"][:, t, :], R["sc"][:, t, :], -2.0))
            STT(R["wd"], R["mr"][:, :, 0:NE], -2.0, R["sc"][:, :, 0:NE], ALU.is_equal, ALU.mult).then_inc(rt_wd, 1)
            dve.wait_ge(rt_flat, 1)
            fl, fm = (R[n].rearrange("p t (f k) -> p (t f) k", k=NK) for n in ("fl", "fm"))
            step(dve.tensor_copy(R["fl"], ps[:, 3, :].rearrange("p (t e) -> p t e", e=NE)))
            step(dve.tensor_reduce(R["gt"][:, :, NE:GATES], R["fl"].rearrange("p t (f k) -> p t f k", k=NK), AX.X, ALU.add))
            step(TS(R["fm"], R["fl"], 0.0, -1e9, ALU.is_equal, ALU.mult))
            step(TTN(R["fm"], R["fm"], R["fl"], ALU.add))
            step(dve.tensor_reduce(R["gmx"], fm, AX.X, ALU.max))
            step(TTN(fm, fm, b3(R["gmx"], NK), ALU.subtract))
            dve.sem_inc(exp_in, 1)
            dve.wait_ge(exp_out, 10)
            step(dve.tensor_reduce(R["gmx"], fm, AX.X, ALU.add))
            step(dve.reciprocal(R["gmx"], R["gmx"]))
            TTN(R["gt"][:, :, 0:NE].rearrange("p t (f k) -> p t f k", k=NK),
                R["fm"].rearrange("p t (f k) -> p t f k", k=NK),
                R["gmx"].rearrange("p (t f) -> p t f", f=NF).unsqueeze(3).to_broadcast([P, TT, NF, NK]),
                ALU.mult).then_inc(rt_gt, 1)
            dve.wait_ge(rt_gates_sb, 1)

            def scale_and_mask(f, s, round_):
                b = slots[s]
                dve.wait_ge(load[f"moe{s}"], round_ * SLOT_LOADED + SLOT_LOADED)
                for j in range(2):
                    v = b["qb"][:, 64 * j:64 * j + 64]
                    TS(v, v, b["s_main"][:, j:j + 1], None, ALU.mult)
                v = b["qb_rest"][0:PACK]
                TS(v, v, b["s_rest"][0:PACK], None, ALU.mult)
                v = b["d"][:, :, 0:64]
                TTN(v, v, b["s_down"].unsqueeze(2).to_broadcast([P, KC, 64]), ALU.mult).then_inc(moe_fixed, 1)
                TS(gates_f[s][0:GATES, :], gates_t[0:GATES, :], group_mask[0:GATES, bass.ds(f, 1)], None, ALU.mult
                   ).then_inc(moe_masked, 1)

            def copy_first(f, s):
                dve.wait_ge(moe_turn_d, f * 2 + 1)
                dve.tensor_copy(slots[s]["mainT"].rearrange("p a k n -> p (a k n)"), ps[:, 3, :]
                                ).then_inc(moe_ev_dve, 1)

            def copy_second(f, s):
                dve.wait_ge(moe_turn_d, f * 2 + 2)
                dve.tensor_copy(slots[s]["dT"], ps[:, 3, 0:256])
                dve.tensor_copy(slots[s]["packT"][0:PACK], ps[0:PACK, 3, 256:512]).then_inc(moe_ev_dve, 1)

            def corrected(f, s, h):
                dve.wait_ge(moe_mu, f * 2 + (h + 1))
                TTN(moe["xe"][:, h], ps[:, 0:2, :], xn_t[:, :, tok(h)], ALU.add).then_inc(moe_xe, 1)

            def weighted_codes(f, s, h):
                n = f * 2 + h
                dve.wait_ge(moe_a, n + 1)
                dve.wait_ge(moe_wr, n + 1)
                TTN(moe["aw"], ps[:, 0, :], moe["wr"][:, h, :], ALU.mult).then_inc(moe_aw, 1)

            def unit(f, s, h, final, round_):
                n = f * 2 + h
                M = moe
                dve.wait_ge(moe_s, n * 2 + 1)
                dve.wait_ge(moe_sr, n + 1)
                TTN(M["s"][:, 0, :], M["s"][:, 0, :], M["sr"][:, h, :], ALU.mult).then_inc(moe_sm, 1)
                dve.wait_ge(moe_sm, n * 2 + 1)
                dve.wait_ge(moe_h, n * 3 + 2)
                TTN(M["h"], ps[:, 3, :], M["s"][:, 0, :], ALU.mult).then_inc(moe_hg, 1)
                v = M["s"][64:PACK, 1, :]
                dve.wait_ge(moe_s, n * 2 + 2)
                TTN(v, v, M["sr"][64:PACK, h, :], ALU.mult).then_inc(moe_sm, 1)
                dve.wait_ge(moe_sm, n * 2 + 2)
                TTN(M["pack"][64:PACK, :], ps[64:PACK, 4, :], v, ALU.mult).then_inc(moe_hg, 1)
                ahead = (f, s, 1) if h == 0 else (f + 1, 1 - s, 0)
                if not final or h == 0:
                    corrected(*ahead)
                dve.wait_ge(moe_ad, n + 1)
                TTN(M["pack"][0:64, :], ps[0:64, 2, :], M["wr"][0:64, h, :], ALU.mult).then_inc(moe_awd, 1)
                if not final or h == 0:
                    weighted_codes(*ahead)
                if not final:
                    (copy_first, copy_second)[h](f + 1, 1 - s)
                dve.wait_ge(moe_y, n + 1)
                TTN(x_t[:, :, tok(h)], ps[:, 5:7, :], x_t[:, :, tok(h)], ALU.add).then_inc(moe_x, 1)
                if h == 1 and round_ is not None:
                    scale_and_mask(f + 2, s, round_)

            dve.sem_inc(moe_x, 1)
            scale_and_mask(0, 0, 0)
            copy_first(0, 0)
            copy_second(0, 0)
            scale_and_mask(1, 1, 0)
            corrected(0, 0, 0)
            weighted_codes(0, 0, 0)
            with dve.Fori(0, NF // 2 - 1) as pair:
                for s in range(2):
                    for h in range(TH):
                        unit(pair * 2 + s, s, h, False, pair + 1)
            for f in (NF - 2, NF - 1):
                for h in range(TH):
                    unit(f, f % 2, h, f == NF - 1, None)

            def gate_std(h, i, r, s, ga, up, hid):
                return TTN(hid, up, s, ALU.mult)
            dve.wait_ge(moe_x, 2 * NF + 1)
            ffn(l1, gate_std)

            layer_norm("l2x")
            A = att_small
            for t in range(TT):
                for j in range(2):
                    n = 2 * t + j
                    dve.wait_ge(pj_ready, n + 1)
                    if j:
                        dve.tensor_copy(k_tok[:, t, :], ps[:, n % 4, 0:D]).then_inc(pj_used, 1)
                    else:
                        TS(q_tok[:, t, :], ps[:, n % 4, 0:D], 1.0 / math.sqrt(HD), None, ALU.mult
                           ).then_inc(pj_used, 1)
            for h in range(TH):
                for o in range(KC):
                    dve.wait_ge(v_ready, 2 * h + o + 1)
                    step(TS(v_t[:, o, tok(h)], ps[:, 4 + 2 * h + o, :], A["bvp"][:, o:o + 1], None, ALU.add))
            step(dve.tensor_reduce(A["vmax"], v_t, AX.X, ALU.max, apply_absolute_value=True))
            step(TS(A["sv"], A["vmax"], 1.0 / 127.0, 1e-8, ALU.mult, ALU.max))
            step(dve.reciprocal(A["vinv"], A["sv"]))
            for o in range(KC):
                step(TS(v_t[:, o, :], v_t[:, o, :], A["vinv"][:, o:o + 1], ROUND, ALU.mult, ALU.add))
            TS(vn_t, v_t, ROUND, None, ALU.subtract).then_inc(vn_ready, 1)
            dve.wait_ge(vn_ready, 1)
            dve.wait_ge(pj_used, 2 * TT)
            for j, (src, s_, three_) in enumerate(((q_tok, A["sq"].rearrange("p t h -> p (t h)"), q3),
                                                   (k_tok, A["sk"], k3))):
                v = src.rearrange("p t (h d) -> p (t h) d", d=HD)
                tmp = q_tmp.rearrange("p t (h d) -> p (t h) d", d=HD)
                o = three_.rearrange("p t h c d -> p (t h) c d")
                step(dve.tensor_reduce(A["amax"], v, AX.X, ALU.max, apply_absolute_value=True))
                step(TS(s_, A["amax"], 1.0 / 127.0, 1e-8, ALU.mult, ALU.max))
                step(dve.reciprocal(A["inv"], s_))
                step(TTN(tmp, v, b3(A["inv"], HD), ALU.mult))
                if j == 0:
                    step(TS(tmp, tmp, ROUND, None, ALU.add))
                    for c_ in range(3):
                        last = TS(o[:, :, c_, :], tmp, ROUND, None, ALU.subtract)
                    last.then_inc(qk_split, 1)
                    dve.wait_ge(qk_split, 1)
                else:
                    step(TS(tmp, tmp, ROUND, ROUND, ALU.add, ALU.subtract))
                    step(TTN(tmp, tmp, b3(s_, HD), ALU.mult))
                    step(dve.tensor_copy(o[:, :, 0, :], tmp))
                    step(TTN(tmp, tmp, o[:, :, 0, :], ALU.subtract))
                    step(dve.tensor_copy(o[:, :, 1, :], tmp))
                    TTN(o[:, :, 2, :], tmp, o[:, :, 1, :], ALU.subtract).then_inc(qk_split, 1)
            for n in range(2 * HEADS):
                if n % 2:
                    dve.wait_ge(head_turned, n + 1)
                    dve.wait_ge(head_copied, n)
                    dst = (q_s, k_s)[n // HEADS]
                    dve.tensor_copy(dst[0:3 * HD, n % HEADS, :], ps[0:3 * HD, n % 2, :].bitcast(BF16)
                                    ).then_inc(head_copied, 1)
            for k in range(KC):
                dve.wait_ge(vn_turned, k + 1)
                dve.tensor_copy(v_tok[:, :, k * P:(k + 1) * P],
                                ps[:, 2 + k, :].bitcast(BF16).rearrange("p (t d) -> p t d", t=TT)).then_inc(v_copied, 1)
            def row_bias(t, i):
                n, b = t * HEADS + (i + 1), i % 2
                dve.wait_ge(att_s, n)
                dve.tensor_reduce(A["nm"][:, b:b + 1], ps[:, 2 * b:2 * b + 2, :], AX.XY, ALU.max, negate=True
                                  ).then_inc(att_max, 1)
                dve.wait_ge(att_max, n)
                TS(A["bias"][:, b:b + 1], A["nm"][:, b:b + 1], A["sq"][:, bass.ds(t + i // HEADS, 1), i % HEADS],
                   math.log(255.0), ALU.mult, ALU.add).then_inc(att_bias, 1)

            def rounding(t, j):
                dve.wait_ge(att_exp, t * HEADS + (j + 1))
                if not (isinstance(t, int) and t * HEADS + j < 2):
                    dve.wait_ge(att_t, t * HEADS + (j - 1))
                TS(att_p[:, j % 2, :], att_e[:, j % 2, :], ROUND, ROUND, ALU.add, ALU.subtract).then_inc(att_round, 1)

            def query_tile(t, final):
                for i in range(4, HEADS + 4):
                    if i < HEADS or not final:
                        row_bias(t, i)
                    if i - 1 < HEADS or not final:
                        rounding(t, i - 1)
                dve.wait_ge(att_o, t + 1)
                dve.reciprocal(A["rz"], A["z"][:, bass.ds(t, 1), :].rearrange("p a h -> p (a h)")).then_inc(att_rz, 1)
                dve.wait_ge(att_rz, t + 1)
                TTN(o_tok[:, bass.ds(t, 1), :].rearrange("p a (h d) -> p (a h) d", d=HD),
                    ps[:, 6, 0:D].rearrange("p (h d) -> p h d", d=HD), b3(A["rz"], HD), ALU.mult
                    ).then_inc(att_o_used, 1)

            dve.sem_inc(att_o_used, 1)
            row_bias(0, 0)
            row_bias(0, 1)
            rounding(0, 0)
            row_bias(0, 2)
            rounding(0, 1)
            row_bias(0, 3)
            rounding(0, 2)
            with dve.Fori(0, TT - 1) as t:
                query_tile(t, False)
            query_tile(TT - 1, True)
            for n in range(4):
                h, k = divmod(n, 2)
                dve.wait_ge(ot_turned, n + 1)
                TS(o_t[:, k, tok(h)], ps[:, n, :], A["sv"][:, k:k + 1], None, ALU.mult).then_inc(ot_copied, 1)
            for h in range(TH):
                dve.wait_ge(att_done, h + 1)
                for o in range(KC):
                    last = STT(x_t[:, o, tok(h)], ps[:, 4 + 2 * h + o, :], A["bpp"][:, o:o + 1], x_t[:, o, tok(h)],
                               ALU.add, ALU.add)
                    if o == 0:
                        step(last)
                last.then_inc(x_ready, 1)

            ternary(w_l2, H2, tern_tmp2, tern_s2, (load["l2"], 16 * 5), False)
            copy_out(dve, "l2", 1)
            layer_norm("l2")
            ffn(l2, gate_std)

            copy_out(dve, "lx", 1)
            layer_norm("l3x")
            step(dve.memset(v1[:, :, :, P:P + 1], 1.0))
            for t in range(TT):
                dve.wait_ge(lx_kv, 2 * t + 1)
                if t >= 2:
                    dve.wait_ge(lx_exp_r, t - 1)
                TS(lx_min[:, t % 2, :], ps[:, t % 2, 0:D], 0.0, None, ALU.min).then_inc(lx_min_r, 1)
                dve.wait_ge(lx_exp_r, t + 1)
                STT(kf[:, t, :], ps[:, t % 2, 0:D], 0.0, lx_exp[:, t % 2, :], ALU.max, ALU.add).then_inc(lx_kf, 1)
            for b in range(BATCH):
                dve.wait_ge(lx_sum, b + 1)
                for m in range(KC):
                    c0 = m * (P + 1)
                    step(TTN(bd[:, b, m, :], ps[:, b, c0:c0 + P], head_mask[:, :], ALU.mult))
                    step(TS(dd[:, b, m, :], head_mask[:, :], ps[:, b, c0 + P:c0 + P + 1], None, ALU.mult))
            dve.sem_inc(lx_bd, 1)
            for h in range(TH):
                dve.wait_ge(lx_qg, 2 * h + 1)
                TS(lx_qmin, ps[:, 0:2, :], 0.0, None, ALU.min).then_inc(lx_qmin_r, 1)
                dve.wait_ge(lx_act, 3 * h + 1)
                STT(lx_q, ps[:, 0:2, :], 0.0, lx_qmin, ALU.max, ALU.add).then_inc(lx_qf, 1)
                dve.wait_ge(lx_att, h + 1)
                step(TS(lx_den, ps[:, 6:8, :], 1e-6, None, ALU.add))
                step(dve.reciprocal(lx_den, lx_den))
                step(TTN(lx_den, ps[:, 4:6, :], lx_den, ALU.mult))
                dve.wait_ge(lx_act, 3 * h + 3)
                TTN(lx_o, lx_den, lx_gate, ALU.mult).then_inc(lx_or, 1)
                dve.wait_ge(y_ready, h + 1)
                TTN(x_t[:, :, tok(h)], ps[:, 0:2, :], x_t[:, :, tok(h)], ALU.add).then_inc(x_ready, 1)

            def mx_quant(v, q, s, n):
                qf = q.rearrange("p (a b) -> p a b", b=MX_BLOCK)
                sc_ = s[:, 0:n]
                step(dve.tensor_reduce(sc_, v, AX.X, ALU.max, apply_absolute_value=True))
                step(TS(sc_, sc_, 1.0 / MX_MAX, 1e-30, ALU.mult, ALU.max))
                step(dve.reciprocal(s2[:, 0:n], sc_))
                step(TTN(v, v, b3(s2[:, 0:n], MX_BLOCK), ALU.mult))
                step(TS(q.bitcast(I32), v.rearrange("p a b -> p (a b)").bitcast(I32), 0x7F800000, None,
                        ALU.bitwise_and))
                step(TS(qf, qf, 2.0 ** -6, 1.5 * 2.0 ** 20, ALU.max, ALU.mult))
                step(TTN(v, v, qf, ALU.add))
                step(TTN(v, v, qf, ALU.subtract))
                return TTN(v, v, b3(sc_, MX_BLOCK), ALU.mult)
            s2 = mx_s[2]
            layer_norm("l3")
            for n in range(8):
                h, k = divmod(n % 4, 2)
                dve.wait_ge(xt_turned, n + 1)
                dst = (xn_tok, x_tok)[n // 4]
                dve.tensor_copy(dst[:, 4 * h:4 * h + 4, k * P:(k + 1) * P],
                                ps[:, n % 4, :].rearrange("p (t d) -> p t d", t=4)).then_inc(xt_copied, 1)
            dve.wait_ge(xt_copied, 8)
            mx_quant(xn_tok.rearrange("p t (a b) -> p (t a) b", b=MX_BLOCK), mxq[0], mx_s[0], 64).then_inc(xq_ready, 1)
            for n in range(4):
                h, k = divmod(n, 2)
                dve.wait_ge(xq_turned, n + 1)
                dve.tensor_copy(xq_t[:, k, tok(h)], ps[:, n, :]).then_inc(xq_copied, 1)
            dve.wait_ge(load["l3"], 16 * 3)
            for i in range(3):
                v = w_l3[i].rearrange("p c (a b) -> p (c a) b", b=MX_BLOCK)
                ins = mx_quant(v, mxq[0], mx_s[0], 64)
                if i < 2:
                    step(ins)
            ins.then_inc(weights_fixed, 1)
            copy_out(dve, "l3", 1)
            for t in range(TT):
                dve.wait_ge(m_act, t + 1)
                dve.wait_ge(m_gu, 2 * t + 2)
                if t:
                    dve.wait_ge(m_ht, t)
                step(TTN(h_tok.rearrange("p (a b) -> p a b", a=2), ps[:, 2:4, :],
                         h_act.rearrange("p (a b) -> p a b", a=2), ALU.mult))
                mx_quant(h_tok.rearrange("p (a b) -> p a b", b=MX_BLOCK), mxq[0][:, 0:H3], mx_s[0], 32
                         ).then_inc(m_h, 1)
                dve.wait_ge(m_o, t + 1)
                if t >= 2:
                    dve.wait_ge(stored[t % 2], 16 * (t // 2))
                TTN(res[:, t % 2, :], ps[:, 6, 0:D], x_tok[:, t, :], ALU.add).then_inc(m_res, 1)


_INS = ['x', 'itok_BxS_13_99985', 'ctx_2048', 'L0_ffn_w1', 'L0_ffn_w3', 'L0_ffn_w2', 'L1_xattn_w', 'L1_xattn_u',
        'L1_ffn_gate_weight', 'L1_ffn_inv_mapping', 'L1_ffn_mask_up_W', 'L1_ffn_gate_W', 'L1_ffn_gate_qa',
        'L1_ffn_gate_qb', 'L1_ffn_gate_scale', 'L1_ffn_up_W', 'L1_ffn_up_qa', 'L1_ffn_up_qb', 'L1_ffn_up_scale',
        'L1_ffn_down_W', 'L1_ffn_down_qa', 'L1_ffn_down_qb', 'L1_ffn_down_scale', 'L1_ffn_sh_gate_W',
        'L1_ffn_sh_up_W', 'L1_ffn_sh_down_W', 'L2_xattn_Wq', 'L2_xattn_bq', 'L2_xattn_Wkv', 'L2_xattn_bkv',
        'L2_xattn_Wp', 'L2_xattn_bp', 'L2_ffn_w1', 'L2_ffn_w2', 'L2_ffn_w3', 'L3_xattn_Wq', 'L3_xattn_Wg',
        'L3_xattn_bg', 'L3_xattn_Wkv', 'L3_xattn_Wo', 'L3_ffn_gate_w', 'L3_ffn_up_w', 'L3_ffn_down_w']


def kernel(**inputs):
    import numpy as _np
    import concourse.bacc as _bacc
    from concourse import mybir as _mybir
    from concourse.bass_utils import run_bass_kernel_spmd as _run

    nc = _bacc.Bacc("TRN2", target_bir_lowering=False, num_devices=1)
    arrays, args = {}, {}
    for name in _INS:
        v = _np.ascontiguousarray(inputs[name])
        arrays[f"in_{name}"] = v
        args[name] = nc.dram_tensor(f"in_{name}", v.shape, _mybir.dt.from_np(v.dtype), kind="ExternalInput").ap()
    out = nc.dram_tensor("out_0", (BATCH, SEQ, D), F32, kind="ExternalOutput").ap()
    build(nc, args, out)
    r = _run(nc, [arrays], core_ids=[0])
    return r.results[0]["out_0"]
```

```python
from contextlib import ExitStack
import math

import concourse.bass as bass
from concourse import mybir

ALU = mybir.AluOpType
ACT = mybir.ActivationFunctionType
AX = mybir.AxisListType
F32 = mybir.dt.float32
BF16 = mybir.dt.bfloat16
I32 = mybir.dt.int32
F32R = mybir.dt.float32r

P = 128
D = 256
KC = D // P
BATCH = 4
SEQ = 256
TOK = BATCH * SEQ
TT = TOK // P
HALF = 512
TH = TOK // HALF

TOKENS_PER_EXPERT = 12500 // 4
NF = 8
NK = 8
NR = 8
NE = NF * NK
TOP = 6
INNER = 176
REST = INNER - P
PACK = 64 + REST
GATES = NE + NF
SLOT_LOADED = 16 * 21
HEADS = 16
HD = D // HEADS
ROUND = 1.5 * 2.0 ** 23
MX_BLOCK = 32
MX_MAX = 448.0
LN_EPS = 1e-5
ARENA = 157
SPLIT = dict(l0=0, l2=1)
TERN_SUM = 6


def chunks(n):
    return [(a, min(P, n - a)) for a in range(0, n, P)]


def build(nc, a, out):
    H0 = a["L0_ffn_w1"].shape[0]
    H1 = a["L1_ffn_sh_gate_W"].shape[0]
    H2 = a["L2_ffn_w1"].shape[0]
    H3 = a["L3_ffn_gate_w"].shape[0]

    with ExitStack() as ctx:
        def sb(name, shape, dt=F32):
            return ctx.enter_context(nc.sbuf_tensor(name, shape, dt))

        def sem(name):
            return ctx.enter_context(nc.semaphore(name))

        ps = ctx.enter_context(nc.psum_tensor("ps", [P, 8, 512], F32))
        x_t = sb("x_t", [P, KC, TOK])
        xn_t = sb("xn_t", [P, KC, TOK])
        xc = sb("xc", [P, TH, KC, HALF])
        sq = sb("sq", [P, KC, HALF])
        sd = sb("sd", [P, TH, 4])
        rsd = sb("rsd", [P, TH, 4])
        rsd_diag = sb("rsd_diag", [P, 4, P])
        ctx_t = sb("ctx_t", [P, KC, TOK])
        act_buf = sb("act_buf", [P, 2, HALF])
        hid_buf = sb("hid_buf", [P, 2, HALF])
        ident = sb("ident", [P, P])
        ident_b = sb("ident_b", [P, P], BF16)
        ones = sb("ones", [P, P])
        mean_w = sb("mean_w", [P, P])
        head_mask = sb("head_mask", [P, P])
        eps_col = sb("eps_col", [P, 1])

        with nc.sbuf_tensor("arena", [P, ARENA * 256], F32) as arena:
            pass
        split_names = []

        def over_arena(words, at):
            name = f"arena_split{len(split_names)}"
            split_names.append(name)
            with ExitStack() as place:
                if at:
                    place.enter_context(nc.sbuf_tensor(name + "_before", [P, at], F32))
                return place.enter_context(nc.sbuf_tensor(name, [P, words], F32R))

        class Cut:
            def __init__(self, kb):
                self.at = int(kb * 256)

            def __call__(self, shape, dt=F32, parts=P):
                n = 1
                for s in shape:
                    n *= s
                words = n if dt in (F32, I32, F32R) else (n + 1) // 2
                if dt == F32R:
                    self.at = -(-self.at // 8) * 8
                    words = -(-words // 8) * 8
                    v = over_arena(words, self.at)[0:parts, 0:n]
                else:
                    v = arena[0:parts, self.at:self.at + words]
                self.at += words
                assert self.at <= ARENA * 256, self.at / 256
                if dt not in (F32, F32R):
                    v = v.bitcast(dt)
                if len(shape) > 1:
                    names = "abcd"[:len(shape)]
                    v = v.rearrange(f"p ({' '.join(names)}) -> p {' '.join(names)}",
                                    **{c: s for c, s in zip(names[1:], shape[1:])})
                return v

        c = Cut(0)
        ctx_nat = c([TT, D])
        x_nat = c([TT, D])
        tid = c([TOK], I32)
        ge_mask = c([3, TOK], BF16)
        tok_mask = c([4, TOK], BF16)
        c = Cut(c.at / 256)
        w_l0 = [c([6, D]), c([6, D]), c([KC, H0])]
        wt_l0 = [c([KC, H0], F32R), c([KC, H0], F32R), c([6, D], F32R)]
        tern_tmp = c([6 * D])
        tern_s = [c([32])]
        assert c.at / 256 <= 75
        c = Cut(0)
        xn_parts = {"l0": [c([KC, TOK], F32R) for _ in range(2)]}
        hid_parts = {"l0": c([3, 2, HALF], F32R)}
        assert c.at / 256 <= 34
        c = Cut(ARENA - 24 - 18)
        late_at = c.at / 256
        w_l2 = [c([6, D]), c([6, D]), c([KC, H2])]
        w_l3_all = c([24, D])
        w_l3 = [w_l3_all[:, 0:8, :], w_l3_all[:, 8:16, :],
                w_l3_all[:, 16:24, :].rearrange("p a b -> p (a b)").rearrange("p (k n) -> p k n", k=KC)]
        c = Cut(75.5)
        w_l1 = [c([3, D]), c([3, D]), c([KC, H1])]
        wt_l1 = [c([KC, H1]), c([KC, H1]), c([3, D])]
        gw_nat = c([D])
        gw_t = c([KC, NE])
        mu_nat = c([KC, NF, NK])
        mu_t = c([D])
        rep = c([P])
        sc_rep = c([P])
        group_mask = c([NF])
        inv_row = c([NE], I32)
        inv_f = c([3, NE])
        e_col = c([1])
        esel = c([NE])
        gate_parts = c([2, TOK], F32R)
        mu_parts = c([2, D], F32R)
        rep_r = c([P], F32R)
        sc_rep_r = c([P], F32R)
        mx_pow = c([2 * D])
        mx_sc = c([2, 2 * D // MX_BLOCK])
        tern_s.append(c([32]))
        assert c.at / 256 <= late_at
        c = Cut(45.0625)
        slots = []
        for _ in range(2):
            slots.append(dict(
                main=c([2, D]), rest=c([D]), qa=c([D]),
                d=c([KC, PACK + P]), dqa=c([PACK + P]), qb=c([P]), qb_rest=c([P]),
                s_main=c([2]), s_rest=c([1]), s_down=c([KC]),
                qbT=c([P]), qb_restT=c([PACK]),
                dqaT=c([64]), dqa_restT=c([64]), dT=c([D]), packT=c([D])))

        def part_weights(b):
            b.update(mainT=c([2, 2 * KC * P], F32R), restT=c([2, KC * PACK], F32R), qaT=c([2, KC * P], F32R))
        part_weights(slots[1])
        assert c.at / 256 <= 75.5
        tern_tmp2 = Cut(45.0625)([6 * D])
        c = Cut(0)
        wk = dict(w=c([KC]), u=c([KC]), wb=c([SEQ]), o=c([BATCH, SEQ + 1]), p=c([BATCH, SEQ + 1]),
                  q=c([BATCH, SEQ + 1]), e1=c([BATCH, SEQ]), e2=c([BATCH, SEQ]), ev=c([BATCH, SEQ]),
                  no=c([BATCH, SEQ]), e3=c([BATCH, SEQ]), e4=c([BATCH, SEQ]), num=c([BATCH, SEQ]),
                  den=c([BATCH, SEQ]))
        c = Cut(0)
        masked = Cut(0)([2, 2, TOK], F32R)
        rt = dict(mx=c([TT]), sum=c([TT]), e=c([TT, NE]), sc=c([TT, NE + 2]), top=c([TT, 8]),
                  mr=c([TT, NE + 2]), wd=c([TT, NE]), wdT=c([TOK]), fl=c([TT, NE]), fm=c([TT, NE]),
                  gmx=c([TT * NF]), gt=c([TT, GATES]))
        moe = dict(xe=xc[:, 0], s=xc[:, 1], h=sq[:, 0, :], pack=sq[:, 1, :], wr=act_buf[:, :, :], sr=hid_buf[:, :, :],
                   aw=c([HALF]), xe_parts=c([TH, 2, KC, HALF], F32R))
        part_weights(slots[0])
        assert c.at / 256 <= 45.25
        c = Cut(0)
        q3 = c([TT, HEADS, 3, HD], BF16)
        k3 = c([TT, HEADS, 3, HD], BF16)
        k_end = c.at / 256
        q_s = c([HEADS, TOK], BF16)
        k_s = c([HEADS, TOK], BF16)
        v_tok = c([TT, D], BF16)
        q_tok = c([TT, D])
        k_tok = c([TT, D])
        v_t = xc[:, :, :, :].rearrange("p h k t -> p (h k t)").rearrange("p (k t) -> p k t", k=KC)
        vn_t = sq[:, :, :].rearrange("p k t -> p (k t)").bitcast(BF16).rearrange("p (k t) -> p k t", k=KC)
        att_small = dict(amax=c([TT * HEADS]), inv=c([TT * HEADS]), sq=c([TT, HEADS]), sk=c([TT * HEADS]),
                         z=c([TT, HEADS]), rz=c([HEADS]), nm=c([2]), bias=c([2]), sv=c([KC]), vinv=c([KC]),
                         vmax=c([KC]), bvp=c([KC]), bpp=c([KC]), vout=c([KC]))
        c2 = Cut(0)
        wkv2 = c2([KC, 2 * D])
        wq2 = c2([KC, D])
        bq_row = c2([D], parts=1)
        bk_row = c2([D], parts=1)
        wp2 = hid_buf[:, 1, :].rearrange("p (k n) -> p k n", k=KC)
        assert c.at / 256 <= late_at
        c2 = Cut(0)
        att_e = xc[:, :, :, :].rearrange("p h k t -> p h (k t)")
        att_p = c2([2, TOK], BF16)
        att_pt = c2([4, TT, P], BF16)
        assert c2.at / 256 <= k_end
        o_tok, o_t = q_tok, k_tok.rearrange("p a b -> p (a b)").rearrange("p (k t) -> p k t", k=KC)
        c = Cut(0)
        wt_l2 = [c([KC, H2], F32R), c([KC, H2], F32R), c([6, D], F32R)]
        lx_nat = [c([KC, D]), c([KC, D]), c([KC, D]), c([4, D])]
        lx_t = [c([KC, D]), c([KC, D]), c([KC, D]), c([KC, 2 * D])]
        c3 = Cut(c.at / 256)
        xn_parts["l2"] = [c3([KC, TOK], F32R) for _ in range(2)]
        hid_parts["l2"] = c3([3, 2, HALF], F32R)
        assert c3.at / 256 <= late_at
        kf = c([TT, D])
        v1 = c([TT, KC, P + 1])
        lx_min = c([2, D])
        lx_exp = c([2, D])
        bd = c([BATCH, KC, P])
        dd = c([BATCH, KC, P])
        bg = c([KC])
        lx_qmin = c([2, KC, SEQ])
        lx_q = c([2, KC, SEQ])
        lx_gate = c([2, KC, SEQ])
        lx_den = c([KC, SEQ])
        lx_o = c([2, KC, SEQ])
        wt_l3 = [c([KC, H3]), c([KC, H3]), c([8, D])]
        assert c.at / 256 <= late_at
        c = Cut(0)
        mxq = c([8 * D])
        mx_s = c([2, 64])
        xn_tok = c([TT, D])
        xq_t = c([KC, TOK])
        h_tok = c([2, H3])
        h_act = c([H3])
        hq_t = c([2, 8, P])
        x_tok = c([TT, D])
        res = c([2, D])

        dve_step, pool_step = sem("dve_step"), sem("pool_step")
        const_ready = sem("const_ready")
        load = {n: sem("load_" + n) for n in ("ctx", "x", "tid", "l0", "l1", "mu", "wku", "inv", "moe0", "moe1",
                                               "l2w", "l2x", "l2", "l3x", "bg", "l3")}
        turned, evac_act, evac_dve = sem("turned"), sem("evac_act"), sem("evac_dve")
        weights_fixed = sem("weights_fixed")
        x_ready = sem("x_ready")
        ln_mean, ln_xc, ln_sq, ln_var, ln_sd, ln_diag, ln_rows, xn_ready = (sem(n) for n in (
            "ln_mean", "ln_xc", "ln_sq", "ln_var", "ln_sd", "ln_diag", "ln_rows", "xn_ready"))
        hid_ready, act_ready, gated, hid_used, y_ready = (sem(n) for n in (
            "hid_ready", "act_ready", "gated", "hid_used", "y_ready"))
        xn_high, xn_low, hid_high, hid_low = (sem(n) for n in ("xn_high", "xn_low", "hid_high", "hid_low"))
        tern_part, tern_sum = sem("tern_part"), sem("tern_sum")
        mx_step = sem("mx_step")
        exp_in, exp_out = sem("exp_in"), sem("exp_out")
        wk_o, wk_e2, wk_p, wk_num = (sem(n) for n in ("wk_o", "wk_e2", "wk_p", "wk_num"))
        rt_logits, rt_wd, rt_wdt, rt_wdt_sb, rt_flat, rt_gt, rt_gatest, rt_gates_sb = (sem(n) for n in (
            "rt_logits", "rt_wd", "rt_wdt", "rt_wdt_sb", "rt_flat", "rt_gt", "rt_gatest", "rt_gates_sb"))
        moe_masked, moe_fixed, moe_turn_a, moe_turn_d, moe_ev_act, moe_ev_dve, slots_clear = (sem(n) for n in (
            "moe_masked", "moe_fixed", "moe_turn_a", "moe_turn_d", "moe_ev_act", "moe_ev_dve", "slots_clear"))
        moe_xh, moe_xl, moe_high = sem("moe_xh"), sem("moe_xl"), sem("moe_high")
        (moe_mu, moe_wrm, moe_srm, moe_xe, moe_wr, moe_sr, moe_a, moe_aw, moe_h, moe_s, moe_sm, moe_hg, moe_ad,
         moe_awd, moe_y, moe_x) = (sem(n) for n in (
             "moe_mu", "moe_wrm", "moe_srm", "moe_xe", "moe_wr", "moe_sr", "moe_a", "moe_aw", "moe_h", "moe_s",
             "moe_sm", "moe_hg", "moe_ad", "moe_awd", "moe_y", "moe_x"))
        pj_ready, pj_used, v_ready, qk_split, head_turned, head_copied = (sem(n) for n in (
            "pj_ready", "pj_used", "v_ready", "qk_split", "head_turned", "head_copied"))
        vn_ready, vn_turned, v_copied = sem("vn_ready"), sem("vn_turned"), sem("v_copied")
        att_s, att_max, att_bias, att_exp, att_round, att_t, att_copied, att_o, att_o_used = (sem(n) for n in (
            "att_s", "att_max", "att_bias", "att_exp", "att_round", "att_t", "att_copied", "att_o",
            "att_o_used"))
        att_rz = sem("att_rz")
        ot_turned, ot_copied, att_done = sem("ot_turned"), sem("ot_copied"), sem("att_done")
        lx_kv, lx_min_r, lx_exp_r, lx_kf, lx_v, lx_sum, lx_bd = (sem(n) for n in (
            "lx_kv", "lx_min_r", "lx_exp_r", "lx_kf", "lx_v", "lx_sum", "lx_bd"))
        lx_qg, lx_qmin_r, lx_act, lx_qf, lx_att, lx_or, lx_x = (sem(n) for n in (
            "lx_qg", "lx_qmin_r", "lx_act", "lx_qf", "lx_att", "lx_or", "lx_x"))
        xt_turned, xt_copied, xq_ready, xq_turned, xq_copied = (sem(n) for n in (
            "xt_turned", "xt_copied", "xq_ready", "xq_turned", "xq_copied"))
        res_copied = sem("res_copied")
        m_gu, m_act, m_mul, m_h, m_ht, m_htc, m_o, m_res = (sem(n) for n in (
            "m_gu", "m_act", "m_mul", "m_h", "m_ht", "m_htc", "m_o", "m_res"))
        stored = [sem("stored_even"), sem("stored_odd")]

        groups = []

        def turn_in(rows, nat, dst, wait, fixed):
            full = rows // P
            todo = [(r, 2) for r in range(0, full - 1, 2)]
            if full % 2:
                todo.append((full - 1, 1))
            todo = [(r * P, [P] * n) for r, n in todo]
            if rows % P:
                todo.append((full * P, [rows % P]))
            for r0, ws in todo:
                turns = [(P, w, k * 256 + j * P, nat[0:w, r0 // P + j, k * P:(k + 1) * P])
                         for k in range(KC) for j, w in enumerate(ws)]
                n = sum(ws)
                groups.append((turns, [(dst[:, :, r0:r0 + n], P, 0, 256, n)], wait, fixed))

        def turn_out(cols, nat, dst, wait, fixed):
            full = cols // P
            for c0 in range(0, full, 2):
                n = min(2, full - c0)
                turns = [(P, P, j * 256 + r * P, nat[:, r, (c0 + j) * P:(c0 + j + 1) * P])
                         for j in range(n) for r in range(KC)]
                groups.append((turns, [(dst[:, c0:c0 + n, :], P, 0, 256, 256)], wait, fixed))
            if cols % P:
                w = cols % P
                turns = [(w, P, r * P, nat[:, r, full * P:cols]) for r in range(KC)]
                groups.append((turns, [(dst[0:w, full:full + 1, :], w, 0, 256, 256)], wait, fixed))

        marks = {}

        def mark(name, f):
            first = len(groups)
            f()
            marks[name] = (first, len(groups))

        def tokens_turned(nat, dst, wait):
            for h in range(TH):
                for k in range(KC):
                    turns = [(P, P, j * P, nat[:, 4 * h + j, k * P:(k + 1) * P]) for j in range(4)]
                    groups.append((turns, [(dst[:, k, h * HALF:(h + 1) * HALF].unsqueeze(1), P, 0, 512, 512)],
                                   wait, 0))

        mark("x", lambda: tokens_turned(x_nat, x_t, (load["x"], 16)))
        mark("ctx", lambda: tokens_turned(ctx_nat, ctx_t, (load["ctx"], 16)))

        def three(ws, wts, h, wait, fixed):
            turn_in(h, ws[0], wts[0], wait, fixed)
            turn_in(h, ws[1], wts[1], wait, fixed)
            turn_out(h, ws[2], wts[2], wait, fixed)
        mark("l0", lambda: three(w_l0, wt_l0, H0, None, 1))
        mark("l1", lambda: three(w_l1, wt_l1, H1, (load["l1"], 16 * 5), 0))

        def small():
            turns = [(P, NE, k * NE, gw_nat[0:NE, k * P:(k + 1) * P]) for k in range(KC)]
            groups.append((turns, [(gw_t[:, :, :], P, 0, NE, NE)], (load["mu"], 16 * 3), 0))
            turns = [(NE, P, k * P, mu_nat[:, k, :, :].rearrange("p f k -> p (f k)")) for k in range(KC)]
            groups.append((turns, [(mu_t[0:NE, :].unsqueeze(1), NE, 0, 256, 256)], (load["mu"], 16 * 3), 0))
        mark("small", small)
        mark("l2", lambda: three(w_l2, wt_l2, H2, None, 3))

        def lx():
            turn_in(D, lx_nat[0], lx_t[0], (load["l3x"], 16 * 4), 0)
            turn_in(D, lx_nat[1], lx_t[1], (load["l3x"], 16 * 4), 0)
            turn_in(D, lx_nat[2], lx_t[2], (load["l3x"], 16 * 4), 0)
            turn_in(2 * D, lx_nat[3], lx_t[3], (load["l3x"], 16 * 4), 0)
        mark("lx", lx)
        mark("l3", lambda: three(w_l3, wt_l3, H3, None, 3))

        by_dve = [g % 2 == 1 and not marks["l1"][0] <= g < marks["small"][1] and g < marks["l3"][0] for g in range(len(groups))]

        def copied(g):
            n = sum(d == by_dve[g] for d in by_dve[0:g + 1])
            return (evac_dve if by_dve[g] else evac_act), n

        def evacuated(eng, upto):
            for g in (upto - 2, upto - 1):
                eng.wait_ge(*copied(g))

        def part_of(name, part):
            g0, g1 = marks[name]
            if part is None:
                return range(g0, g1)
            i, n = part
            return range(g0 + (g1 - g0) * i // n, g0 + (g1 - g0) * (i + 1) // n)

        def pe_turn(pe, name, part=None):
            for g in part_of(name, part):
                turns, _, wait, fixed = groups[g]
                if g >= 2:
                    pe.wait_ge(*copied(g - 2))
                if wait:
                    pe.wait_ge(*wait)
                if fixed:
                    pe.wait_ge(weights_fixed, fixed)
                for m, w, col, src in turns:
                    last = pe.transpose(ps[0:m, 6 + g % 2, col:col + w], src, ident[0:src.shape[0], 0:src.shape[0]])
                last.then_inc(turned, 1)

        def copy_out(eng, name, dve, part=None):
            for g in part_of(name, part):
                if by_dve[g] != dve:
                    continue
                eng.wait_ge(turned, g + 1)
                for dst, m, col, step, n in groups[g][1]:
                    k = dst.shape[1]
                    src = ps[0:m, 6 + g % 2, col:col + k * step].rearrange("p (k n) -> p k n", k=k)[:, :, 0:n]
                    if dve:
                        last = eng.tensor_copy(dst, src)
                    else:
                        last = eng.activation(dst, src, ACT.Copy)
                last.then_inc(evac_dve if dve else evac_act, 1)

        def std_ffn(name, wts, h):
            ch = chunks(h)
            return dict(name=name, n=len(ch), rows=[w for _, w in ch],
                        w1=lambda k, i: wts[0][:, k, ch[i][0]:ch[i][0] + ch[i][1]],
                        w3=lambda k, i: wts[1][:, k, ch[i][0]:ch[i][0] + ch[i][1]],
                        w2=lambda i, o: wts[2][0:ch[i][1], i, o * P:(o + 1) * P])

        l0x = dict(name="l0x", n=4 * KC, rows=[P] * 4 * KC,
                   w1=lambda k, i: ctx_t[:, k, i * P:(i + 1) * P], w3=None,
                   w2=lambda i, o: ctx_t[:, i % KC, (i // KC) * SEQ + o * P:(i // KC) * SEQ + (o + 1) * P])
        l0 = std_ffn("l0", wt_l0, H0)
        l1 = std_ffn("l1", wt_l1, H1)
        l2 = std_ffn("l2", wt_l2, H2)
        unit = split_unit = 0
        for s in (l0x, l0, l1, l2):
            s["u0"], s["v0"] = unit, split_unit
            unit += TH * s["n"]
            s["split"] = s["name"] in SPLIT
            if s["split"]:
                split_unit += TH * s["n"]
        LN = dict(l0x=0, l0=1, wkv=2, l1=3, l2x=4, l2=5, l3x=6, l3=7)

        def ln_bank(name, h):
            return 4 if (name, h) in (("l0x", 0), ("l1", 0), ("l1", 1), ("l2", 0)) else 6

        INSIDE = dict(l0x=(("l0x", 1), ("l0", 0)), l0=(("l0", 1), ("wkv", 0)), l1=(None, ("l2x", 0)),
                      l2=(("l2", 1), ("l3x", 0)))

        def ln_steps(n):
            if n < 6:
                return dict(mean=0, xc=0, sq=1, var=1, sd=2, diag=2, rows=2, xn=2, parts=2)
            if n == 6:
                return dict(mean=1, xc=1, sq=2, var=2, sd=3, diag=3, rows=4, xn=5, parts=5)
            return dict(mean=1, xc=1, sq=2, var=3, sd=4, diag=4, rows=5, xn=6, parts=7)

        def head_by_dve(n):
            return n >= 2 * HEADS - 14 and n % 2 == 1

        def tok(h):
            return slice(h * HALF, (h + 1) * HALF)

        block = ctx.enter_context(nc.Block())

        @block.sync
        def _(sp):
            sp.dma_start(x_nat, a["x"].rearrange("b (c p) d -> p (b c) d", p=P)).then_inc(load["x"], 16)
            sp.dma_start(ctx_nat, a["ctx_2048"].rearrange("b (c p) d -> p (b c) d", p=P)).then_inc(load["ctx"], 16)
            sp.dma_start(tid, a["itok_BxS_13_99985"].rearrange("b s -> (b s)").partition_broadcast(P)
                         ).then_inc(load["tid"], 16)

            def rows_in(dst, src, s):
                full = src.shape[0] // P
                sp.dma_start(dst[:, 0:full, :], src[0:full * P, :].rearrange("(c p) d -> p c d", p=P)).then_inc(s, 16)
                if src.shape[0] % P:
                    sp.dma_start(dst[0:src.shape[0] % P, full, :], src[full * P:, :]).then_inc(s, 16)

            for w, n in zip(w_l0, ("L0_ffn_w1", "L0_ffn_w3", "L0_ffn_w2")):
                rows_in(w, a[n], load["l0"])
            for w, n in zip(w_l1, ("L1_ffn_sh_gate_W", "L1_ffn_sh_up_W", "L1_ffn_sh_down_W")):
                rows_in(w, a[n], load["l1"])
            sp.dma_start(gw_nat[0:NE, :], a["L1_ffn_gate_weight"]).then_inc(load["mu"], 16)
            for k in range(KC):
                sp.dma_start(mu_nat[:, k], a["L1_ffn_mask_up_W"][:, k * P:(k + 1) * P, :].rearrange("f p k -> p f k")
                             ).then_inc(load["mu"], 16)
            sp.dma_start(inv_row[0:NE], a["L1_ffn_inv_mapping"].rearrange("f k -> (f k)").partition_broadcast(NE)
                         ).then_inc(load["inv"], 16)

            for w, n in zip(w_l2, ("L2_ffn_w1", "L2_ffn_w2", "L2_ffn_w3")):
                rows_in(w, a[n], load["l2"])
            for w, n in zip(w_l3, ("L3_ffn_gate_w", "L3_ffn_up_w", "L3_ffn_down_w")):
                rows_in(w, a[n], load["l3"])

            def load_slot(f, s):
                b = slots[s]
                done = load[f"moe{s}"]
                f1 = bass.ds(f, 1)

                def go(dst, src, columns=False):
                    sp.dma_start(dst, src, allow_slow_non_contiguous=columns).then_inc(done, 16)
                for j, (w, qb, qa, sc) in enumerate((
                        ("L1_ffn_gate_W", "L1_ffn_gate_qb", "L1_ffn_gate_qa", "L1_ffn_gate_scale"),
                        ("L1_ffn_up_W", "L1_ffn_up_qb", "L1_ffn_up_qa", "L1_ffn_up_scale"))):
                    r0 = 64 * j
                    go(b["main"][:, j, :], a[w][f1, 0:P].rearrange("f p d -> p (f d)"))
                    go(b["rest"][r0:r0 + REST], a[w][f1, P:INNER].rearrange("f p d -> p (f d)"))
                    go(b["qa"][r0:r0 + 64], a[qa][f1].rearrange("f k r d -> (f k r) d"))
                    go(b["qb"][:, r0:r0 + 64].rearrange("p (k r) -> p k r", k=NK),
                       a[qb][f1, :, 0:P, :].rearrange("f k p r -> p (f k) r"))
                    go(b["qb_rest"][r0:r0 + REST, r0:r0 + 64].rearrange("p (k r) -> p k r", k=NK),
                       a[qb][f1, :, P:INNER, :].rearrange("f k p r -> p (f k) r"))
                    go(b["s_main"][:, j:j + 1], a[sc][f1, 0:P].rearrange("f p -> p f"), True)
                    go(b["s_rest"][r0:r0 + REST], a[sc][f1, P:INNER].rearrange("f p -> p f"), True)
                down = a["L1_ffn_down_W"][f1].rearrange("f (c p) d -> p (f c) d", p=P)
                go(b["d"][:, :, PACK:], down[:, :, 0:P])
                go(b["d"][:, :, 64:PACK], down[:, :, P:INNER])
                dqa = a["L1_ffn_down_qa"][f1].rearrange("f k r d -> (f k r) d")
                go(b["dqa"][0:64, PACK:], dqa[:, 0:P])
                go(b["dqa"][0:64, 64:PACK], dqa[:, P:INNER])
                for i in range(KC):
                    go(b["d"][:, i, 0:64].rearrange("p (k r) -> p k r", k=NK),
                       a["L1_ffn_down_qb"][f1, :, i * P:(i + 1) * P, :].rearrange("f k p r -> p (f k) r"))
                go(b["s_down"], a["L1_ffn_down_scale"][f1].rearrange("f (c p) -> p (f c)", p=P), True)

            sp.wait_ge(x_ready, 2 * LN["wkv"] + 2)
            for n, d in (("L1_xattn_w", wk["w"]), ("L1_xattn_u", wk["u"])):
                sp.dma_start(d, a[n].rearrange("(k p) -> p k", p=P),
                             allow_slow_non_contiguous=True).then_inc(load["wku"], 16)
            sp.wait_ge(slots_clear, 1)
            load_slot(0, 0)
            load_slot(1, 1)
            with sp.Fori(1, NF // 2) as pair:
                for s in range(2):
                    sp.wait_ge(moe_turn_a, pair * 4 + (2 * s - 2))
                    sp.wait_ge(moe_turn_d, pair * 4 + (2 * s - 2))
                    load_slot(pair * 2 + s, s)
            sp.wait_ge(moe_x, 2 * NF + 1)
            bkv = a["L2_xattn_bkv"]
            for d, w in ((wkv2, a["L2_xattn_Wkv"]), (wq2, a["L2_xattn_Wq"])):
                sp.dma_start(d, w.rearrange("(k p) n -> p k n", p=P)).then_inc(load["l2w"], 16)
            sp.dma_start(bq_row, a["L2_xattn_bq"].unsqueeze(0)).then_inc(load["l2w"], 16)
            sp.dma_start(bk_row, bkv[0:D].unsqueeze(0)).then_inc(load["l2w"], 16)
            sp.wait_ge(x_ready, 2 * LN["l2x"] + 2)
            sp.dma_start(wp2, a["L2_xattn_Wp"].rearrange("(k p) n -> p k n", p=P)).then_inc(load["l2x"], 16)
            sp.dma_start(att_small["bvp"], bkv[D:2 * D].rearrange("(k p) -> p k", p=P),
                             allow_slow_non_contiguous=True).then_inc(load["l2x"], 16)
            sp.dma_start(att_small["bpp"], a["L2_xattn_bp"].rearrange("(k p) -> p k", p=P),
                             allow_slow_non_contiguous=True).then_inc(load["l2x"], 16)
            sp.wait_ge(x_ready, 2 * LN["l2"] + 2)
            for w, n in zip(lx_nat, ("L3_xattn_Wq", "L3_xattn_Wg", "L3_xattn_Wo", "L3_xattn_Wkv")):
                rows_in(w, a[n], load["l3x"])
            sp.dma_start(bg, a["L3_xattn_bg"].rearrange("(k p) -> p k", p=P),
                             allow_slow_non_contiguous=True).then_inc(load["bg"], 16)
            rows = out.rearrange("b (c p) d -> (b c) p d", p=P)
            for t in range(TT):
                sp.wait_ge(m_res, t + 1)
                sp.dma_start(rows[t], res[:, t % 2, :]).then_inc(stored[t % 2], 16)
            for s in stored:
                sp.wait_ge(s, 16 * TT // 2)

        @block.gpsimd
        def _(pool):
            made = 0

            def step(ins):
                nonlocal made
                made += 1
                ins.then_inc(pool_step, 1)
                pool.wait_ge(pool_step, made)

            step(pool.memset(ones[:, :], 1.0))
            step(pool.memset(mean_w[:, :], 1.0 / D))
            step(pool.memset(eps_col[:, :], LN_EPS))
            step(pool.affine_select(out=ident[:, :], in_=ones[:, :], compare_op=ALU.is_equal, fill=0.0, base=0,
                                    pattern=[[-1, P]], channel_multiplier=1))
            step(pool.tensor_copy(ident_b[:, :], ident[:, :]))
            pool.sem_inc(const_ready, 1)
            hm = head_mask[:, :].rearrange("p (a b) -> p a b", a=P // HD)
            on = ones[:, :].rearrange("p (a b) -> p a b", a=P // HD)
            step(pool.affine_select(out=hm, in_=on, compare_op=ALU.is_ge, fill=0.0, base=0,
                                    pattern=[[-HD, P // HD], [0, HD]], channel_multiplier=1))
            step(pool.affine_select(out=hm, in_=hm, compare_op=ALU.is_ge, fill=0.0, base=HD - 1,
                                    pattern=[[HD, P // HD], [0, HD]], channel_multiplier=-1))
            g0 = group_mask[0:NE, :]
            step(pool.memset(group_mask, 1.0))
            step(pool.affine_select(out=g0, in_=g0, compare_op=ALU.is_ge, fill=0.0, base=0,
                                    pattern=[[-NK, NF]], channel_multiplier=1))
            step(pool.affine_select(out=g0, in_=g0, compare_op=ALU.is_ge, fill=0.0, base=NK - 1,
                                    pattern=[[NK, NF]], channel_multiplier=-1))
            g1 = group_mask[NE:GATES, :]
            step(pool.affine_select(out=g1, in_=g1, compare_op=ALU.is_equal, fill=0.0, base=0,
                                    pattern=[[-1, NF]], channel_multiplier=1))
            step(pool.memset(sc_rep[0:NE, :], 0.0))
            step(pool.memset(sc_rep[NE:GATES, :], 1.0))
            step(pool.memset(rep[0:NE, :], 0.0))
            step(pool.memset(rep[NE:GATES, :], 0.0))
            rp = rep[0:NE, :].rearrange("p (a k r) -> p a k r", a=2, k=NK)
            for m in range(NF):
                step(pool.affine_select(out=rp, in_=rp, compare_op=ALU.not_equal, fill=1.0, base=-NK * m,
                                        pattern=[[0, 2], [-1, NK], [0, NR]], channel_multiplier=1))
            step(pool.iota(e_col[0:NE, :], pattern=[[0, 1]], base=0, channel_multiplier=1,
                           allow_small_or_imprecise_dtypes=True))
            step(pool.memset(mu_t[NE:GATES, :], 0.0))
            pool.sem_inc(const_ready, 1)
            pool.wait_ge(x_ready, 2 * LN["wkv"] + 2)
            for b in slots:
                step(pool.memset(b["rest"], 0.0))
                step(pool.memset(b["qb_rest"], 0.0))
                step(pool.memset(b["dqa"], 0.0))
                step(pool.memset(b["s_rest"], 0.0))
            pool.sem_inc(slots_clear, 1)
            W = wk
            for k in range(KC):
                kk = xn_t[:, k, :].rearrange("p (b s) -> p b s", b=BATCH)
                vv = ctx_t[:, k, :].rearrange("p (b s) -> p b s", b=BATCH)
                pool.wait_ge(wk_o, k + 1)
                pool.tensor_tensor(W["e2"], kk, W["o"][:, :, 1:SEQ + 1], ALU.subtract).then_inc(wk_e2, 1)
                pool.wait_ge(exp_out, 4 * k + 4)
                pool.wait_ge(wk_p, k + 1)
                step(pool.tensor_tensor(W["num"], W["e3"], W["p"][:, :, 0:SEQ], ALU.mult))
                step(pool.tensor_tensor(W["ev"], W["e4"], vv, ALU.mult))
                pool.tensor_tensor(W["num"], W["num"], W["ev"], ALU.add).then_inc(wk_num, 1)

        @block.tensor
        def _(pe):
            def mm(o, l, r, start, stop):
                return pe.matmul(o, l, r, start=start, stop=stop)

            def ln_mean_of(name, h):
                L = LN[name]
                n = 2 * L + h
                pe.wait_ge(x_ready, 2 * L + (2 if name == "l1" else h + 1))
                if n:
                    pe.wait_ge(ln_xc, n)
                for k in range(KC):
                    last = mm(ps[:, ln_bank(name, h), :], mean_w[:, :], x_t[:, k, tok(h)], k == 0, k == KC - 1)
                last.then_inc(ln_mean, 1)

            def ln_var_of(name, h):
                n = 2 * LN[name] + h
                pe.wait_ge(ln_sq, n + 1)
                if n:
                    pe.wait_ge(xn_ready, n)
                for j in range(4):
                    for k in range(KC):
                        last = mm(ps[:, ln_bank(name, h) + 1, j:j + 1], sq[:, k, j * P:(j + 1) * P], mean_w[:, 0:1],
                                  k == 0, k == KC - 1)
                last.then_inc(ln_var, 1)

            def ln_rows_of(name, h):
                pe.wait_ge(ln_diag, 2 * LN[name] + h + 1)
                mm(ps[:, ln_bank(name, h) + 1, :], ones[:, :], rsd_diag[:, :, :].rearrange("p a b -> p (a b)"), True,
                   True).then_inc(ln_rows, 1)

            def ffn(s, between=None):
                L = LN[s["name"]]
                at = ln_steps(s["n"])
                name = s["name"]
                lag = 2 if s["split"] else 1
                for h in range(TH):
                    if s["split"]:
                        pe.wait_ge(xn_low, 2 * SPLIT[name] + h + 1)
                        xs = xn_parts[name]
                    else:
                        pe.wait_ge(xn_ready, 2 * L + h + 1)
                        xs = [xn_t[:, :, :]]
                    norm = INSIDE[name][h]

                    def down(i):
                        u = s["u0"] + h * s["n"] + i
                        if s["split"]:
                            v = s["v0"] + h * s["n"] + i
                            pe.wait_ge(hid_low, v + 1)
                            hid = [hid_parts[name][:, v % 3, j, :] for j in range(2)]
                        else:
                            pe.wait_ge(gated, u + 1)
                            hid = [hid_buf[:, u % 2, :]]
                        if i == 0:
                            pe.wait_ge(x_ready, 2 * L + h + 2)
                        r = s["rows"][i]
                        for o in range(KC):
                            for part in hid:
                                last = mm(ps[:, 4 + o, :], s["w2"](i, o), part[0:r], i == 0 and part is hid[0],
                                          i == s["n"] - 1 and part is hid[-1])
                        last.then_inc(hid_used, 1)

                    for i in range(s["n"]):
                        u = s["u0"] + h * s["n"] + i
                        if u >= 2:
                            pe.wait_ge(gated, u - 1)
                        r = s["rows"][i]
                        b = 2 * (u % 2)
                        for j, w in enumerate([s["w1"], s["w3"]] if s["w3"] else [s["w1"]]):
                            for k in range(KC):
                                for x in xs:
                                    last = mm(ps[0:r, b + j, :], w(k, i), x[:, k, tok(h)], k == 0 and x is xs[0],
                                              k == KC - 1 and x is xs[-1])
                        last.then_inc(hid_ready, 1)
                        if i >= lag:
                            down(i - lag)
                        if norm and i == at["mean"]:
                            ln_mean_of(*norm)
                        if norm and i == at["var"]:
                            ln_var_of(*norm)
                        if norm and i == at["rows"]:
                            ln_rows_of(*norm)
                        if between:
                            between(h * s["n"] + i)
                    for i in range(s["n"] - lag, s["n"]):
                        down(i)

            def ternary(n):
                pe.wait_ge(tern_part, n)
                if n == 1:
                    pe.wait_ge(xn_ready, 2)
                mm(ps[:, 7, 0:6], ones[:, :], tern_s[n - 1][:, 0:6], True, True).then_inc(tern_sum, 1)

            def sums(n, at):
                def go(i):
                    if i == at:
                        ternary(n)
                return go

            pe.wait_ge(const_ready, 1)
            pe_turn(pe, "x")
            ln_mean_of("l0x", 0)
            pe_turn(pe, "ctx")
            ln_var_of("l0x", 0)
            ln_rows_of("l0x", 0)
            evacuated(pe, marks["ctx"][1])
            ffn(l0x, sums(1, TERN_SUM))
            pe_turn(pe, "l0")
            evacuated(pe, marks["l0"][1])
            ffn(l0)
            ln_mean_of("wkv", 1)
            ln_var_of("wkv", 1)
            ln_rows_of("wkv", 1)
            pe.wait_ge(xn_ready, 2 * LN["wkv"] + 2)
            pe_turn(pe, "l1")
            pe_turn(pe, "small")
            evacuated(pe, marks["small"][1])
            def turned(m, bank, col, src):
                n = src.shape[0]
                return pe.transpose(ps[0:m, bank, col:col + n], src, ident[0:n, 0:n])

            def turn_first(f, s):
                b = slots[s]
                pe.wait_ge(moe_fixed, f + 1)
                for k in range(KC):
                    turned(P, 1, k * P, b["qa"][:, k * P:(k + 1) * P])
                turned(PACK, 1, 320, b["dqa"][0:64, 0:PACK])
                turned(P, 1, 256, b["dqa"][0:64, PACK:]).then_inc(moe_turn_a, 1)
                for j in range(2):
                    for k in range(KC):
                        last = turned(P, 3, (2 * j + k) * P, b["main"][:, j, k * P:(k + 1) * P])
                last.then_inc(moe_turn_d, 1)

            def turn_second(f, s):
                b = slots[s]
                for k in range(KC):
                    turned(P, 1, k * PACK, b["rest"][0:PACK, k * P:(k + 1) * P])
                turned(P, 1, 256, b["qb"])
                turned(P, 1, 384, b["qb_rest"][0:PACK]).then_inc(moe_turn_a, 1)
                for k in range(KC):
                    turned(P, 3, k * P, b["d"][:, k, PACK:])
                for k in range(KC):
                    last = turned(PACK, 3, 256 + k * P, b["d"][:, k, 0:PACK])
                last.then_inc(moe_turn_d, 1)

            for h in range(TH):
                ln_mean_of("l1", h)
            turn_first(0, 0)
            for h in range(TH):
                ln_var_of("l1", h)
                ln_rows_of("l1", h)
            pe.wait_ge(xn_ready, 2 * LN["l1"] + 2)
            for t in range(TT):
                for k in range(KC):
                    last = mm(ps[:, 0, t * NE:(t + 1) * NE], xn_t[:, k, t * P:(t + 1) * P], gw_t[:, k, :],
                              k == 0, k == KC - 1)
            last.then_inc(rt_logits, 1)
            pe.wait_ge(moe_ev_act, 1)
            pe.wait_ge(moe_ev_dve, 1)
            turn_second(0, 0)
            pe.wait_ge(moe_ev_act, 2)
            pe.wait_ge(moe_ev_dve, 2)
            pe.wait_ge(rt_wd, 1)
            for t in range(TT):
                last = pe.transpose(ps[0:NE, 1 + t // 4, (t % 4) * P:(t % 4 + 1) * P], rt["wd"][:, t, :], ident[:, :])
            last.then_inc(rt_wdt, 1)
            pe.wait_ge(rt_wdt_sb, 1)
            for t in range(TT):
                last = mm(ps[:, 3, t * NE:(t + 1) * NE], rt["wdT"][0:NE, t * P:(t + 1) * P], esel[0:NE, :], True, True)
            last.then_inc(rt_flat, 1)
            pe.wait_ge(rt_gt, 1)
            for t in range(TT):
                last = pe.transpose(ps[0:GATES, 1 + t // 4, (t % 4) * P:(t % 4 + 1) * P], rt["gt"][:, t, :], ident[:, :])
            last.then_inc(rt_gatest, 1)
            pe.wait_ge(rt_gates_sb, 1)

            def correction(f, s, h):
                n = f * 2 + h
                g = [masked[0:GATES, s, j, tok(h)] for j in range(2)]
                if h == 0:
                    pe.wait_ge(moe_masked, f + 1)
                    pe.wait_ge(moe_ev_act, f * 2 + 1)
                if not (isinstance(f, int) and n == 0):
                    pe.wait_ge(moe_sr, n)
                mm(ps[:, 7, :], rep_r[0:GATES, :], g[0], True, False)
                mm(ps[:, 7, :], rep_r[0:GATES, :], g[1], False, True).then_inc(moe_wrm, 1)
                for o in range(KC):
                    high, low = (mu_parts[0:GATES, j, o * P:(o + 1) * P] for j in range(2))
                    mm(ps[:, o, :], high, g[0], True, False)
                    mm(ps[:, o, :], high, g[1], False, False)
                    last = mm(ps[:, o, :], low, g[0], False, True)
                last.then_inc(moe_mu, 1)
                pe.wait_ge(moe_wr, n + 1)
                mm(ps[:, 7, :], sc_rep_r[0:GATES, :], g[0], True, False)
                mm(ps[:, 7, :], sc_rep_r[0:GATES, :], g[1], False, True).then_inc(moe_srm, 1)

            def in_parts(o, w, h, start, stop):
                m = w.shape[2] // KC
                for k in range(KC):
                    for i, j in ((0, 0), (0, 1), (1, 0)):
                        last = mm(o, w[:, i, k * m:(k + 1) * m], moe["xe_parts"][:, h, j, k, :],
                                  start and k == 0 and i == j, stop and k == KC - 1 and i == 1)
                return last

            def codes(f, s, h):
                n = f * 2 + h
                if h == 0:
                    pe.wait_ge(moe_ev_act, f * 2 + 1)
                    pe.wait_ge(moe_ev_dve, f * 2 + 1)
                pe.wait_ge(moe_xl, n + 1)
                in_parts(ps[:, 0, :], slots[s]["qaT"], h, True, True).then_inc(moe_a, 1)

            def inner(f, s, h, last_expert):
                n = f * 2 + h
                b, aw = slots[s], moe["aw"]
                if h == 0:
                    pe.wait_ge(moe_ev_act, f * 2 + 2)
                if h == 0:
                    pe.wait_ge(moe_ev_dve, f * 2 + 2)
                elif not last_expert:
                    pe.wait_ge(moe_ev_dve, f * 2 + 3)
                in_parts(ps[:, 2, :], b["mainT"][:, :, 0:KC * P], h, True, False)
                in_parts(ps[0:PACK, 4, :], b["restT"], h, True, False)
                in_parts(ps[:, 3, :], b["mainT"][:, :, KC * P:], h, True, False)
                pe.wait_ge(moe_aw, n + 1)
                mm(ps[:, 2, :], b["qbT"][0:64, :], aw[0:64, :], False, True).then_inc(moe_h, 1)
                mm(ps[:, 3, :], b["qbT"][64:128, :], aw[64:128, :], False, True).then_inc(moe_h, 1)
                mm(ps[0:PACK, 4, :], b["qb_restT"], aw, False, True).then_inc(moe_h, 1)

            def down_codes(f, s, h):
                n = f * 2 + h
                pe.wait_ge(moe_hg, n * 2 + 2)
                mm(ps[0:64, 2, :], slots[s]["dqaT"], moe["h"], True, False)
                mm(ps[0:64, 2, :], slots[s]["dqa_restT"][64:PACK, :], moe["pack"][64:PACK, :], False, True
                   ).then_inc(moe_ad, 1)

            def result_first(f, s, h):
                n = f * 2 + h
                pe.wait_ge(moe_x, n + 1)
                for o in range(KC):
                    mm(ps[:, 5 + o, :], slots[s]["dT"][:, o * P:(o + 1) * P], moe["h"], True, False)

            def result_second(f, s, h):
                n = f * 2 + h
                pe.wait_ge(moe_awd, n + 1)
                for o in range(KC):
                    last = mm(ps[:, 5 + o, :], slots[s]["packT"][0:PACK, o * P:(o + 1) * P], moe["pack"][0:PACK, :],
                              False, True)
                last.then_inc(moe_y, 1)

            def unit(f, s, h, final):
                ahead = (f, s, 1) if h == 0 else (f + 1, 1 - s, 0)
                inner(f, s, h, final)
                if not final or h == 0:
                    correction(*ahead)
                down_codes(f, s, h)
                if not final:
                    pe.wait_ge(moe_xe, f * 2 + (h + 2))
                    (turn_first, turn_second)[h](f + 1, 1 - s)
                result_first(f, s, h)
                if not final or h == 0:
                    codes(*ahead)
                result_second(f, s, h)

            correction(0, 0, 0)
            codes(0, 0, 0)
            with pe.Fori(0, NF // 2 - 1) as pair:
                for s in range(2):
                    for h in range(TH):
                        unit(pair * 2 + s, s, h, False)
            for f in (NF - 2, NF - 1):
                for h in range(TH):
                    unit(f, f % 2, h, f == NF - 1)
            pe.wait_ge(moe_x, 2 * NF + 1)
            ffn(l1, sums(2, 0))

            ln_mean_of("l2x", 1)
            pe.wait_ge(load["l2w"], 16 * 4)
            for n in range(2 * TT):
                t = n % TT
                src, w, row = (xn_t, wq2, bq_row) if n >= TT else (ctx_t, wkv2, bk_row)
                if n == 2:
                    ln_var_of("l2x", 1)
                if n == TT // 2:
                    ln_rows_of("l2x", 1)
                if n == TT + TT // 2:
                    pe.wait_ge(xn_ready, 2 * LN["l2x"] + 2)
                if n >= 4:
                    pe.wait_ge(pj_used, n - 3)
                o = ps[:, n % 4, 0:D]
                for k in range(KC):
                    mm(o, src[:, k, t * P:(t + 1) * P], w[:, k, 0:D], k == 0, False)
                mm(o, ones[0:1, :], row, False, True).then_inc(pj_ready, 1)
            for h in range(TH):
                for o in range(KC):
                    n = 2 * h + o
                    bnk = (4, 5, 6, 7)[n]
                    for k in range(KC):
                        last = mm(ps[:, bnk, :], wkv2[:, k, D + o * P:D + (o + 1) * P], ctx_t[:, k, tok(h)],
                                  k == 0, k == KC - 1)
                    last.then_inc(v_ready, 1)
            for n in range(2 * HEADS):
                src = (k3, q3)[n // HEADS]
                if n % HEADS == 0:
                    pe.wait_ge(qk_split, 2 + 2 * (n // HEADS))
                if n >= 2:
                    pe.wait_ge(head_copied, n - 1)
                else:
                    pe.wait_ge(pj_used, 2 * TT)
                o = ps[:, n % 2, :].bitcast(BF16)
                for t in range(TT):
                    last = pe.transpose(o[0:3 * HD, t * P:(t + 1) * P],
                                        src[:, t, n % HEADS].rearrange("p a b -> p (a b)"), ident_b[:, :])
                last.then_inc(head_turned, 1)
            pe.wait_ge(vn_ready, 1)
            for k in range(KC):
                o = ps[:, 2 + k, :].bitcast(BF16)
                for t in range(TT):
                    last = pe.transpose(o[:, t * P:(t + 1) * P], vn_t[:, k, t * P:(t + 1) * P], ident_b[:, :])
                last.then_inc(vn_turned, 1)
            pe.wait_ge(head_copied, 2 * HEADS)
            pe.wait_ge(v_copied, KC)
            def scores(t, i):
                t, i = t + i // HEADS, i % HEADS
                for kh in range(2):
                    last = mm(ps[:, 2 * (i % 2) + kh, :], q_s[0:3 * HD, i, bass.ds(t * P, P)],
                              k_s[0:3 * HD, i, kh * 512:(kh + 1) * 512], True, True)
                last.then_inc(att_s, 1)

            def turn_probs(t, j):
                pe.wait_ge(att_round, t * HEADS + (j + 1))
                if not (isinstance(t, int) and t * HEADS + j < 2):
                    pe.wait_ge(att_copied, t * HEADS + (j - 1))
                o = ps[:, 4 + j % 2, :].bitcast(BF16)
                for k in range(TT):
                    last = pe.transpose(o[:, k * P:(k + 1) * P], att_p[:, j % 2, k * P:(k + 1) * P], ident_b[:, :])
                last.then_inc(att_t, 1)

            def values(t, j):
                pe.wait_ge(att_copied, t * HEADS + (j + 1))
                if j == 0:
                    pe.wait_ge(att_o_used, t + 1)
                for k in range(TT):
                    last = mm(ps[:, 6, j * HD:(j + 1) * HD], att_pt[:, j % 4, k, :],
                              v_tok[:, k, j * HD:(j + 1) * HD], k == 0, k == TT - 1)
                if j == HEADS - 1:
                    last.then_inc(att_o, 1)

            def query_tile(t, final):
                for i in range(4, HEADS + 4):
                    if i < HEADS or not final:
                        pe.wait_ge(att_exp, t * HEADS + (i - 1))
                        scores(t, i)
                    values(t, i - 4)
                    if i - 2 < HEADS or not final:
                        turn_probs(t, i - 2)

            scores(0, 0)
            scores(0, 1)
            pe.wait_ge(att_exp, 1)
            scores(0, 2)
            turn_probs(0, 0)
            pe.wait_ge(att_exp, 2)
            scores(0, 3)
            turn_probs(0, 1)
            with pe.Fori(0, TT - 1) as t:
                query_tile(t, False)
            query_tile(TT - 1, True)
            pe.wait_ge(att_o_used, TT + 1)
            pe.wait_ge(load["l2x"], 16 * 3)
            for h in range(TH):
                for k in range(KC):
                    for j in range(4):
                        last = pe.transpose(ps[:, 2 * h + k, j * P:(j + 1) * P],
                                            o_tok[:, 4 * h + j, k * P:(k + 1) * P], ident[:, :])
                    last.then_inc(ot_turned, 1)
            for h in range(TH):
                pe.wait_ge(ot_copied, 2 * h + 2)
                for o in range(KC):
                    for k in range(KC):
                        last = mm(ps[:, 4 + 2 * h + o, :], wp2[:, k, o * P:(o + 1) * P], o_t[:, k, tok(h)],
                                  k == 0, k == KC - 1)
                last.then_inc(att_done, 1)
            pe.wait_ge(x_ready, 2 * LN["l2"] + 2)
            ln_mean_of("l2", 0)
            pe_turn(pe, "l2", (0, 2))
            ln_var_of("l2", 0)
            ln_rows_of("l2", 0)
            pe_turn(pe, "l2", (1, 2))
            evacuated(pe, marks["l2"][1])
            ffn(l2)
            pe_turn(pe, "lx")
            evacuated(pe, marks["lx"][1])
            ln_mean_of("l3x", 1)
            for t in range(TT):
                if t == TT // 2:
                    ln_var_of("l3x", 1)
                    ln_rows_of("l3x", 1)
                if t >= 2:
                    pe.wait_ge(lx_kf, t - 1)
                    pe.wait_ge(lx_v, t - 1)
                for j in range(2):
                    for k in range(KC):
                        last = mm(ps[:, 2 * j + t % 2, 0:D], ctx_t[:, k, t * P:(t + 1) * P],
                                  lx_t[3][:, k, j * D:(j + 1) * D], k == 0, k == KC - 1)
                    last.then_inc(lx_kv, 1)
            pe.wait_ge(lx_kf, TT)
            pe.wait_ge(lx_v, TT)
            for b in range(BATCH):
                for m in range(KC):
                    for j in range(2):
                        t = 2 * b + j
                        last = mm(ps[:, b, m * (P + 1):(m + 1) * (P + 1)], kf[:, t, m * P:(m + 1) * P], v1[:, t, m, :],
                                  j == 0, j == 1)
                last.then_inc(lx_sum, 1)
            pe.wait_ge(xn_ready, 2 * LN["l3x"] + 2)
            pe.wait_ge(lx_bd, 1)
            def batch(b):
                return slice(b * SEQ, (b + 1) * SEQ)

            def query_and_gate(b):
                if b:
                    pe.wait_ge(lx_qf, b)
                    pe.wait_ge(lx_act, 2 * b)
                for j in range(2):
                    for o in range(KC):
                        for k in range(KC):
                            last = mm(ps[:, j, o * SEQ:(o + 1) * SEQ], lx_t[j][:, k, o * P:(o + 1) * P],
                                      xn_t[:, k, batch(b)], k == 0, k == KC - 1)
                    last.then_inc(lx_qg, 1)

            query_and_gate(0)
            for b in range(BATCH):
                pe.wait_ge(lx_qf, b + 1)
                for j, w in enumerate((bd, dd)):
                    for m in range(KC):
                        last = mm(ps[:, 2 + j, m * SEQ:(m + 1) * SEQ], w[:, b, m, :], lx_q[:, b % 2, m, :], True, True)
                last.then_inc(lx_att, 1)
                if b + 1 < BATCH:
                    query_and_gate(b + 1)
                pe_turn(pe, "l3", (b, BATCH))
                pe.wait_ge(lx_or, b + 1)
                if b:
                    pe.wait_ge(lx_x, b)
                for o in range(KC):
                    for k in range(KC):
                        last = mm(ps[:, 4, o * SEQ:(o + 1) * SEQ], lx_t[2][:, k, o * P:(o + 1) * P],
                                  lx_o[:, b % 2, k, :], k == 0, k == KC - 1)
                last.then_inc(y_ready, 1)
            evacuated(pe, marks["l3"][1])
            def tokens_turned_back(src, h, done=None):
                for k in range(KC):
                    if done is not None:
                        pe.wait_ge(*done(2 * h + k))
                    for j in range(4):
                        t = 4 * h + j
                        last = pe.transpose(ps[:, 2 * h + k, j * P:(j + 1) * P], src[:, k, t * P:(t + 1) * P],
                                            ident[:, :])
                    last.then_inc(xt_turned, 1)

            for h in range(TH):
                ln_mean_of("l3", h)
            for h in range(TH):
                ln_var_of("l3", h)
                ln_rows_of("l3", h)
                pe.wait_ge(xn_ready, 2 * LN["l3"] + h + 1)
                tokens_turned_back(xn_t, h)
            for h in range(TH):
                tokens_turned_back(x_t, h, lambda n: (xt_copied, n + 1))
            pe.wait_ge(res_copied, 4)
            def tokens_quantised(h):
                pe.wait_ge(xq_ready, h + 1)
                for k in range(KC):
                    for j in range(4):
                        t = 4 * h + j
                        last = pe.transpose(ps[:, 4 + k, j * P:(j + 1) * P], xn_tok[:, t, k * P:(k + 1) * P],
                                            ident[:, :])
                    last.then_inc(xq_turned, 1)
            def gate_up(t):
                if t:
                    pe.wait_ge(m_mul, t)
                pe.wait_ge(xq_copied, 2 * (t // 4) + 2)
                for i in range(4):
                    j, c2_ = divmod(i, 2)
                    for k in range(KC):
                        last = mm(ps[:, i, :], xq_t[:, k, t * P:(t + 1) * P],
                                  wt_l3[j][:, k, c2_ * 512:(c2_ + 1) * 512], k == 0, k == KC - 1)
                    if c2_:
                        last.then_inc(m_gu, 1)

            def hidden_turned(t):
                pe.wait_ge(m_h, t + 1)
                if t:
                    pe.wait_ge(m_htc, t)
                else:
                    pe.wait_ge(xq_copied, 4)
                for k in range(8):
                    last = pe.transpose(ps[:, 4 + k // 4, (k % 4) * P:(k % 4 + 1) * P],
                                        h_tok[:, t % 2, k * P:(k + 1) * P], ident[:, :])
                last.then_inc(m_ht, 1)

            def down(t):
                pe.wait_ge(m_htc, t + 1)
                if t:
                    pe.wait_ge(m_res, t)
                for k in range(8):
                    last = mm(ps[:, 6, 0:D], hq_t[:, t % 2, k, :], wt_l3[2][:, k, :], k == 0, k == 7)
                last.then_inc(m_o, 1)

            tokens_quantised(0)
            gate_up(0)
            tokens_quantised(1)
            gate_up(1)
            for t in range(TT):
                hidden_turned(t)
                if t:
                    down(t - 1)
                if t + 2 < TT:
                    gate_up(t + 2)
            down(TT - 1)

        @block.scalar
        def _(act):
            def ln_sq_of(name, h):
                n = 2 * LN[name] + h
                act.wait_ge(ln_xc, n + 1)
                if n:
                    act.wait_ge(ln_var, n)
                act.activation(sq[:, :, :], xc[:, h], ACT.Square).then_inc(ln_sq, 1)

            def ln_sd_of(name, h):
                n = 2 * LN[name] + h
                act.wait_ge(ln_var, n + 1)
                act.activation(sd[:, h, :], ps[:, ln_bank(name, h) + 1, 0:4], ACT.Sqrt, bias=eps_col[:, :]
                               ).then_inc(ln_sd, 1)

            def ln_high(name, h):
                if name in SPLIT:
                    act.wait_ge(xn_ready, 2 * LN[name] + h + 1)
                    act.activation(xn_parts[name][0][:, :, tok(h)], xn_t[:, :, tok(h)], ACT.Copy).then_inc(xn_high, 1)

            def hidden_high(s, h, i):
                u, v, r = s["u0"] + h * s["n"] + i, s["v0"] + h * s["n"] + i, s["rows"][i]
                act.wait_ge(gated, u + 1)
                if i >= 3 or h:
                    act.wait_ge(hid_used, u - 2)
                act.activation(hid_parts[s["name"]][0:r, v % 3, 0, :], hid_buf[0:r, u % 2, :], ACT.Copy
                               ).then_inc(hid_high, 1)

            def ffn(s, func, scale=None):
                at = ln_steps(s["n"])
                for h in range(TH):
                    norm = INSIDE[s["name"]][h]
                    for i in range(s["n"]):
                        u = s["u0"] + h * s["n"] + i
                        r = s["rows"][i]
                        act.wait_ge(hid_ready, u + 1)
                        if u >= 2:
                            act.wait_ge(gated, u - 1)
                        act.activation(act_buf[0:r, u % 2, :], ps[0:r, 2 * (u % 2), :], func,
                                       scale=1.0 if scale is None else scale[0:r, :]).then_inc(act_ready, 1)
                        if s["split"] and i:
                            hidden_high(s, h, i - 1)
                        if norm and i == at["sq"]:
                            ln_sq_of(*norm)
                        if norm and i == at["sd"]:
                            ln_sd_of(*norm)
                        if norm and i == at["parts"]:
                            ln_high(*norm)
                    if s["split"]:
                        hidden_high(s, h, s["n"] - 1)

            act.wait_ge(const_ready, 1)
            copy_out(act, "x", False)
            ln_sq_of("l0x", 0)
            copy_out(act, "ctx", False)
            ln_sd_of("l0x", 0)
            ffn(l0x, ACT.Silu)
            copy_out(act, "l0", False)
            ffn(l0, ACT.Silu, tern_s[0][:, 8:9])
            ln_sq_of("wkv", 1)
            ln_sd_of("wkv", 1)
            copy_out(act, "l1", False)
            copy_out(act, "small", False)
            for k in range(KC):
                for j, names in enumerate((("e1", "e2"), ("e3", "e4"))):
                    for i, nm in enumerate(names):
                        if nm == "e2":
                            act.wait_ge(wk_e2, k + 1)
                        else:
                            act.wait_ge(exp_in, 3 * k + (1 if nm == "e1" else 3))
                        act.activation(wk[nm], wk[nm], ACT.Exp).then_inc(exp_out, 1)
            for h in range(TH):
                ln_sq_of("l1", h)
                ln_sd_of("l1", h)
            def copy_first(f, s):
                b = slots[s]
                act.wait_ge(moe_turn_a, f * 2 + 1)
                act.activation(b["qaT"][:, 0, :], ps[:, 1, 0:256], ACT.Copy)
                act.activation(b["dqa_restT"][0:PACK], ps[0:PACK, 1, 320:384], ACT.Copy)
                act.activation(b["dqaT"], ps[:, 1, 256:320], ACT.Copy).then_inc(moe_ev_act, 1)

            def copy_second(f, s):
                b = slots[s]
                act.wait_ge(moe_turn_a, f * 2 + 2)
                act.activation(b["restT"][:, 0, :], ps[:, 1, 0:KC * PACK], ACT.Copy)
                act.activation(b["qbT"], ps[:, 1, 256:384], ACT.Copy)
                act.activation(b["qb_restT"], ps[:, 1, 384:384 + PACK], ACT.Copy).then_inc(moe_ev_act, 1)

            copy_first(0, 0)
            copy_second(0, 0)
            act.wait_ge(exp_in, 7)
            act.activation(rt["e"], rt["e"], ACT.Exp).then_inc(exp_out, 1)
            act.wait_ge(rt_wdt, 1)
            act.activation(rt["wdT"][0:NE, :].rearrange("p (a b) -> p a b", a=2), ps[0:NE, 1:3, :], ACT.Copy
                           ).then_inc(rt_wdt_sb, 1)
            act.wait_ge(exp_in, 8)
            act.activation(rt["fm"], rt["fm"], ACT.Exp).then_inc(exp_out, 1)
            act.wait_ge(rt_gatest, 1)
            act.activation(gate_parts[0:GATES, 0, :].rearrange("p (a b) -> p a b", a=2), ps[0:GATES, 1:3, :],
                           ACT.Copy).then_inc(rt_gates_sb, 1)

            def spread(f, s, h):
                n = f * 2 + h
                act.wait_ge(moe_wrm, n + 1)
                act.activation(moe["wr"][:, h, :], ps[:, 7, :], ACT.Copy).then_inc(moe_wr, 1)
                act.wait_ge(moe_srm, n + 1)
                act.activation(moe["sr"][:, h, :], ps[:, 7, :], ACT.Copy).then_inc(moe_sr, 1)

            def x_high(f, s, h):
                act.wait_ge(moe_xe, f * 2 + (h + 1))
                act.activation(moe["xe_parts"][:, h, 0], moe["xe"], ACT.Copy).then_inc(moe_xh, 1)

            def unit(f, s, h, final):
                n = f * 2 + h
                act.wait_ge(moe_h, n * 3 + 1)
                act.activation(moe["s"][:, 0, :], ps[:, 2, :], ACT.Silu).then_inc(moe_s, 1)
                act.wait_ge(moe_h, n * 3 + 3)
                act.activation(moe["s"][64:PACK, 1, :], ps[0:REST, 4, :], ACT.Silu).then_inc(moe_s, 1)
                if not final or h == 0:
                    ahead = (f, s, 1) if h == 0 else (f + 1, 1 - s, 0)
                    spread(*ahead)
                    x_high(*ahead)
                if not final:
                    (copy_first, copy_second)[h](f + 1, 1 - s)

            spread(0, 0, 0)
            x_high(0, 0, 0)
            with act.Fori(0, NF // 2 - 1) as pair:
                for s in range(2):
                    for h in range(TH):
                        unit(pair * 2 + s, s, h, False)
            for f in (NF - 2, NF - 1):
                for h in range(TH):
                    unit(f, f % 2, h, f == NF - 1)
            ffn(l1, ACT.Silu)

            ln_sq_of("l2x", 1)
            for n in range(2 * TT):
                t = n % TT
                if n == 2:
                    ln_sd_of("l2x", 1)
                act.wait_ge(pj_ready, n + 1)
                if n < TT:
                    act.activation(k_tok[:, t, :], ps[:, n % 4, 0:D], ACT.Copy).then_inc(pj_used, 1)
                else:
                    act.activation(q_tok[:, t, :], ps[:, n % 4, 0:D], ACT.Copy, scale=1.0 / math.sqrt(HD)
                                   ).then_inc(pj_used, 1)
            for n in range(2 * HEADS):
                if not head_by_dve(n):
                    act.wait_ge(head_turned, n + 1)
                    if n and head_by_dve(n - 1):
                        act.wait_ge(head_copied, n)
                    dst = (k_s, q_s)[n // HEADS]
                    act.activation(dst[0:3 * HD, n % HEADS, :], ps[0:3 * HD, n % 2, :].bitcast(BF16), ACT.Copy
                                   ).then_inc(head_copied, 1)
            def exponentials(t, i):
                act.wait_ge(att_bias, t * HEADS + (i + 1))
                if not (isinstance(t, int) and t * HEADS + i < 2):
                    act.wait_ge(att_round, t * HEADS + (i - 1))
                t, i = t + i // HEADS, i % HEADS
                act.activation(att_e[:, i % 2, :].rearrange("p (a b) -> p a b", a=2),
                               ps[:, 2 * (i % 2):2 * (i % 2) + 2, :], ACT.Exp,
                               bias=att_small["bias"][:, i % 2:i % 2 + 1],
                               scale=att_small["sq"][:, bass.ds(t, 1), i],
                               accum_out=att_small["z"][:, bass.ds(t, 1), i]).then_inc(att_exp, 1)

            def probs_copy(t, j):
                act.wait_ge(att_t, t * HEADS + (j + 1))
                act.activation(att_pt[:, j % 4].rearrange("p a b -> p (a b)"),
                               ps[:, 4 + j % 2, :].bitcast(BF16), ACT.Copy).then_inc(att_copied, 1)

            def query_tile(t, final):
                for i in range(4, HEADS + 2 if final else HEADS + 4):
                    if i < HEADS or not final:
                        exponentials(t, i)
                    probs_copy(t, i - 2)

            exponentials(0, 0)
            exponentials(0, 1)
            exponentials(0, 2)
            probs_copy(0, 0)
            exponentials(0, 3)
            probs_copy(0, 1)
            with act.Fori(0, TT - 1) as t:
                query_tile(t, False)
            query_tile(TT - 1, True)
            ln_sq_of("l2", 0)
            copy_out(act, "l2", False, (0, 2))
            ln_sd_of("l2", 0)
            ln_high("l2", 0)
            copy_out(act, "l2", False, (1, 2))
            ffn(l2, ACT.Sigmoid)
            copy_out(act, "lx", False)
            ln_sq_of("l3x", 1)
            for t in range(TT):
                if t == TT // 2:
                    ln_sd_of("l3x", 1)
                act.wait_ge(lx_kv, 2 * t + 2)
                act.activation(v1[:, t, :, 0:P], ps[:, 2 + t % 2, 0:D].rearrange("p (m n) -> p m n", m=KC), ACT.Copy
                               ).then_inc(lx_v, 1)
                act.wait_ge(lx_min_r, t + 1)
                if t >= 2:
                    act.wait_ge(lx_kf, t - 1)
                act.activation(lx_exp[:, t % 2, :], lx_min[:, t % 2, :], ACT.Exp).then_inc(lx_exp_r, 1)
            act.wait_ge(load["bg"], 16)
            for b in range(BATCH):
                act.wait_ge(lx_qmin_r, b + 1)
                act.activation(lx_qmin[:, b % 2], lx_qmin[:, b % 2], ACT.Exp).then_inc(lx_act, 1)
                act.wait_ge(lx_qg, 2 * b + 2)
                if b >= 2:
                    act.wait_ge(lx_or, b - 1)
                for o in range(KC):
                    last = act.activation(lx_gate[:, b % 2, o, :], ps[:, 1, o * SEQ:(o + 1) * SEQ], ACT.Sigmoid,
                                          bias=bg[:, o:o + 1])
                last.then_inc(lx_act, 1)
                copy_out(act, "l3", False, (b, BATCH))
            for h in range(TH):
                ln_sq_of("l3", h)
                ln_sd_of("l3", h)
            for n in range(4, 8):
                h, k = divmod(n - 4, 2)
                act.wait_ge(xt_turned, n + 1)
                act.activation(x_tok[:, 4 * h:4 * h + 4, k * P:(k + 1) * P],
                               ps[:, n - 4, :].rearrange("p (t d) -> p t d", t=4), ACT.Copy).then_inc(res_copied, 1)
            for n in range(4):
                h, k = divmod(n, 2)
                act.wait_ge(xq_turned, n + 1)
                act.activation(xq_t[:, k, tok(h)], ps[:, 4 + k, :], ACT.Copy).then_inc(xq_copied, 1)

            def gate_act(t):
                act.wait_ge(m_gu, 2 * t + 1)
                if t:
                    act.wait_ge(m_mul, t)
                act.activation(h_act.rearrange("p (a b) -> p a b", a=2), ps[:, 0:2, :], ACT.Silu).then_inc(m_act, 1)

            def hidden_copied(t):
                act.wait_ge(m_ht, t + 1)
                if t >= 2:
                    act.wait_ge(m_o, t - 1)
                act.activation(hq_t[:, t % 2].rearrange("p a b -> p (a b)").rearrange("p (a b) -> p a b", a=2), ps[:, 4:6, :],
                               ACT.Copy).then_inc(m_htc, 1)

            gate_act(0)
            for t in range(1, TT):
                gate_act(t)
                hidden_copied(t - 1)
            hidden_copied(TT - 1)

        @block.vector
        def _(dve):
            made = 0

            def step(ins):
                nonlocal made
                made += 1
                ins.then_inc(dve_step, 1)
                dve.wait_ge(dve_step, made)

            TS, TTN, STT = dve.tensor_scalar, dve.tensor_tensor, dve.scalar_tensor_tensor

            def b3(v, n):
                return v.unsqueeze(2).to_broadcast([P, v.shape[1], n])

            def ln_xc_of(name, h):
                dve.wait_ge(ln_mean, 2 * LN[name] + h + 1)
                b = ln_bank(name, h)
                TTN(xc[:, h], x_t[:, :, tok(h)], ps[:, b:b + 1, :].to_broadcast([P, KC, HALF]), ALU.subtract
                    ).then_inc(ln_xc, 1)

            def ln_diag_of(name, h):
                n = 2 * LN[name] + h
                dve.wait_ge(ln_sd, n + 1)
                step(dve.reciprocal(rsd[:, h, :], sd[:, h, :]))
                if n:
                    dve.wait_ge(ln_rows, n)
                TTN(rsd_diag[:, :, :], ident[:, :].unsqueeze(1).to_broadcast([P, 4, P]),
                    rsd[:, h, :].unsqueeze(2).to_broadcast([P, 4, P]), ALU.mult).then_inc(ln_diag, 1)

            def ln_xn_of(name, h):
                dve.wait_ge(ln_rows, 2 * LN[name] + h + 1)
                b = ln_bank(name, h) + 1
                TTN(xn_t[:, :, tok(h)], xc[:, h], ps[:, b:b + 1, :].to_broadcast([P, KC, HALF]), ALU.mult
                    ).then_inc(xn_ready, 1)

            def layer_norm(name):
                for h in range(TH):
                    ln_xc_of(name, h)
                for h in range(TH):
                    ln_diag_of(name, h)
                    ln_xn_of(name, h)

            def add_y(h, scalar=None):
                y = ps[:, 4:6, :]
                if scalar is None:
                    return TTN(x_t[:, :, tok(h)], y, x_t[:, :, tok(h)], ALU.add)
                return STT(x_t[:, :, tok(h)], y, scalar, x_t[:, :, tok(h)], ALU.mult, ALU.add)

            def ln_low(name, h):
                if name in SPLIT:
                    dve.wait_ge(xn_high, 2 * SPLIT[name] + h + 1)
                    high, low = xn_parts[name]
                    TTN(low[:, :, tok(h)], xn_t[:, :, tok(h)], high[:, :, tok(h)], ALU.subtract).then_inc(xn_low, 1)

            def hidden_low(s, h, i):
                u, v, r = s["u0"] + h * s["n"] + i, s["v0"] + h * s["n"] + i, s["rows"][i]
                dve.wait_ge(hid_high, v + 1)
                parts = hid_parts[s["name"]]
                TTN(parts[0:r, v % 3, 1, :], hid_buf[0:r, u % 2, :], parts[0:r, v % 3, 0, :], ALU.subtract
                    ).then_inc(hid_low, 1)

            def ffn(s, gate, y_scale=None, between=None):
                at = ln_steps(s["n"])
                for h in range(TH):
                    norm = INSIDE[s["name"]][h]
                    for i in range(s["n"]):
                        u = s["u0"] + h * s["n"] + i
                        r = s["rows"][i]
                        dve.wait_ge(act_ready, u + 1)
                        if s["split"] and (h or i >= 2):
                            dve.wait_ge(hid_low, s["v0"] + h * s["n"] + i - 1)
                        elif u >= 2:
                            dve.wait_ge(hid_used, u - 1)
                        gate(h, i, r, act_buf[0:r, u % 2, :], ps[0:r, 2 * (u % 2), :], ps[0:r, 2 * (u % 2) + 1, :],
                             hid_buf[0:r, u % 2, :]).then_inc(gated, 1)
                        if s["split"] and i:
                            hidden_low(s, h, i - 1)
                        if between:
                            between(h * s["n"] + i)
                        if norm and i == at["xc"]:
                            ln_xc_of(*norm)
                        if norm and i == at["diag"]:
                            ln_diag_of(*norm)
                        if norm and i == at["xn"]:
                            ln_xn_of(*norm)
                        if norm and i == at["parts"]:
                            ln_low(*norm)
                    if s["split"]:
                        hidden_low(s, h, s["n"] - 1)
                    dve.wait_ge(hid_used, s["u0"] + (h + 1) * s["n"])
                    add_y(h, y_scale).then_inc(x_ready, 1)

            def ternary(ws, h, st, tmp, wait, n):
                full = h // P
                parts = [(ws[i][:, 0:full, :], P, 2 * i) for i in range(2)]
                parts += [(ws[i][0:h % P, full, :], h % P, 2 * i + 1) for i in range(2)]
                parts += [(ws[2], P, 4)]

                def piece(i):
                    if i == 0:
                        dve.wait_ge(*wait)
                        step(dve.memset(st, 0.0))
                    if i < len(parts):
                        w, r, col = parts[i]
                        ins = dve.tensor_reduce(st[0:r, col:col + 1], w, AX.XY if len(w.shape) == 3 else AX.X,
                                                ALU.add, apply_absolute_value=True)
                        if i == len(parts) - 1:
                            ins.then_inc(tern_part, 1)
                        else:
                            step(ins)
                    if i == TERN_SUM + 1:
                        dve.wait_ge(tern_sum, n)
                        step(dve.tensor_reduce(st[:, 8:11], ps[:, 7, 0:6].rearrange("p (a b) -> p a b", b=2), AX.X,
                                               ALU.add))
                        step(TS(st[:, 8:11], st[:, 8:11], 1.0 / (h * D), None, ALU.mult))
                        if n == 2:
                            step(TS(st[:, 8:11], st[:, 8:11], 1e-8, None, ALU.add))
                        step(TS(st[:, 12:15], st[:, 8:11], 0.5, None, ALU.mult))
                        step(TS(st[:, 16:19], st[:, 8:11], -0.5, None, ALU.mult))
                        step(TTN(st[:, 20:21], st[:, 9:10], st[:, 10:11], ALU.mult))
                    at = {TERN_SUM + 1: [0], TERN_SUM + 2: [1], TERN_SUM + 3: [2, 3], TERN_SUM + 4: [4]}
                    for j in at.get(i, []):
                        w, r, col = parts[j]
                        i_ = col // 2
                        t = tmp[0:r, 0:w.free_size() if callable(w.free_size) else w.free_size]
                        if len(w.shape) == 3:
                            t = t.rearrange("p (a b) -> p a b", a=w.shape[1])
                        step(TS(t, w, st[0:r, 16 + i_:17 + i_], None, ALU.is_lt))
                        step(STT(w, w, st[0:r, 12 + i_:13 + i_], t, ALU.is_gt, ALU.subtract))
                    if i == TERN_SUM + 4:
                        dve.sem_inc(weights_fixed, 1)
                return piece

            def mx_quant(v, power, scale, back, n, step):
                qf = power.rearrange("p (a b) -> p a b", b=MX_BLOCK)
                flat = v.rearrange("p a b -> p (a b)")
                step(dve.tensor_reduce(scale, v, AX.X, ALU.max, apply_absolute_value=True))
                step(TS(scale, scale, 1.0 / MX_MAX, 1e-30, ALU.mult, ALU.max))
                step(dve.reciprocal(back, scale))
                step(TTN(v, v, b3(back, MX_BLOCK), ALU.mult))
                step(TS(power.bitcast(I32), flat.bitcast(I32), 0x7F800000, None, ALU.bitwise_and))
                step(TS(qf, qf, 2.0 ** -6, 1.5 * 2.0 ** 20, ALU.max, ALU.mult))
                step(TTN(v, v, qf, ALU.add))
                step(TTN(v, v, qf, ALU.subtract))
                return TTN(v, v, b3(scale, MX_BLOCK), ALU.mult)

            copy_out(dve, "x", True)
            dve.wait_ge(evac_act, 2)
            dve.wait_ge(evac_dve, 2)
            dve.sem_inc(x_ready, 2)
            ln_xc_of("l0x", 0)
            copy_out(dve, "ctx", True)
            ln_diag_of("l0x", 0)
            ln_xn_of("l0x", 0)
            dve.wait_ge(load["tid"], 16)
            for e in range(1, 4):
                step(TS(ge_mask[:, e - 1, :], tid, float(e * TOKENS_PER_EXPERT), None, ALU.is_ge))
            step(TS(tok_mask[:, 0, :], ge_mask[:, 0, :], -1.0, 1.0, ALU.mult, ALU.add))
            step(TTN(tok_mask[:, 1, :], ge_mask[:, 0, :], ge_mask[:, 1, :], ALU.subtract))
            step(TTN(tok_mask[:, 2, :], ge_mask[:, 1, :], ge_mask[:, 2, :], ALU.subtract))
            step(dve.tensor_copy(tok_mask[:, 3, :], ge_mask[:, 2, :]))

            def gate_l0x(h, i, r, s, ga, up, hid):
                step(TTN(hid, ga, s, ALU.mult))
                return TTN(hid, hid, tok_mask[:, i // KC, tok(h)], ALU.mult)
            ffn(l0x, gate_l0x, between=ternary(w_l0, H0, tern_s[0], tern_tmp, (load["l0"], 16 * 5), 1))
            copy_out(dve, "l0", True)

            def gate_l0(h, i, r, s, ga, up, hid):
                return STT(hid, up, tern_s[0][0:r, 20:21], s, ALU.mult, ALU.mult)
            ffn(l0, gate_l0)

            ln_xc_of("wkv", 1)
            ln_diag_of("wkv", 1)
            ln_xn_of("wkv", 1)
            dve.wait_ge(load["wku"], 32)
            W = wk
            for k in range(KC):
                kk = xn_t[:, k, :].rearrange("p (b s) -> p b s", b=BATCH)
                vv = ctx_t[:, k, :].rearrange("p (b s) -> p b s", b=BATCH)
                xx = x_t[:, k, :].rearrange("p (b s) -> p b s", b=BATCH)
                w, u = W["w"][:, k:k + 1], W["u"][:, k:k + 1]
                o0, o1 = W["o"][:, :, 0:SEQ], W["o"][:, :, 1:SEQ + 1]
                p0, q0 = W["p"][:, :, 0:SEQ], W["q"][:, :, 0:SEQ]
                step(dve.memset(W["wb"], 0.0))
                step(TS(W["wb"], W["wb"], w, None, ALU.add))
                step(dve.memset(W["o"][:, :, 0:1], -1e38))
                step(dve.memset(W["p"][:, :, 0:1], 0.0))
                step(dve.memset(W["q"][:, :, 0:1], 0.0))
                for b in range(BATCH):
                    step(dve.tensor_tensor_scan(o1[:, b, :], W["wb"], kk[:, b, :], -1e38, ALU.add, ALU.max))
                dve.sem_inc(wk_o, 1)
                step(STT(W["e1"], o0, w, o1, ALU.add, ALU.subtract))
                dve.sem_inc(exp_in, 1)
                step(STT(W["no"], kk, u, o0, ALU.add, ALU.max))
                step(TTN(W["e3"], o0, W["no"], ALU.subtract))
                step(STT(W["e4"], kk, u, W["no"], ALU.add, ALU.subtract))
                dve.sem_inc(exp_in, 2)
                dve.wait_ge(exp_out, 4 * k + 2)
                step(TTN(W["ev"], W["e2"], vv, ALU.mult))
                for b in range(BATCH):
                    step(dve.tensor_tensor_scan(W["p"][:, b, 1:], W["e1"][:, b, :], W["ev"][:, b, :], 0.0,
                                                ALU.mult, ALU.add))
                    step(dve.tensor_tensor_scan(W["q"][:, b, 1:], W["e1"][:, b, :], W["e2"][:, b, :], 0.0,
                                                ALU.mult, ALU.add))
                dve.sem_inc(wk_p, 1)
                dve.wait_ge(exp_out, 4 * k + 4)
                step(TTN(W["den"], W["e3"], q0, ALU.mult))
                step(TTN(W["den"], W["den"], W["e4"], ALU.add))
                step(dve.reciprocal(W["den"], W["den"]))
                dve.wait_ge(wk_num, k + 1)
                step(TTN(W["num"], W["num"], W["den"], ALU.mult))
                TTN(xx, xx, W["num"], ALU.add).then_inc(x_ready, 1)
            def fold_scales(f, s, round_):
                b = slots[s]
                dve.wait_ge(load[f"moe{s}"], round_ * SLOT_LOADED + SLOT_LOADED)
                for j in range(2):
                    v = b["qb"][:, 64 * j:64 * j + 64]
                    TS(v, v, b["s_main"][:, j:j + 1], None, ALU.mult)
                v = b["qb_rest"][0:PACK]
                TS(v, v, b["s_rest"][0:PACK], None, ALU.mult)
                v = b["d"][:, :, 0:64]
                TTN(v, v, b["s_down"].unsqueeze(2).to_broadcast([P, KC, 64]), ALU.mult).then_inc(moe_fixed, 1)

            def copy_first(f, s):
                b = slots[s]
                dve.wait_ge(moe_turn_d, f * 2 + 1)
                dve.tensor_copy(b["mainT"][:, 0, :], ps[:, 3, :]).then_inc(moe_high, 1)
                dve.wait_ge(moe_high, f + 1)
                TTN(b["mainT"][:, 1, :], ps[:, 3, :], b["mainT"][:, 0, :], ALU.subtract)
                dve.wait_ge(moe_ev_act, f * 2 + 1)
                TTN(b["qaT"][:, 1, :], ps[:, 1, 0:256], b["qaT"][:, 0, :], ALU.subtract).then_inc(moe_ev_dve, 1)

            def copy_second(f, s):
                b = slots[s]
                dve.wait_ge(moe_turn_d, f * 2 + 2)
                dve.tensor_copy(b["dT"], ps[:, 3, 0:256])
                dve.tensor_copy(b["packT"][0:PACK], ps[0:PACK, 3, 256:512])
                dve.wait_ge(moe_ev_act, f * 2 + 2)
                TTN(b["restT"][:, 1, :], ps[:, 1, 0:KC * PACK], b["restT"][:, 0, :], ALU.subtract
                    ).then_inc(moe_ev_dve, 1)

            fold_scales(0, 0, 0)
            layer_norm("l1")

            dve.wait_ge(*copied(marks["small"][1] - 1))
            dve.wait_ge(const_ready, 2)
            g = slice(0, GATES)
            dve.tensor_copy(rep_r[g], rep[g])
            dve.tensor_copy(sc_rep_r[g], sc_rep[g])
            step(dve.tensor_copy(mu_parts[g, 0], mu_t[g]))
            step(TTN(mu_parts[g, 1], mu_t[g], mu_parts[g, 0], ALU.subtract))
            dve.wait_ge(load["inv"], 16)
            iv = inv_f[0:NE]
            step(dve.tensor_copy(iv[:, 0, :], inv_row[0:NE]))
            step(TS(iv[:, 1, :], iv[:, 0, :], 0.0, float(NE), ALU.is_lt, ALU.mult))
            step(TTN(iv[:, 0, :], iv[:, 0, :], iv[:, 1, :], ALU.add))
            step(TS(iv[:, 2, :], iv[:, 0, :], 0.0, float(NE - 1), ALU.max, ALU.min))
            dve.wait_ge(const_ready, 1)
            step(TS(esel[0:NE, :], iv[:, 2, :], e_col[0:NE, :], None, ALU.is_equal))
            copy_first(0, 0)
            dve.wait_ge(rt_logits, 1)
            lg = ps[:, 0, :].rearrange("p (t e) -> p t e", e=NE)
            R = rt

            step(dve.tensor_reduce(R["mx"], lg, AX.X, ALU.max))
            step(TTN(R["e"], lg, b3(R["mx"], NE), ALU.subtract))
            dve.sem_inc(exp_in, 1)
            copy_second(0, 0)
            dve.wait_ge(exp_out, 9)
            step(dve.tensor_reduce(R["sum"], R["e"], AX.X, ALU.add))
            step(dve.reciprocal(R["sum"], R["sum"]))
            step(TTN(R["sc"][:, :, 0:NE], R["e"], b3(R["sum"], NE), ALU.mult))
            step(dve.memset(R["sc"][:, :, NE:NE + 2], -1.0))
            for t in range(TT):
                step(dve.max(R["top"][:, t, :], R["sc"][:, t, 0:NE]))
            step(dve.memset(R["top"][:, :, TOP:8], -1.0))
            for t in range(TT):
                step(dve.match_replace(R["mr"][:, t, :], R["top"][:, t, :], R["sc"][:, t, :], -2.0))
            STT(R["wd"], R["mr"][:, :, 0:NE], -2.0, R["sc"][:, :, 0:NE], ALU.is_equal, ALU.mult).then_inc(rt_wd, 1)
            dve.wait_ge(rt_flat, 1)
            fl, fm = (R[n].rearrange("p t (f k) -> p (t f) k", k=NK) for n in ("fl", "fm"))
            step(dve.tensor_copy(R["fl"], ps[:, 3, :].rearrange("p (t e) -> p t e", e=NE)))
            step(dve.tensor_reduce(R["gt"][:, :, NE:GATES], R["fl"].rearrange("p t (f k) -> p t f k", k=NK), AX.X, ALU.add))
            step(TS(R["fm"], R["fl"], 0.0, -1e9, ALU.is_equal, ALU.mult))
            step(TTN(R["fm"], R["fm"], R["fl"], ALU.add))
            step(dve.tensor_reduce(R["gmx"], fm, AX.X, ALU.max))
            step(TTN(fm, fm, b3(R["gmx"], NK), ALU.subtract))
            dve.sem_inc(exp_in, 1)
            dve.wait_ge(exp_out, 10)
            step(dve.tensor_reduce(R["gmx"], fm, AX.X, ALU.add))
            step(dve.reciprocal(R["gmx"], R["gmx"]))
            TTN(R["gt"][:, :, 0:NE].rearrange("p t (f k) -> p t f k", k=NK),
                R["fm"].rearrange("p t (f k) -> p t f k", k=NK),
                R["gmx"].rearrange("p (t f) -> p t f", f=NF).unsqueeze(3).to_broadcast([P, TT, NF, NK]),
                ALU.mult).then_inc(rt_gt, 1)
            dve.wait_ge(rt_gates_sb, 1)
            step(TTN(gate_parts[0:GATES, 1, :].rearrange("p (a b) -> p a b", a=2), ps[0:GATES, 1:3, :],
                     gate_parts[0:GATES, 0, :].rearrange("p (a b) -> p a b", a=2), ALU.subtract))

            def mask_gates(f, s):
                TS(masked[0:GATES, s], gate_parts[0:GATES], group_mask[0:GATES, bass.ds(f, 1)], None, ALU.mult
                   ).then_inc(moe_masked, 1)

            def corrected(f, s, h):
                dve.wait_ge(moe_mu, f * 2 + (h + 1))
                if not (isinstance(f, int) and f * 2 + h == 0):
                    dve.wait_ge(moe_xl, f * 2 + h)
                TTN(moe["xe"], ps[:, 0:2, :], xn_t[:, :, tok(h)], ALU.add).then_inc(moe_xe, 1)

            def x_low(f, s, h):
                dve.wait_ge(moe_xh, f * 2 + (h + 1))
                parts = moe["xe_parts"]
                TTN(parts[:, h, 1], moe["xe"], parts[:, h, 0], ALU.subtract).then_inc(moe_xl, 1)

            def weighted_codes(f, s, h):
                n = f * 2 + h
                dve.wait_ge(moe_a, n + 1)
                dve.wait_ge(moe_wr, n + 1)
                TTN(moe["aw"], ps[:, 0, :], moe["wr"][:, h, :], ALU.mult).then_inc(moe_aw, 1)

            def mx_weights(unit):
                def after(ins):
                    nonlocal at
                    at += 1
                    ins.then_inc(mx_step, 1)
                    dve.wait_ge(mx_step, unit * 9 + at)
                at = 0
                v = w_l3_all[:, bass.ds(unit * 2, 2), :].rearrange("p a b -> p (a b)").rearrange(
                    "p (a b) -> p a b", b=MX_BLOCK)
                after(mx_quant(v, mx_pow, mx_sc[:, 0, :], mx_sc[:, 1, :], 16, after))

            def unit(f, s, h, final, round_):
                n = f * 2 + h
                M = moe
                dve.wait_ge(moe_sr, n + 1)
                dve.wait_ge(moe_h, n * 3 + 2)
                TTN(M["h"], ps[:, 3, :], M["sr"][:, h, :], ALU.mult).then_inc(moe_sm, 1)
                dve.wait_ge(moe_sm, n * 2 + 1)
                dve.wait_ge(moe_s, n * 2 + 1)
                TTN(M["h"], M["h"], M["s"][:, 0, :], ALU.mult).then_inc(moe_hg, 1)
                v = M["pack"][64:PACK, :]
                dve.wait_ge(moe_h, n * 3 + 3)
                TTN(v, ps[64:PACK, 4, :], M["sr"][64:PACK, h, :], ALU.mult).then_inc(moe_sm, 1)
                dve.wait_ge(moe_sm, n * 2 + 2)
                dve.wait_ge(moe_s, n * 2 + 2)
                TTN(v, v, M["s"][64:PACK, 1, :], ALU.mult).then_inc(moe_hg, 1)
                ahead = (f, s, 1) if h == 0 else (f + 1, 1 - s, 0)
                if not final or h == 0:
                    corrected(*ahead)
                dve.wait_ge(moe_ad, n + 1)
                TTN(M["pack"][0:64, :], ps[0:64, 2, :], M["wr"][0:64, h, :], ALU.mult).then_inc(moe_awd, 1)
                if not final or h == 0:
                    x_low(*ahead)
                if not final:
                    (copy_first, copy_second)[h](f + 1, 1 - s)
                if not final or h == 0:
                    weighted_codes(*ahead)
                if not final and h == 0:
                    mask_gates(f + 1, 1 - s)
                if round_ is not None:
                    mx_weights(n)
                dve.wait_ge(moe_y, n + 1)
                TTN(x_t[:, :, tok(h)], ps[:, 5:7, :], x_t[:, :, tok(h)], ALU.add).then_inc(moe_x, 1)
                if h == 1 and round_ is not None:
                    fold_scales(f + 2, s, round_)

            dve.sem_inc(moe_x, 1)
            dve.wait_ge(load["l3"], 16 * 3)
            mask_gates(0, 0)
            fold_scales(1, 1, 0)
            corrected(0, 0, 0)
            x_low(0, 0, 0)
            weighted_codes(0, 0, 0)
            with dve.Fori(0, NF // 2 - 1) as pair:
                for s in range(2):
                    for h in range(TH):
                        unit(pair * 2 + s, s, h, False, pair + 1)
            tern2 = ternary(w_l2, H2, tern_s[1], tern_tmp2, (load["l2"], 16 * 5), 2)
            tern2(0)
            for f in (NF - 2, NF - 1):
                for h in range(TH):
                    unit(f, f % 2, h, f == NF - 1, None)
                    tern2((f - NF + 2) * TH + h + 1)

            dve.sem_inc(weights_fixed, 1)

            def gate_std(h, i, r, s, ga, up, hid):
                return TTN(hid, up, s, ALU.mult)
            dve.wait_ge(moe_x, 2 * NF + 1)

            def tern2_beside(i):
                if i:
                    tern2(TERN_SUM + i)
            ffn(l1, gate_std, between=tern2_beside)

            ln_xc_of("l2x", 1)
            A = att_small
            ln_diag_of("l2x", 1)
            ln_xn_of("l2x", 1)
            def split_heads(is_q, h):
                dve.wait_ge(pj_used, is_q * TT + 4 * h + 4)
                half = slice(4 * HEADS * h, 4 * HEADS * (h + 1))
                s_ = (A["sq"].rearrange("p t h -> p (t h)") if is_q else A["sk"])[:, half]
                amax, inv = A["amax"][:, half], A["inv"][:, half]
                v = (q_tok if is_q else k_tok)[:, 4 * h:4 * h + 4, :].rearrange("p t (h d) -> p (t h) d", d=HD)
                o = (q3 if is_q else k3)[:, 4 * h:4 * h + 4].rearrange("p t h c d -> p (t h) c d")
                step(dve.tensor_reduce(amax, v, AX.X, ALU.max, apply_absolute_value=True))
                step(TS(s_, amax, 1.0 / 127.0, 1e-8, ALU.mult, ALU.max))
                step(dve.reciprocal(inv, s_))
                step(TTN(v, v, b3(inv, HD), ALU.mult))
                if is_q:
                    step(TS(v, v, ROUND, None, ALU.add))
                    for c_ in range(3):
                        last = TS(o[:, :, c_, :], v, ROUND, None, ALU.subtract)
                else:
                    step(TS(v, v, ROUND, ROUND, ALU.add, ALU.subtract))
                    step(TTN(v, v, b3(s_, HD), ALU.mult))
                    step(dve.tensor_copy(o[:, :, 0, :], v))
                    step(TTN(v, v, o[:, :, 0, :], ALU.subtract))
                    step(dve.tensor_copy(o[:, :, 1, :], v))
                    last = TTN(o[:, :, 2, :], v, o[:, :, 1, :], ALU.subtract)
                last.then_inc(qk_split, 1)
                dve.wait_ge(qk_split, 2 * is_q + h + 1)

            for h in range(TH):
                split_heads(0, h)
            dve.wait_ge(v_ready, 2 * KC)
            for h in range(TH):
                split_heads(1, h)
            dve.wait_ge(load["l2x"], 16 * 3)
            for h in range(TH):
                for o in range(KC):
                    dve.wait_ge(v_ready, 2 * h + o + 1)
                    step(TS(v_t[:, o, tok(h)], ps[:, 4 + 2 * h + o, :], A["bvp"][:, o:o + 1], None, ALU.add))
            step(dve.tensor_reduce(A["vmax"], v_t, AX.X, ALU.max, apply_absolute_value=True))
            step(TS(A["sv"], A["vmax"], 1.0 / 127.0, 1e-8, ALU.mult, ALU.max))
            step(dve.reciprocal(A["vinv"], A["sv"]))
            for o in range(KC):
                step(TS(v_t[:, o, :], v_t[:, o, :], A["vinv"][:, o:o + 1], ROUND, ALU.mult, ALU.add))
            TS(vn_t, v_t, ROUND, None, ALU.subtract).then_inc(vn_ready, 1)
            for n in range(2 * HEADS):
                if head_by_dve(n):
                    dve.wait_ge(head_turned, n + 1)
                    dve.wait_ge(head_copied, n)
                    dst = (k_s, q_s)[n // HEADS]
                    dve.tensor_copy(dst[0:3 * HD, n % HEADS, :], ps[0:3 * HD, n % 2, :].bitcast(BF16)
                                    ).then_inc(head_copied, 1)
            for k in range(KC):
                dve.wait_ge(vn_turned, k + 1)
                dve.tensor_copy(v_tok[:, :, k * P:(k + 1) * P],
                                ps[:, 2 + k, :].bitcast(BF16).rearrange("p (t d) -> p t d", t=TT)).then_inc(v_copied, 1)
            def row_bias(t, i):
                n, b = t * HEADS + (i + 1), i % 2
                dve.wait_ge(att_s, n)
                dve.tensor_reduce(A["nm"][:, b:b + 1], ps[:, 2 * b:2 * b + 2, :], AX.XY, ALU.max, negate=True
                                  ).then_inc(att_max, 1)
                dve.wait_ge(att_max, n)
                TS(A["bias"][:, b:b + 1], A["nm"][:, b:b + 1], A["sq"][:, bass.ds(t + i // HEADS, 1), i % HEADS],
                   math.log(255.0), ALU.mult, ALU.add).then_inc(att_bias, 1)

            def rounding(t, j):
                dve.wait_ge(att_exp, t * HEADS + (j + 1))
                if not (isinstance(t, int) and t * HEADS + j < 2):
                    dve.wait_ge(att_t, t * HEADS + (j - 1))
                TS(att_p[:, j % 2, :], att_e[:, j % 2, :], ROUND, ROUND, ALU.add, ALU.subtract).then_inc(att_round, 1)

            def query_tile(t, final):
                for i in range(4, HEADS + 4):
                    if i < HEADS or not final:
                        row_bias(t, i)
                    if i - 1 < HEADS or not final:
                        rounding(t, i - 1)
                dve.wait_ge(att_o, t + 1)
                dve.reciprocal(A["rz"], A["z"][:, bass.ds(t, 1), :].rearrange("p a h -> p (a h)")).then_inc(att_rz, 1)
                dve.wait_ge(att_rz, t + 1)
                TTN(o_tok[:, bass.ds(t, 1), :].rearrange("p a (h d) -> p (a h) d", d=HD),
                    ps[:, 6, 0:D].rearrange("p (h d) -> p h d", d=HD), b3(A["rz"], HD), ALU.mult
                    ).then_inc(att_o_used, 1)

            dve.sem_inc(att_o_used, 1)
            row_bias(0, 0)
            row_bias(0, 1)
            rounding(0, 0)
            row_bias(0, 2)
            rounding(0, 1)
            row_bias(0, 3)
            rounding(0, 2)
            with dve.Fori(0, TT - 1) as t:
                query_tile(t, False)
            query_tile(TT - 1, True)
            for n in range(4):
                h, k = divmod(n, 2)
                dve.wait_ge(ot_turned, n + 1)
                TS(o_t[:, k, tok(h)], ps[:, n, :], A["sv"][:, k:k + 1], None, ALU.mult).then_inc(ot_copied, 1)
            for h in range(TH):
                dve.wait_ge(att_done, h + 1)
                for o in range(KC):
                    last = STT(x_t[:, o, tok(h)], ps[:, 4 + 2 * h + o, :], A["bpp"][:, o:o + 1], x_t[:, o, tok(h)],
                               ALU.add, ALU.add)
                    if o == 0:
                        step(last)
                last.then_inc(x_ready, 1)

            ln_xc_of("l2", 0)
            copy_out(dve, "l2", True, (0, 2))
            ln_diag_of("l2", 0)
            ln_xn_of("l2", 0)
            ln_low("l2", 0)
            copy_out(dve, "l2", True, (1, 2))
            ffn(l2, gate_std)

            copy_out(dve, "lx", True)
            ln_xc_of("l3x", 1)
            step(dve.memset(v1[:, :, :, P:P + 1], 1.0))
            for t in range(TT):
                if t == TT // 2:
                    ln_diag_of("l3x", 1)
                    ln_xn_of("l3x", 1)
                dve.wait_ge(lx_kv, 2 * t + 1)
                if t >= 2:
                    dve.wait_ge(lx_exp_r, t - 1)
                TS(lx_min[:, t % 2, :], ps[:, t % 2, 0:D], 0.0, None, ALU.min).then_inc(lx_min_r, 1)
                dve.wait_ge(lx_exp_r, t + 1)
                STT(kf[:, t, :], ps[:, t % 2, 0:D], 0.0, lx_exp[:, t % 2, :], ALU.max, ALU.add).then_inc(lx_kf, 1)
            for b in range(BATCH):
                dve.wait_ge(lx_sum, b + 1)
                for m in range(KC):
                    c0 = m * (P + 1)
                    step(TTN(bd[:, b, m, :], ps[:, b, c0:c0 + P], head_mask[:, :], ALU.mult))
                    step(TS(dd[:, b, m, :], head_mask[:, :], ps[:, b, c0 + P:c0 + P + 1], None, ALU.mult))
            dve.sem_inc(lx_bd, 1)
            def query_negative(b):
                dve.wait_ge(lx_qg, 2 * b + 1)
                if b >= 2:
                    dve.wait_ge(lx_qf, b - 1)
                TS(lx_qmin[:, b % 2], ps[:, 0, :].rearrange("p (k t) -> p k t", k=KC), 0.0, None, ALU.min
                   ).then_inc(lx_qmin_r, 1)

            def query_features(b):
                dve.wait_ge(lx_act, 2 * b + 1)
                if b >= 2:
                    dve.wait_ge(lx_att, b - 1)
                STT(lx_q[:, b % 2], ps[:, 0, :].rearrange("p (k t) -> p k t", k=KC), 0.0, lx_qmin[:, b % 2], ALU.max,
                    ALU.add).then_inc(lx_qf, 1)

            query_negative(0)
            query_features(0)
            for b in range(BATCH):
                dve.wait_ge(lx_att, b + 1)
                step(TS(lx_den, ps[:, 3, :].rearrange("p (k t) -> p k t", k=KC), 1e-6, None, ALU.add))
                step(dve.reciprocal(lx_den, lx_den))
                if b + 1 < BATCH:
                    query_negative(b + 1)
                step(TTN(lx_den, ps[:, 2, :].rearrange("p (k t) -> p k t", k=KC), lx_den, ALU.mult))
                dve.wait_ge(lx_act, 2 * b + 2)
                if b >= 2:
                    dve.wait_ge(y_ready, b - 1)
                TTN(lx_o[:, b % 2], lx_den, lx_gate[:, b % 2], ALU.mult).then_inc(lx_or, 1)
                if b + 1 < BATCH:
                    query_features(b + 1)
                dve.wait_ge(y_ready, b + 1)
                xb = x_t[:, :, b * SEQ:(b + 1) * SEQ]
                TTN(xb, ps[:, 4, :].rearrange("p (k t) -> p k t", k=KC), xb, ALU.add).then_inc(lx_x, 1)
                if b % 2:
                    dve.wait_ge(lx_x, b + 1)
                    dve.sem_inc(x_ready, 1)

            for h in range(TH):
                ln_xc_of("l3", h)
            for h in range(TH):
                ln_diag_of("l3", h)
                ln_xn_of("l3", h)
                for k in range(KC):
                    n = 2 * h + k
                    dve.wait_ge(xt_turned, n + 1)
                    dve.tensor_copy(xn_tok[:, 4 * h:4 * h + 4, k * P:(k + 1) * P],
                                    ps[:, n, :].rearrange("p (t d) -> p t d", t=4)).then_inc(xt_copied, 1)
                dve.wait_ge(xt_copied, 2 * h + 2)
                mx_quant(xn_tok[:, 4 * h:4 * h + 4, :].rearrange("p t (a b) -> p (t a) b", b=MX_BLOCK),
                         mxq[:, 0:4 * D], mx_s[:, 0, 0:32], mx_s[:, 1, 0:32], 32, step).then_inc(xq_ready, 1)
                dve.wait_ge(xq_ready, h + 1)

            def product(t):
                h = h_tok[:, t % 2, :]
                dve.wait_ge(m_act, t + 1)
                dve.wait_ge(m_gu, 2 * t + 2)
                if t >= 2:
                    dve.wait_ge(m_ht, t - 1)
                TTN(h.rearrange("p (a b) -> p a b", a=2), ps[:, 2:4, :],
                    h_act.rearrange("p (a b) -> p a b", a=2), ALU.mult).then_inc(m_mul, 1)
                dve.wait_ge(m_mul, t + 1)
                mx_quant(h.rearrange("p (a b) -> p a b", b=MX_BLOCK), mxq[:, 0:H3], mx_s[:, 0, 0:32], mx_s[:, 1, 0:32], 32,
                         step).then_inc(m_h, 1)

            def result(t):
                dve.wait_ge(m_o, t + 1)
                if t >= 2:
                    dve.wait_ge(stored[t % 2], 16 * (t // 2))
                TTN(res[:, t % 2, :], ps[:, 6, 0:D], x_tok[:, t, :], ALU.add).then_inc(m_res, 1)

            product(0)
            product(1)
            for t in range(TT - 2):
                product(t + 2)
                result(t)
            result(TT - 2)
            result(TT - 1)


_INS = ['x', 'itok_BxS_13_99985', 'ctx_2048', 'L0_ffn_w1', 'L0_ffn_w3', 'L0_ffn_w2', 'L1_xattn_w', 'L1_xattn_u',
        'L1_ffn_gate_weight', 'L1_ffn_inv_mapping', 'L1_ffn_mask_up_W', 'L1_ffn_gate_W', 'L1_ffn_gate_qa',
        'L1_ffn_gate_qb', 'L1_ffn_gate_scale', 'L1_ffn_up_W', 'L1_ffn_up_qa', 'L1_ffn_up_qb', 'L1_ffn_up_scale',
        'L1_ffn_down_W', 'L1_ffn_down_qa', 'L1_ffn_down_qb', 'L1_ffn_down_scale', 'L1_ffn_sh_gate_W',
        'L1_ffn_sh_up_W', 'L1_ffn_sh_down_W', 'L2_xattn_Wq', 'L2_xattn_bq', 'L2_xattn_Wkv', 'L2_xattn_bkv',
        'L2_xattn_Wp', 'L2_xattn_bp', 'L2_ffn_w1', 'L2_ffn_w2', 'L2_ffn_w3', 'L3_xattn_Wq', 'L3_xattn_Wg',
        'L3_xattn_bg', 'L3_xattn_Wkv', 'L3_xattn_Wo', 'L3_ffn_gate_w', 'L3_ffn_up_w', 'L3_ffn_down_w']


def kernel(**inputs):
    import numpy as _np
    import concourse.bacc as _bacc
    from concourse import mybir as _mybir
    from concourse.bass_utils import run_bass_kernel_spmd as _run

    nc = _bacc.Bacc("TRN2", target_bir_lowering=False, num_devices=1)
    arrays, args = {}, {}
    for name in _INS:
        v = _np.ascontiguousarray(inputs[name])
        arrays[f"in_{name}"] = v
        args[name] = nc.dram_tensor(f"in_{name}", v.shape, _mybir.dt.from_np(v.dtype), kind="ExternalInput").ap()
    out = nc.dram_tensor("out_0", (BATCH, SEQ, D), F32, kind="ExternalOutput").ap()
    build(nc, args, out)
    r = _run(nc, [arrays], core_ids=[0])
    return r.results[0]["out_0"]
```
